# Optimizing a Trainium2 kernel written in Bass

```python
import numpy as np
import jax
import jax.numpy as jnp

def _softmax(x, axis=-1):
    return jax.nn.softmax(x, axis=axis)

def _gelu(x):
    return jax.nn.gelu(x, approximate=True)

def _silu(x):
    return jax.nn.silu(x)

def _sigmoid(x):
    return jax.nn.sigmoid(x)

def _layernorm(x, axis=-1, eps=1e-05):
    m = jnp.mean(x, axis=axis, keepdims=True)
    v = jnp.var(x, axis=axis, keepdims=True)
    return (x - m) / jnp.sqrt(v + eps)

def _scatter_add(tgt, idx, src, axis=0):
    return tgt.at[idx].add(src)

def _segment_sum(src, seg, n):
    return jax.ops.segment_sum(src, seg, n)
kernel_name = 'mk_gnn_resnorm_d4_gnn_r8_2f9f11'

def setup_inputs(seed: int=0):
    np.random.seed(seed)
    _w = jnp.asarray

    def _rec_inputs():
        import jax
        import jax.numpy as jnp
        _gk = jax.random.key(seed)
        x = -0.0003713 + 1 * jax.random.normal(jax.random.fold_in(_gk, 1), (12500, 128), jnp.float32)
        src = jax.random.randint(jax.random.fold_in(_gk, 2), (200000,), 0, 12500, jnp.int32)
        dst = jax.random.randint(jax.random.fold_in(_gk, 3), (200000,), 0, 12500, jnp.int32)
        _o = jnp.argsort(dst, stable=True)
        src = src[_o]
        dst = dst[_o]
        edge_attr_64 = 0.000102155 + 1.00015 * jax.random.normal(jax.random.fold_in(_gk, 11), (200000, 64), jnp.float32)
        edge_type_3 = jax.random.randint(jax.random.fold_in(_gk, 13), (200000,), 0, 3, jnp.int32)
        edge_weight = jax.random.uniform(jax.random.fold_in(_gk, 14), (200000,), jnp.float32, 0.0, 0.999999)
        return (x, src, dst, edge_attr_64, edge_type_3, edge_weight)
    x, src, dst, edge_attr_64, edge_type_3, edge_weight = _rec_inputs()

    def _L0_gnn_setup():
        import jax, jax.numpy as jnp
        import numpy as np
        N_NODES = 12500
        D = 128
        N_EDGES = 80000
        BN_EPS = 0.001

        def _bn(x, gamma, beta, mean, var):
            return (x - mean) * jax.lax.rsqrt(var + BN_EPS) * gamma + beta
        key = jax.random.key(seed)
        ks = jax.random.split(key, 12)
        node_repr = jax.random.normal(ks[0], (N_NODES, D), dtype=jnp.float32)
        edges = jax.random.randint(ks[1], (2, N_EDGES), 0, N_NODES, dtype=jnp.int64)
        bn1_gamma = jax.random.normal(ks[2], (D,), dtype=jnp.float32) * 0.1 + 1.0
        bn1_beta = jax.random.normal(ks[3], (D,), dtype=jnp.float32) * 0.1
        bn1_mean = jax.random.normal(ks[4], (D,), dtype=jnp.float32) * 0.1
        bn1_var = jax.random.uniform(ks[5], (D,), dtype=jnp.float32) + 0.5
        W1 = jax.random.normal(ks[6], (D, D), dtype=jnp.float32) / np.sqrt(D)
        b1 = jnp.zeros((D,), dtype=jnp.float32)
        bn2_gamma = jax.random.normal(ks[7], (2 * D,), dtype=jnp.float32) * 0.1 + 1.0
        bn2_beta = jax.random.normal(ks[8], (2 * D,), dtype=jnp.float32) * 0.1
        bn2_mean = jax.random.normal(ks[9], (2 * D,), dtype=jnp.float32) * 0.1
        bn2_var = jax.random.uniform(ks[10], (2 * D,), dtype=jnp.float32) + 0.5
        W2 = jax.random.normal(ks[11], (2 * D, D), dtype=jnp.float32) / np.sqrt(2 * D)
        b2 = jnp.zeros((D,), dtype=jnp.float32)
        return dict(node_repr=node_repr, edges=edges, bn1_gamma=bn1_gamma, bn1_beta=bn1_beta, bn1_mean=bn1_mean, bn1_var=bn1_var, W1=W1, b1=b1, bn2_gamma=bn2_gamma, bn2_beta=bn2_beta, bn2_mean=bn2_mean, bn2_var=bn2_var, W2=W2, b2=b2)
    _L0_gnn_all = _L0_gnn_setup()
    _L0_gnn_in = {k: v for k, v in _L0_gnn_all.items() if k in ('bn1_gamma', 'bn1_beta', 'bn1_mean', 'bn1_var', 'W1', 'b1', 'bn2_gamma', 'bn2_beta', 'bn2_mean', 'bn2_var', 'W2', 'b2')}
    del _L0_gnn_all

    def _L1_gnn_setup():
        import jax, jax.numpy as jnp
        import numpy as np
        N_NODES = 12500
        N_EDGES = 62500
        IN_CH = 128
        EDGE_CH = 64

        def _glorot(key, shape):
            fan_in, fan_out = (shape[0], shape[1])
            lim = (6.0 / (fan_in + fan_out)) ** 0.5
            return jax.random.uniform(key, shape, jnp.float32, -lim, lim)
        key = jax.random.key(seed)
        ks = jax.random.split(key, 14)
        x = jax.random.normal(ks[0], (N_NODES, IN_CH), jnp.float32)
        edge_index = jax.random.randint(ks[1], (2, N_EDGES), 0, N_NODES, jnp.int64)
        edge_attr = jax.random.normal(ks[2], (N_EDGES, EDGE_CH), jnp.float32)
        timestamps = jax.random.uniform(ks[3], (N_EDGES,), jnp.float32)
        We1 = _glorot(ks[4], (EDGE_CH, 2 * EDGE_CH))
        be1 = jnp.zeros((2 * EDGE_CH,), jnp.float32)
        We2 = _glorot(ks[5], (2 * EDGE_CH, IN_CH))
        be2 = jnp.zeros((IN_CH,), jnp.float32)
        Wt = _glorot(ks[6], (1, IN_CH))
        bt = jnp.zeros((IN_CH,), jnp.float32)
        Wn1 = _glorot(ks[7], (2 * IN_CH, IN_CH))
        bn1 = jnp.zeros((IN_CH,), jnp.float32)
        Wn2 = _glorot(ks[8], (IN_CH, IN_CH))
        bn2 = jnp.zeros((IN_CH,), jnp.float32)
        return {'x': x, 'edge_index': edge_index, 'edge_attr': edge_attr, 'timestamps': timestamps, 'We1': We1, 'be1': be1, 'We2': We2, 'be2': be2, 'Wt': Wt, 'bt': bt, 'Wn1': Wn1, 'bn1': bn1, 'Wn2': Wn2, 'bn2': bn2}
    _L1_gnn_all = _L1_gnn_setup()
    _L1_gnn_in = {k: v for k, v in _L1_gnn_all.items() if k in ('We1', 'be1', 'We2', 'be2', 'Wt', 'bt', 'Wn1', 'bn1', 'Wn2', 'bn2')}
    del _L1_gnn_all

    def _L2_gnn_setup():
        import jax, jax.numpy as jnp
        import numpy as np
        N_NODES = 12500
        DIM = 128
        N_EDGES = 75000

        def _gcn_conv(x, src, dst, dinv, W, b, n):
            h = x @ W
            coef = (dinv[src] * dinv[dst])[:, None]
            msg = h[src] * coef
            out = jax.ops.segment_sum(msg, dst, num_segments=n)
            return out + b
        key = jax.random.key(seed)
        k1, k2, k3, k4 = jax.random.split(key, 4)
        scale = 1.0 / np.sqrt(DIM)
        return {'x': jax.random.normal(k1, (N_NODES, DIM), dtype=jnp.float32), 'edge_index': jax.random.randint(k2, (2, N_EDGES), 0, N_NODES, dtype=jnp.int32), 'W1': jax.random.normal(k3, (DIM, DIM), dtype=jnp.float32) * scale, 'b1': jnp.zeros((DIM,), dtype=jnp.float32), 'W2': jax.random.normal(k4, (DIM, DIM), dtype=jnp.float32) * scale, 'b2': jnp.zeros((DIM,), dtype=jnp.float32)}
    _L2_gnn_all = _L2_gnn_setup()
    _L2_gnn_in = {k: v for k, v in _L2_gnn_all.items() if k in ('W1', 'b1', 'W2', 'b2')}
    del _L2_gnn_all

    def _L3_gnn_setup():
        import jax, jax.numpy as jnp
        import numpy as np
        N, E = (12500, 80000)
        IN_DIM, OUT_DIM, H, D = (128, 128, 4, 32)
        NUM_EDGE_TYPES = 3
        NEG_SLOPE = 0.2
        key = jax.random.key(seed)
        ks = jax.random.split(key, 10)
        x = jax.random.normal(ks[0], (N, IN_DIM), dtype=jnp.float32)
        edge_index = jax.random.randint(ks[1], (2, E), 0, N, dtype=jnp.int32)
        edge_type = jax.random.randint(ks[2], (E,), 0, NUM_EDGE_TYPES, dtype=jnp.int32)
        s = 1.0 / np.sqrt(IN_DIM)
        Wq = jax.random.uniform(ks[3], (IN_DIM, H * D), jnp.float32, -s, s)
        Wk = jax.random.uniform(ks[4], (IN_DIM, H * D), jnp.float32, -s, s)
        Wv = jax.random.uniform(ks[5], (IN_DIM, H * D), jnp.float32, -s, s)
        a = np.sqrt(6.0 / (2 * D + H))
        attn_lin = jax.random.uniform(ks[6], (1, H, 2 * D), jnp.float32, -a, a)
        edge_embed_table = jax.random.normal(ks[7], (NUM_EDGE_TYPES, H * D), dtype=jnp.float32)
        so = 1.0 / np.sqrt(H * D)
        Wout = jax.random.uniform(ks[8], (H * D, OUT_DIM), jnp.float32, -so, so)
        bout = jax.random.uniform(ks[9], (OUT_DIM,), jnp.float32, -so, so)
        return {'x': x, 'Wq': Wq, 'Wk': Wk, 'Wv': Wv, 'attn_lin': attn_lin, 'edge_embed_table': edge_embed_table, 'Wout': Wout, 'bout': bout, 'edge_index': edge_index, 'edge_type': edge_type}
    _L3_gnn_all = _L3_gnn_setup()
    _L3_gnn_in = {k: v for k, v in _L3_gnn_all.items() if k in ('Wq', 'Wk', 'Wv', 'attn_lin', 'edge_embed_table', 'Wout', 'bout')}
    del _L3_gnn_all
    return {'x': x, 'src': src, 'dst': dst, 'edge_attr_64': edge_attr_64, 'edge_type_3': edge_type_3, 'edge_weight': edge_weight, 'L0_gnn_bn1_gamma': _L0_gnn_in['bn1_gamma'], 'L0_gnn_bn1_beta': _L0_gnn_in['bn1_beta'], 'L0_gnn_bn1_mean': _L0_gnn_in['bn1_mean'], 'L0_gnn_bn1_var': _L0_gnn_in['bn1_var'], 'L0_gnn_W1': _L0_gnn_in['W1'], 'L0_gnn_b1': _L0_gnn_in['b1'], 'L0_gnn_bn2_gamma': _L0_gnn_in['bn2_gamma'], 'L0_gnn_bn2_beta': _L0_gnn_in['bn2_beta'], 'L0_gnn_bn2_mean': _L0_gnn_in['bn2_mean'], 'L0_gnn_bn2_var': _L0_gnn_in['bn2_var'], 'L0_gnn_W2': _L0_gnn_in['W2'], 'L0_gnn_b2': _L0_gnn_in['b2'], 'L1_gnn_We1': _L1_gnn_in['We1'], 'L1_gnn_be1': _L1_gnn_in['be1'], 'L1_gnn_We2': _L1_gnn_in['We2'], 'L1_gnn_be2': _L1_gnn_in['be2'], 'L1_gnn_Wt': _L1_gnn_in['Wt'], 'L1_gnn_bt': _L1_gnn_in['bt'], 'L1_gnn_Wn1': _L1_gnn_in['Wn1'], 'L1_gnn_bn1': _L1_gnn_in['bn1'], 'L1_gnn_Wn2': _L1_gnn_in['Wn2'], 'L1_gnn_bn2': _L1_gnn_in['bn2'], 'L2_gnn_W1': _L2_gnn_in['W1'], 'L2_gnn_b1': _L2_gnn_in['b1'], 'L2_gnn_W2': _L2_gnn_in['W2'], 'L2_gnn_b2': _L2_gnn_in['b2'], 'L3_gnn_Wq': _L3_gnn_in['Wq'], 'L3_gnn_Wk': _L3_gnn_in['Wk'], 'L3_gnn_Wv': _L3_gnn_in['Wv'], 'L3_gnn_attn_lin': _L3_gnn_in['attn_lin'], 'L3_gnn_edge_embed_table': _L3_gnn_in['edge_embed_table'], 'L3_gnn_Wout': _L3_gnn_in['Wout'], 'L3_gnn_bout': _L3_gnn_in['bout']}

def reference(x, src, dst, edge_attr_64, edge_type_3, edge_weight, L0_gnn_bn1_gamma, L0_gnn_bn1_beta, L0_gnn_bn1_mean, L0_gnn_bn1_var, L0_gnn_W1, L0_gnn_b1, L0_gnn_bn2_gamma, L0_gnn_bn2_beta, L0_gnn_bn2_mean, L0_gnn_bn2_var, L0_gnn_W2, L0_gnn_b2, L1_gnn_We1, L1_gnn_be1, L1_gnn_We2, L1_gnn_be2, L1_gnn_Wt, L1_gnn_bt, L1_gnn_Wn1, L1_gnn_bn1, L1_gnn_Wn2, L1_gnn_bn2, L2_gnn_W1, L2_gnn_b1, L2_gnn_W2, L2_gnn_b2, L3_gnn_Wq, L3_gnn_Wk, L3_gnn_Wv, L3_gnn_attn_lin, L3_gnn_edge_embed_table, L3_gnn_Wout, L3_gnn_bout):
    import jax
    import jax.numpy as jnp

    def _L0_gnn_ref(node_repr, edges, bn1_gamma, bn1_beta, bn1_mean, bn1_var, W1, b1, bn2_gamma, bn2_beta, bn2_mean, bn2_var, W2, b2):
        import jax, jax.numpy as jnp
        import numpy as np
        N_NODES = 12500
        D = 128
        N_EDGES = 80000
        BN_EPS = 0.001

        def _bn(x, gamma, beta, mean, var):
            return (x - mean) * jax.lax.rsqrt(var + BN_EPS) * gamma + beta
        num_nodes = node_repr.shape[0]
        node_indices, neighbour_indices = (edges[0], edges[1])
        neigh = node_repr[neighbour_indices]
        msg = jax.nn.gelu(_bn(neigh, bn1_gamma, bn1_beta, bn1_mean, bn1_var) @ W1 + b1, approximate=False)
        sums = jax.ops.segment_sum(msg, node_indices, num_segments=num_nodes)
        cnt = jax.ops.segment_sum(jnp.ones((edges.shape[1],), msg.dtype), node_indices, num_segments=num_nodes)
        agg = sums / jnp.maximum(cnt, 1.0)[:, None]
        h = jnp.concatenate([node_repr, agg], axis=1)
        out = jax.nn.gelu(_bn(h, bn2_gamma, bn2_beta, bn2_mean, bn2_var) @ W2 + b2, approximate=False)
        return out

    def _L1_gnn_ref(x, edge_index, edge_attr, timestamps, We1, be1, We2, be2, Wt, bt, Wn1, bn1, Wn2, bn2):
        import jax, jax.numpy as jnp
        import numpy as np
        N_NODES = 12500
        N_EDGES = 62500
        IN_CH = 128
        EDGE_CH = 64

        def _glorot(key, shape):
            fan_in, fan_out = (shape[0], shape[1])
            lim = (6.0 / (fan_in + fan_out)) ** 0.5
            return jax.random.uniform(key, shape, jnp.float32, -lim, lim)
        ts = timestamps[:, None]
        ef = jax.nn.relu(edge_attr @ We1 + be1) @ We2 + be2
        tw = jax.nn.sigmoid(ts @ Wt + bt)
        ef = ef * tw
        row, col = (edge_index[0], edge_index[1])
        combined = jnp.concatenate([x[row], ef], axis=1)
        msg = jax.nn.relu(combined @ Wn1 + bn1) @ Wn2 + bn2
        out = jax.ops.segment_sum(msg, col, num_segments=x.shape[0])
        return out + x

    def _L2_gnn_ref(x, edge_index, W1, b1, W2, b2):
        import jax, jax.numpy as jnp
        import numpy as np
        N_NODES = 12500
        DIM = 128
        N_EDGES = 75000

        def _gcn_conv(x, src, dst, dinv, W, b, n):
            h = x @ W
            coef = (dinv[src] * dinv[dst])[:, None]
            msg = h[src] * coef
            out = jax.ops.segment_sum(msg, dst, num_segments=n)
            return out + b
        n = x.shape[0]
        loop = jnp.arange(n, dtype=edge_index.dtype)
        src = jnp.concatenate([edge_index[0], loop])
        dst = jnp.concatenate([edge_index[1], loop])
        deg = jax.ops.segment_sum(jnp.ones_like(dst, dtype=x.dtype), dst, num_segments=n)
        dinv = jnp.where(deg > 0, jax.lax.rsqrt(deg), 0.0)
        identity = x
        out = _gcn_conv(x, src, dst, dinv, W1, b1, n)
        out = jax.nn.relu(out)
        out = _gcn_conv(out, src, dst, dinv, W2, b2, n)
        out = jax.nn.relu(out + identity)
        return out

    def _L3_gnn_ref(x, Wq, Wk, Wv, attn_lin, edge_embed_table, Wout, bout, edge_index, edge_type):
        import jax, jax.numpy as jnp
        import numpy as np
        N, E = (12500, 80000)
        IN_DIM, OUT_DIM, H, D = (128, 128, 4, 32)
        NUM_EDGE_TYPES = 3
        NEG_SLOPE = 0.2
        n = x.shape[0]
        src, dst = (edge_index[0], edge_index[1])
        q = (x @ Wq).reshape(n, H, D)
        k = (x @ Wk).reshape(n, H, D)
        v = (x @ Wv).reshape(n, H, D)
        q_src = q[src]
        k_dst = k[dst]
        a_q, a_k = (attn_lin[0, :, :D], attn_lin[0, :, D:])
        scores = jnp.einsum('ehd,hd->eh', q_src, a_q) + jnp.einsum('ehd,hd->eh', k_dst, a_k)
        scores = jnp.where(scores >= 0, scores, NEG_SLOPE * scores)
        edge_embed = edge_embed_table[edge_type].reshape(-1, H, D)
        scores = scores + jnp.sum(q_src * edge_embed, axis=-1)
        m = jax.ops.segment_max(jax.lax.stop_gradient(scores), dst, num_segments=n)
        m = jnp.maximum(m, -100.0)
        ex = jnp.exp(scores - m[dst])
        denom = jax.ops.segment_sum(ex, dst, num_segments=n)
        alpha = ex / (denom[dst] + 1e-10)
        messages = alpha[:, :, None] * v[src]
        out = jax.ops.segment_sum(messages, dst, num_segments=n)
        out = out.reshape(n, H * D)
        return out @ Wout + bout
    edge_index = jnp.stack([src, dst])
    x = _layernorm(x + _L0_gnn_ref(x, edge_index, L0_gnn_bn1_gamma, L0_gnn_bn1_beta, L0_gnn_bn1_mean, L0_gnn_bn1_var, L0_gnn_W1, L0_gnn_b1, L0_gnn_bn2_gamma, L0_gnn_bn2_beta, L0_gnn_bn2_mean, L0_gnn_bn2_var, L0_gnn_W2, L0_gnn_b2), axis=-1)
    x = _layernorm(x + _L1_gnn_ref(x, edge_index, edge_attr_64, edge_weight, L1_gnn_We1, L1_gnn_be1, L1_gnn_We2, L1_gnn_be2, L1_gnn_Wt, L1_gnn_bt, L1_gnn_Wn1, L1_gnn_bn1, L1_gnn_Wn2, L1_gnn_bn2), axis=-1)
    x = _layernorm(x + _L2_gnn_ref(x, edge_index, L2_gnn_W1, L2_gnn_b1, L2_gnn_W2, L2_gnn_b2), axis=-1)
    x = _layernorm(x + _L3_gnn_ref(x, L3_gnn_Wq, L3_gnn_Wk, L3_gnn_Wv, L3_gnn_attn_lin, L3_gnn_edge_embed_table, L3_gnn_Wout, L3_gnn_bout, edge_index, edge_type_3), axis=-1)
    return x

_drawn_inputs = setup_inputs


def setup_inputs(seed=0):
    import zlib

    import numpy as np

    out = dict(_drawn_inputs(seed))
    spreads = {'L0_gnn_b1': (0.0, 0.353),
     'L0_gnn_b2': (0.0, 0.379),
     'L1_gnn_be1': (0.0, 0.393),
     'L1_gnn_be2': (0.0, 0.1),
     'L1_gnn_bt': (0.0, 0.74),
     'L1_gnn_bn1': (0.0, 0.1),
     'L1_gnn_bn2': (0.0, 0.1),
     'L2_gnn_b1': (0.0, 0.339),
     'L2_gnn_b2': (0.0, 0.1)}
    factors = {'edge_weight': 21.512,
     'L0_gnn_bn1_gamma': 119.532,
     'L0_gnn_bn1_var': 18.583,
     'L1_gnn_Wt': 8.0,
     'L3_gnn_Wk': 200.0,
     'L3_gnn_attn_lin': 19.358,
     'L0_gnn_bn1_beta': 4.866,
     'L0_gnn_bn2_beta': 2.857}
    for name, (base, spread) in spreads.items():
        noise = np.random.default_rng([zlib.crc32(name.encode()), seed]).standard_normal(out[name].shape)
        drawn = base * np.exp(spread * noise) if base else spread * noise
        out[name] = jnp.asarray(drawn.astype(out[name].dtype))
    for name, factor in factors.items():
        out[name] = (out[name] * factor).astype(out[name].dtype)
    return out
```

```python
import concourse.bass as bass
from concourse import mybir
from contextlib import ExitStack

F32, I32, BF16 = mybir.dt.float32, mybir.dt.int32, mybir.dt.bfloat16
ALU = mybir.AluOpType
ACT = mybir.ActivationFunctionType
AX = mybir.AxisListType

N, F, E = 12500, 128, 200000
H, HD, KINDS, EC = 4, 32, 3, 64

NP, NW, WB = 125, 100, 10
NPAIR = NW // (2 * WB)

TE = 128
FULL, REM = E // TE, E % TE
HB = 16
NPASS = -(-(FULL + 1) // (2 * HB))
NT = NPASS * 2 * HB
NCH = -(-(FULL + 1) // TE)
CHT, CHR = FULL // TE, FULL % TE

BP, BC = 112, NT // 112
PAD_DST, NO_KEY = 16000.0, 30000.0
ZERO_ROW = (TE - 1) * NT + NT - 1
SW = TE + 4
PAD_PLACE = 30000.0
BN_EPS, LN_EPS, DEN_EPS, MAX_FLOOR, FAR = 1e-3, 1e-5, 1e-10, -100.0, 2.0 ** 100
SLOPE = 0.2
RW = F + 2 * H
TW = F + H + KINDS * H
NACC = 99 * 128
AW = F + 4
NACCS = 4
CLEARS = 9
STOP_AFTER = None


class Count:

    def __init__(self, sem):
        self.sem, self.base = sem, 0

    def at(self, n):
        return self.base + n

    def close(self, n):
        self.base += n


class Chain:

    def __init__(self, eng, count, per=0, i=0):
        self.eng, self.count, self.offset, self.n = eng, count, per * i if per else 0, 0

    def link(self, instruction):
        self.n += 1
        instruction.then_inc(self.count.sem, 1)
        self.eng.wait_ge(self.count.sem, self.count.base + self.n + self.offset)


def gnn_kernel(nc, a, out):
    ctx = ExitStack()
    with ctx:
        build(nc, a, out, ctx)


def build(nc, a, out, ctx):
    def sb(name, shape, dt=F32, at=ctx):
        return at.enter_context(nc.sbuf_tensor(name, shape, dt))

    def dram(name, shape):
        return nc.dram_tensor(name, shape, F32, kind="Internal").ap()

    def count(name):
        return Count(ctx.enter_context(nc.semaphore(name)))

    x_state = [dram(f"x_state{n}", [N, F]) for n in range(2)]
    table = [dram(f"table{n}", [N, F]) for n in range(2)]
    table3 = dram("table3", [N, TW])
    runs = dram("runs", [TE * NT, F])
    runs3 = dram("runs3", [TE * NT, RW])
    keys = dram("keys", [NCH * TE, 2 * TE])
    starts_d = dram("starts_d", [NCH * TE, SW])
    src_rows = nc.dram_tensor("src_rows", [1, NT * TE], I32, kind="Internal").ap()
    primed = dram("primed", [4, 1])
    edge_before = dram("edge_before", [NP + 1, 1])
    by_run = dram("by_run", [NACC, F])
    acc = [dram(f"acc{k}", [NACC, AW]) for k in range(NACCS)]
    kd_edge = dram("kd_edge", [NCH * TE * TE + NP * TE, H])
    kd_rows = dram("kd_rows", [N, H])

    ident = sb("ident", [128, 128])
    iota_run = sb("iota_run", [128, 128])
    ones = sb("ones", [128, 128])
    kd_node = sb("kd_node", [NP, NW, H])
    zeros = sb("zeros", [128, 128])
    eps_ln = sb("eps_ln", [128, 1])
    src_T = sb("src_T", [128, NT + 2 * HB], I32)
    rank_T = sb("rank_T", [128, NT])
    carries = sb("carries", [128, NT])
    through = sb("through", [128, NT])
    last_row = sb("last_row", [BP, BC], I32)
    node_row = sb("node_row", [NP, NW + 2 * WB], I32)
    degree = sb("degree", [NP, NW])
    inv_count = sb("inv_count", [NP, NW])
    dinv = sb("dinv", [NP, NW])
    first_edge = sb("first_edge", [NP, NW])
    place = sb("place", [NP, NW + 2 * WB], I32)
    tile_place = sb("tile_place", [1, NT + 2 * HB], I32)
    idx_buf = sb("idx_buf", [128, 2, HB], I32)
    rank_buf = sb("rank_buf", [128, 2, HB])
    row_buf = sb("row_buf", [NP, 2, WB], I32)

    ps = ctx.enter_context(nc.psum_tensor("ps", [128, 8 * 512], F32))

    def bank(n, k=1):
        return ps[:, n * 512:(n + k) * 512]

    loaded = [count(f"loaded{s}") for s in range(2)]
    stored = [count(f"stored{s}") for s in range(2)]
    tab_stored = [count(f"tab_stored{s}") for s in range(2)]
    gathered = [count(f"gathered{s}") for s in range(4)]
    idx_ready = [count(f"idx_ready{s}") for s in range(4)]
    onehot_ready = [count(f"onehot_ready{s}") for s in range(2)]
    sums_ready = [count(f"sums_ready{s}") for s in range(2)]
    evacuated = [count(f"evacuated{s}") for s in range(2)]
    scattered = [count(f"scattered{k}") for k in range(NACCS)]
    window_in = [count(f"window_in{s}") for s in range(2)]
    counts_ready, counts_out, scatter_idx = count("counts_ready"), count("counts_out"), count("scatter_idx")
    dve_chain, act_chain, pool_chain = count("dve_chain"), count("act_chain"), count("pool_chain")
    stage_chains = count("update_chain"), count("norm_chain")
    pause = count("pause")
    setup_dma = count("setup_dma")
    names = ("agg_scaled x_turned x_turned_out agg_turned agg_turned_out product product_out residual "
             "variance deviation normed normed_turned normed_turned_out table_product table_out "
             "ea_turned ea_out gate_ready gate_out hid_ready hid_out ef_ready ef_out z_ready z_out msg_out "
             "pe_setup act_setup dve_setup pool_setup batch_done activated exponent exponent_out").split()
    c = {n: count(n) for n in names}
    every = [*stage_chains, counts_ready, counts_out, scatter_idx, *idx_ready, *onehot_ready, *sums_ready, *evacuated, *c.values()]

    mat = {}
    with_cols = {}

    def weight(name, shape, src, pieces=None):
        t = sb("w_" + name, shape)
        mat[name] = t
        loads.append((t, src))
        return t

    loads = []
    for n in ("bn1_gamma", "bn1_beta", "bn1_mean", "bn1_var"):
        weight(n, [F, 1], a["L0_gnn_" + n].rearrange("(p o) -> p o", o=1))
    for n in ("bn2_gamma", "bn2_beta", "bn2_mean", "bn2_var"):
        weight(n, [F, 2], a["L0_gnn_" + n].rearrange("(o p) -> p o", o=2))
    for n, key in (("be1", "L1_gnn_be1"), ("be2", "L1_gnn_be2"), ("bt", "L1_gnn_bt"), ("gcn_b1", "L2_gnn_b1")):
        weight(n, [F, 1], a[key].rearrange("(p o) -> p o", o=1))
    for n, key in (("b1_rows", "L0_gnn_b1"), ("b2_rows", "L0_gnn_b2"), ("nb1_rows", "L1_gnn_bn1"),
                   ("nb2_rows", "L1_gnn_bn2"), ("gcn_b2_rows", "L2_gnn_b2"), ("bout_rows", "L3_gnn_bout")):
        weight(n, [128, F], a[key].partition_broadcast(128))
    weight("W1", [F, F], a["L0_gnn_W1"])
    weight("W2", [F, 2, F], a["L0_gnn_W2"].rearrange("(k p) n -> p k n", k=2))
    weight("We1", [EC, F], a["L1_gnn_We1"])
    weight("We2", [F, F], a["L1_gnn_We2"])
    weight("Wt", [1, F], a["L1_gnn_Wt"])
    weight("Wn1", [F, 2, F], a["L1_gnn_Wn1"].rearrange("(k p) n -> p k n", k=2))
    weight("Wn2", [F, F], a["L1_gnn_Wn2"])
    weight("gcn_W1", [F, F], a["L2_gnn_W1"])
    weight("gcn_W2", [F, F], a["L2_gnn_W2"])
    weight("Wq", [F, F], a["L3_gnn_Wq"])
    weight("Wk", [F, F], a["L3_gnn_Wk"])
    weight("Wv", [F, F], a["L3_gnn_Wv"])
    weight("Wout", [F, F], a["L3_gnn_Wout"])
    weight("a_q", [128, H, HD], a["L3_gnn_attn_lin"][0, :, 0:HD].partition_broadcast(128))
    weight("a_k", [128, H, HD], a["L3_gnn_attn_lin"][0, :, HD:2 * HD].partition_broadcast(128))
    weight("embed", [128, KINDS, F], a["L3_gnn_edge_embed_table"].partition_broadcast(128))
    bn1_scale, bn1_shift = sb("bn1_scale", [F, 1]), sb("bn1_shift", [F, 1])
    bn2_scale, bn2_shift = sb("bn2_scale", [F, 2]), sb("bn2_shift", [F, 2])
    score_w = sb("score_w", [F, (2 + KINDS) * H])
    score_tmp = sb("score_tmp", [F, F])
    m = mat

    setup = ExitStack()
    edge_i = sb("edge_i", [128, 3, NCH, TE], I32, at=setup)
    edge_f = sb("edge_f", [128, 3, NCH, TE], at=setup)
    with nc.Block() as block:
        @block.gpsimd
        def _(pool):
            ch = Chain(pool, pool_chain)
            nc.gpsimd.memset(zeros[:, :], 0.0)
            nc.gpsimd.memset(ones[:, :], 1.0)
            nc.gpsimd.memset(src_T[:, NT:NT + 2 * HB], 0)
            nc.gpsimd.memset(eps_ln[:, :], LN_EPS)
            ch.link(nc.gpsimd.memset(ident[:, :], 0.0))
            nc.gpsimd.affine_select(out=ident[:, :], in_=ident[:, :], compare_op=ALU.not_equal, fill=1.0, base=0,
                                    pattern=[[-1, 128]], channel_multiplier=1)
            nc.gpsimd.iota(iota_run[:, :], pattern=[[1, 128]], base=0, channel_multiplier=0,
                           allow_small_or_imprecise_dtypes=True)
            pool_chain.close(ch.n)
            for k in every:
                pool.sem_inc(k.sem, 1)
                k.close(1)

        @block.vector
        def _(dve):
            nc.vector.memset(edge_i[:, 0, CHT:NCH, :], int(PAD_DST))
            nc.vector.memset(edge_i[:, 1:3, CHT:NCH, :], 0)

        @block.sync
        def _(sp):
            for t, s in loads:
                full = t[:, :] if len(t.shape) == 2 else t[:, :, :]
                sp.dma_start(full, s, allow_slow_non_contiguous=True).then_inc(setup_dma.sem, 16)
            setup_dma.close(16 * len(loads))
            sp.wait_ge(setup_dma.sem, setup_dma.at(0))

    with nc.Block() as block:
        @block.sync
        def _(sp):
            n = 0
            for k, key in enumerate(("dst", "src", "edge_type_3")):
                v = a[key]
                whole, rest = CHT * TE * TE, CHR * TE
                sp.dma_start(edge_i[:, k, 0:CHT, :], v[0:whole].rearrange("(c p e) -> p c e", c=CHT, p=128)
                             ).then_inc(setup_dma.sem, 16)
                sp.dma_start(edge_i[0:CHR, k, CHT, :], v[whole:whole + rest].rearrange("(p e) -> p e", e=TE)
                             ).then_inc(setup_dma.sem, 16)
                sp.dma_start(edge_i[CHR:CHR + 1, k, CHT, 0:REM], v[FULL * TE:E].rearrange("(p e) -> p e", p=1)
                             ).then_inc(setup_dma.sem, 16)
                n += 3
            setup_dma.close(16 * n)
            sp.wait_ge(setup_dma.sem, setup_dma.at(0))

        @block.scalar
        def _(act):
            act.wait_ge(c["dve_setup"].sem, c["dve_setup"].at(2))
            nc.scalar.activation(bn1_scale[:, :], bn1_shift[:, :], ACT.Sqrt)
            nc.scalar.activation(bn2_scale[:, :], bn2_shift[:, :], ACT.Sqrt).then_inc(c["act_setup"].sem, 1)

        @block.vector
        def _(dve):
            ch = Chain(dve, dve_chain)
            nc.vector.tensor_scalar_add(bn1_shift[:, :], m["bn1_var"][:, :], BN_EPS).then_inc(c["dve_setup"].sem, 1)
            nc.vector.tensor_scalar_add(bn2_shift[:, :], m["bn2_var"][:, :], BN_EPS).then_inc(c["dve_setup"].sem, 1)
            c["dve_setup"].close(2)
            cols = [("Wq", m["a_q"][:, :, :])] + [("Wq", m["embed"][:, k, :].rearrange("p (h d) -> p h d", h=H))
                                                 for k in range(KINDS)] + [("Wk", m["a_k"][:, :, :])]
            tmp = score_tmp[:, :].rearrange("p (h d) -> p h d", h=H)
            for k, (w, row) in enumerate(cols):
                ch.link(nc.vector.tensor_tensor(tmp, m[w][:, :].rearrange("p (h d) -> p h d", h=H), row, ALU.mult))
                ch.link(nc.vector.tensor_reduce(score_w[:, k * H:(k + 1) * H], tmp, AX.X, ALU.add))
            dve.wait_ge(c["act_setup"].sem, c["act_setup"].at(1))
            c["act_setup"].close(1)
            for scale, shift, g, b, mean in ((bn1_scale, bn1_shift, "bn1_gamma", "bn1_beta", "bn1_mean"),
                                             (bn2_scale, bn2_shift, "bn2_gamma", "bn2_beta", "bn2_mean")):
                ch.link(nc.vector.reciprocal(scale[:, :], scale[:, :]))
                ch.link(nc.vector.tensor_tensor(scale[:, :], scale[:, :], m[g][:, :], ALU.mult))
                ch.link(nc.vector.tensor_tensor(shift[:, :], scale[:, :], m[mean][:, :], ALU.mult))
                ch.link(nc.vector.tensor_tensor(shift[:, :], m[b][:, :], shift[:, :], ALU.subtract))
            dve_chain.close(ch.n)

    work = ExitStack()
    start = sb("start", [128, NCH, TE], at=work)
    ranks = sb("ranks", [128, NCH, TE], at=work)
    valid = sb("valid", [128, NCH, TE], at=work)
    key_out = sb("key_out", [128, NCH, 2 * TE], at=work)
    dst_T = sb("dst_T", [128, NT], at=work)
    marks = sb("marks", [128, NCH, SW], at=work)
    with nc.Block() as block:
        @block.vector
        def _(dve):
            ch = Chain(dve, dve_chain)
            dst = edge_f[:, 0, :, :]
            ch.link(nc.vector.tensor_copy(edge_f[:, :, :, :], edge_i[:, :, :, :]))
            nc.vector.memset(start[:, :, 0:1], 1.0)
            ch.link(nc.vector.tensor_tensor(start[:, :, 1:TE], dst[:, :, 1:TE], dst[:, :, 0:TE - 1], ALU.not_equal))
            ch.link(nc.vector.tensor_scalar(valid[:, :, :], dst, float(N), None, ALU.is_lt))
            for k in range(NCH):
                last = nc.vector.tensor_tensor_scan(ranks[:, k, :], start[:, k, :], zeros[:, :], 0.0, ALU.add, ALU.add)
            ch.link(last)
            ch.link(nc.vector.tensor_tensor(ranks[:, :, :], ranks[:, :, :], valid[:, :, :], ALU.mult))
            nc.vector.tensor_scalar_add(ranks[:, :, :], ranks[:, :, :], -1.0).then_inc(c["dve_setup"].sem, 1)
            ch.link(nc.vector.scalar_tensor_tensor(key_out[:, :, 0:TE], dst, -NO_KEY, start[:, :, :], ALU.add, ALU.mult))
            ch.link(nc.vector.tensor_scalar_add(key_out[:, :, 0:TE], key_out[:, :, 0:TE], NO_KEY))
            ch.link(nc.vector.memset(marks[:, :, :], 0.0))
            nc.vector.tensor_scalar(marks[:, :, 0:TE], start[:, :, :], -FAR, None, ALU.mult)
            ch.link(nc.vector.memset(marks[:, :, TE:TE + 1], -FAR))
            nc.vector.tensor_copy(key_out[:, :, TE:2 * TE], dst).then_inc(c["dve_setup"].sem, 1)
            for k in range(NCH):
                wide = min(TE, NT - k * TE)
                for j, dest in enumerate((dst_T, src_T, rank_T)):
                    n = 3 * k + j
                    dve.wait_ge(c["pe_setup"].sem, c["pe_setup"].at(n + 1))
                    nc.vector.tensor_copy(dest[:, k * TE:k * TE + wide], bank(n % 8)[:, 0:wide]
                                          ).then_inc(c["x_turned_out"].sem, 1)
            dve_chain.close(ch.n)

        @block.tensor
        def _(pe):
            pe.wait_ge(c["dve_setup"].sem, c["dve_setup"].at(1))
            for k in range(NCH):
                for j, s in enumerate((edge_f[:, 0, k, :], edge_f[:, 1, k, :], ranks[:, k, :])):
                    n = 3 * k + j
                    if n >= 8:
                        pe.wait_ge(c["x_turned_out"].sem, c["x_turned_out"].at(n - 7))
                    nc.tensor.transpose(bank(n % 8)[:, 0:128], s, ident[:, :]).then_inc(c["pe_setup"].sem, 1)

        @block.sync
        def _(sp):
            sp.dma_start(src_rows[0, 0:NT * TE - NT * TE % (TE * TE)].rearrange("(c p e) -> p c e", p=128, e=TE),
                         edge_i[:, 1, 0:NT // TE, :]).then_inc(setup_dma.sem, 16)
            rest = NT % TE
            sp.dma_start(src_rows[0, (NT - rest) * TE:NT * TE].rearrange("(p e) -> p e", e=TE),
                         edge_i[0:rest, 1, NT // TE, :]).then_inc(setup_dma.sem, 16)
            setup_dma.close(32)
            sp.wait_ge(c["dve_setup"].sem, c["dve_setup"].at(2))
            sp.dma_start(keys.rearrange("(c p) k -> p c k", p=128), key_out[:, :, :]).then_inc(setup_dma.sem, 16)
            sp.dma_start(starts_d.rearrange("(c p) k -> p c k", p=128), marks[:, :, :]).then_inc(setup_dma.sem, 16)
            setup_dma.close(32)
            sp.wait_ge(setup_dma.sem, setup_dma.at(0))
    c["dve_setup"].close(2)
    c["pe_setup"].close(3 * NCH)
    c["x_turned_out"].close(3 * NCH)

    pick = sb("pick", [128, 2, 128], at=work)
    first_bc = sb("first_bc", [128, NT], at=work)
    last_bc = sb("last_bc", [128, NT], at=work)
    node_id = sb("node_id", [NP, NW], at=work)
    tiles_at = sb("tiles_at", [NP, NW], at=work)
    tile_f = sb("tile_f", [NP, NW], at=work)
    tile_i = sb("tile_i", [NP, NW], I32, at=work)
    junk = sb("junk", [128, NT], at=work)
    row_f = sb("row_f", [BP, BC], at=work)
    single = sb("single", [128, NT], at=work)
    rank_bc = sb("rank_bc", [128, NT], at=work)
    place_f = sb("place_f", [1, NT], at=work)
    zero_row = sb("zero_row", [1, NT], at=work)
    blank = valid[:, :, :].rearrange("p c e -> p (c e)")[:, 0:NACC // 128 // CLEARS * AW]
    WIDE = NT // 4
    with nc.Block() as block:
        @block.gpsimd
        def _(pool):
            ch = Chain(pool, pool_chain)
            nc.gpsimd.memset(zero_row[:, :], 0.0)
            ch.link(nc.gpsimd.memset(pick[:, :, :], 0.0))
            for k, p in enumerate((0, TE - 1)):
                ins = nc.gpsimd.affine_select(out=pick[:, k, :], in_=pick[:, k, :], compare_op=ALU.not_equal,
                                              fill=1.0, base=-p, pattern=[[0, 128]], channel_multiplier=1)
            ins.then_inc(c["pool_setup"].sem, 1)
            nc.gpsimd.iota(node_id[:, :], pattern=[[1, NW]], base=0, channel_multiplier=NW,
                           allow_small_or_imprecise_dtypes=True).then_inc(c["pool_setup"].sem, 1)
            nc.gpsimd.iota(row_f[:, :], pattern=[[BP, BC]], base=0, channel_multiplier=1,
                           allow_small_or_imprecise_dtypes=True).then_inc(c["pool_setup"].sem, 1)
            ch.link(nc.gpsimd.memset(blank[:, :], 0.0))
            pool.sem_inc(c["pool_setup"].sem, 1)
            pool_chain.close(ch.n)
            for part in range(CLEARS):
                for k in range(NACCS):
                    pool.dma_start(acc[k].rearrange("(p a b) f -> p a (b f)", p=128, a=CLEARS)[:, part, :], blank[:, :]
                                   ).then_inc(scattered[k].sem, 16)
            for k in range(NACCS):
                pool.wait_ge(scattered[k].sem, scattered[k].at(16 * CLEARS))

        @block.sync
        def _(sp):
            sp.wait_ge(c["pool_setup"].sem, c["pool_setup"].at(4))
            wide = NACC // 128 // CLEARS
            sp.dma_start(by_run.rearrange("(p a b) f -> p a (b f)", p=128, a=CLEARS),
                         blank[:, 0:wide * F].unsqueeze(1).to_broadcast([128, CLEARS, wide * F])).then_inc(setup_dma.sem, 16)
            setup_dma.close(16)
            sp.wait_ge(setup_dma.sem, setup_dma.at(0))

        @block.tensor
        def _(pe):
            pe.wait_ge(c["pool_setup"].sem, c["pool_setup"].at(1))
            for k in range(2):
                for q in range(4):
                    nc.tensor.matmul(bank(4 * k + q)[:, 0:WIDE], pick[:, k, :], dst_T[:, q * WIDE:(q + 1) * WIDE],
                                     start=True, stop=True).then_inc(c["pe_setup"].sem, 1)
            for q in range(4):
                pe.wait_ge(c["x_turned_out"].sem, c["x_turned_out"].at(q + 1))
                nc.tensor.matmul(bank(4 + q)[:, 0:WIDE], pick[:, 1, :], rank_T[:, q * WIDE:(q + 1) * WIDE],
                                 start=True, stop=True).then_inc(c["normed_turned"].sem, 1)
            pe.wait_ge(c["dve_setup"].sem, c["dve_setup"].at(1))
            for k in range(BC):
                last = nc.tensor.matmul(bank(0)[0:BP, k:k + 1], rank_T[:, k * BP:(k + 1) * BP], pick[:, 1, 0:1],
                                        start=True, stop=True)
            last.then_inc(c["pe_setup"].sem, 1)

        @block.vector
        def _(dve):
            ch = Chain(dve, dve_chain)
            for k, dest in enumerate((first_bc, last_bc)):
                for q in range(4):
                    dve.wait_ge(c["pe_setup"].sem, c["pe_setup"].at(4 * k + q + 1))
                    ins = nc.vector.tensor_copy(dest[:, q * WIDE:(q + 1) * WIDE], bank(4 * k + q)[:, 0:WIDE])
                    if k == 1 and q < 3:
                        ins.then_inc(c["x_turned_out"].sem, 1)
            ins.then_inc(c["dve_setup"].sem, 1)
            dve.wait_ge(c["dve_setup"].sem, c["dve_setup"].at(1))
            dve.sem_inc(c["x_turned_out"].sem, 1)
            for q in range(4):
                dve.wait_ge(c["normed_turned"].sem, c["normed_turned"].at(q + 1))
                ins = nc.vector.tensor_copy(rank_bc[:, q * WIDE:(q + 1) * WIDE], bank(4 + q)[:, 0:WIDE])
            ch.link(ins)
            dve.wait_ge(c["dve_setup"].sem, c["dve_setup"].at(1))
            nc.vector.memset(carries[:, 0:1], 0.0)
            nc.vector.tensor_tensor(carries[:, 1:NT], first_bc[:, 1:NT], last_bc[:, 0:NT - 1], ALU.is_equal)
            ch.link(nc.vector.tensor_scalar(junk[:, :], first_bc[:, :], float(N), None, ALU.is_lt))
            ch.link(nc.vector.tensor_tensor(carries[:, :], carries[:, :], junk[:, :], ALU.mult))
            nc.vector.memset(through[:, 0:1], 0.0)
            ch.link(nc.vector.tensor_tensor(single[:, :], first_bc[:, :], last_bc[:, :], ALU.is_equal))
            ch.link(nc.vector.tensor_tensor(through[:, 1:NT], carries[:, 1:NT], single[:, 0:NT - 1], ALU.mult))
            row = rank_bc[0:1, :]
            ch.link(nc.vector.scalar_tensor_tensor(row, row, 1.0, carries[0:1, :], ALU.add, ALU.subtract))
            nc.vector.memset(place_f[0:1, 0:1], 0.0)
            ch.link(nc.vector.tensor_tensor_scan(place_f[0:1, 1:NT], row[:, 0:NT - 1], zero_row[0:1, 0:NT - 1], 0.0,
                                                 ALU.add, ALU.add))
            ch.link(nc.vector.tensor_tensor(place_f[0:1, :], place_f[0:1, :], carries[0:1, :], ALU.subtract))
            ch.link(nc.vector.tensor_scalar(place_f[0:1, :], place_f[0:1, :], 0.0, float(N), ALU.max, ALU.min))
            nc.vector.tensor_copy(tile_place[:, 0:NT], place_f[0:1, :])
            nc.vector.memset(tile_place[:, NT:NT + 2 * HB], 0)
            dve.wait_ge(c["pe_setup"].sem, c["pe_setup"].at(9))
            dve.wait_ge(c["pool_setup"].sem, c["pool_setup"].at(3))
            ch.link(nc.vector.tensor_scalar(junk[0:BP, 0:BC], bank(0)[0:BP, 0:BC], 0.0, float(NT), ALU.max, ALU.mult))
            ch.link(nc.vector.tensor_tensor(row_f[:, :], row_f[:, :], junk[0:BP, 0:BC], ALU.add))
            nc.vector.tensor_copy(last_row[:, :], row_f[:, :])
            with dve.Fori(0, NW) as w:
                nc.vector.tensor_scalar(junk[0:NP, :], first_bc[0:NP, :], node_id[:, bass.ds(w, 1)], 0.0, ALU.is_le,
                                        ALU.add, accum_out=tiles_at[:, bass.ds(w, 1)]).then_inc(dve_chain.sem, 1)
                dve.wait_ge(dve_chain.sem, dve_chain.at(w + ch.n + 1))
            ch.n += NW
            ch.link(nc.vector.tensor_scalar(tile_f[:, :], tiles_at[:, :], -1.0, 0.0, ALU.add, ALU.max))
            nc.vector.tensor_copy(tile_i[:, :], tile_f[:, :])
            dve_chain.close(ch.n)
    c["pool_setup"].close(4)
    c["pe_setup"].close(9)
    for k in scattered:
        k.close(16 * CLEARS)
    c["dve_setup"].close(1)
    c["x_turned_out"].close(4)
    c["normed_turned"].close(4)

    found = sb("found", [NP, 2, WB, 2 * TE], at=work)
    found_junk = sb("found_junk", [NP, TE], at=work)
    tally = sb("tally", [NP, 3, NW], at=work)
    edge_end = sb("edge_end", [NP, NW], at=work)
    tmp_n = sb("tmp_n", [NP, NW], at=work)
    held = sb("held", [NP, 1], at=work)
    before = sb("before", [NP, NP], at=work)
    tile_buf = sb("tile_buf", [NP, 2, WB], I32, at=work)
    with nc.Block() as block:
        @block.gpsimd
        def _(pool):
            ch = Chain(pool, pool_chain)
            ch.link(nc.gpsimd.memset(before[:, :], 1.0))
            nc.gpsimd.affine_select(out=before[:, :], in_=before[:, :], compare_op=ALU.is_gt, fill=0.0, base=0,
                                    pattern=[[1, NP]], channel_multiplier=-1).then_inc(c["pool_setup"].sem, 1)
            pool_chain.close(ch.n)
            with pool.Fori(0, NPAIR) as i:
                for s in range(2):
                    pool.wait_ge(idx_ready[s].sem, idx_ready[s].at(i + 1))
                    pool.sem_inc(pause.sem, 1)
                    for j in range(WB):
                        nc.gpsimd.indirect_dma_start(found[:, s, j, :], None, keys, bass.IndirectOffsetOnAxis(
                            ap=tile_buf[:, s, j:j + 1], axis=0)).then_inc(gathered[s].sem, 16)

        @block.vector
        def _(dve):
            PER = WB
            with dve.Fori(0, NPAIR) as i:
                for s in range(2):
                    nc.vector.tensor_copy(tile_buf[:, s, :], tile_i[:, bass.ds(i * 2 * WB + s * WB, WB)]
                                          ).then_inc(idx_ready[s].sem, 1)
                for s in range(2):
                    dve.wait_ge(gathered[s].sem, gathered[s].at((i + 1) * 16 * WB))
                    for j in range(WB):
                        w = bass.ds(i * 2 * WB + s * WB + j, 1)
                        for k, (half, op) in enumerate(((0, ALU.is_le), (0, ALU.is_equal), (1, ALU.is_le))):
                            nc.vector.tensor_scalar(found_junk[:, :], found[:, s, j, half * TE:(half + 1) * TE],
                                                    node_id[:, w], 0.0, op, ALU.add, accum_out=tally[:, k, w]
                                                    ).then_inc(dve_chain.sem, 1)
                            dve.wait_ge(dve_chain.sem, dve_chain.at(3 * (i * 2 * WB) + 3 * (s * WB + j) + k + 1))
            dve_chain.close(3 * NW)
            dve.wait_ge(dve_chain.sem, dve_chain.at(0))
            ch = Chain(dve, dve_chain)
            ch.link(nc.vector.tensor_scalar(tmp_n[:, :], tally[:, 0, :], -1.0, float(NT), ALU.add, ALU.mult))
            ch.link(nc.vector.tensor_tensor(tmp_n[:, :], tmp_n[:, :], tile_f[:, :], ALU.add))
            ch.link(nc.vector.scalar_tensor_tensor(tmp_n[:, :], tmp_n[:, :], -float(ZERO_ROW), tally[:, 1, :],
                                                   ALU.add, ALU.mult))
            ch.link(nc.vector.tensor_scalar_add(tmp_n[:, :], tmp_n[:, :], float(ZERO_ROW)))
            nc.vector.memset(node_row[:, NW:NW + 2 * WB], 0)
            ch.link(nc.vector.tensor_copy(node_row[:, 0:NW], tmp_n[:, :]))
            ch.link(nc.vector.tensor_tensor_scan(tmp_n[:, :], tally[:, 1, :], zeros[0:NP, 0:NW], 0.0, ALU.add, ALU.add))
            nc.vector.tensor_copy(held[:, :], tmp_n[:, NW - 1:NW]).then_inc(c["x_turned_out"].sem, 1)
            dve.wait_ge(c["x_turned"].sem, c["x_turned"].at(1))
            ch.link(nc.vector.tensor_copy(held[:, :], bank(0)[0:NP, 0:1]))
            ch.link(nc.vector.tensor_tensor(tmp_n[:, :], tmp_n[:, :], tally[:, 1, :], ALU.subtract))
            ch.link(nc.vector.tensor_scalar(tmp_n[:, :], tmp_n[:, :], held[:, 0:1], -PAD_PLACE, ALU.add, ALU.add))
            ch.link(nc.vector.tensor_tensor(tmp_n[:, :], tmp_n[:, :], tally[:, 1, :], ALU.mult))
            ch.link(nc.vector.tensor_scalar_add(tmp_n[:, :], tmp_n[:, :], PAD_PLACE))
            nc.vector.memset(place[:, NW:NW + 2 * WB], 0)
            ch.link(nc.vector.tensor_copy(place[:, 0:NW], tmp_n[:, :]))
            ch.link(nc.vector.scalar_tensor_tensor(edge_end[:, :], tile_f[:, :], float(TE), tally[:, 2, :],
                                                   ALU.mult, ALU.add))
            nc.vector.tensor_copy(first_edge[:, 1:NW], edge_end[:, 0:NW - 1]).then_inc(c["dve_setup"].sem, 1)
            dve.wait_ge(setup_dma.sem, setup_dma.at(48))
            ch.link(nc.vector.tensor_tensor(degree[:, :], edge_end[:, :], first_edge[:, :], ALU.subtract))
            ch.link(nc.vector.tensor_scalar_max(inv_count[:, :], degree[:, :], 1.0))
            nc.vector.reciprocal(inv_count[:, :], inv_count[:, :])
            ch.link(nc.vector.tensor_scalar_add(tmp_n[:, :], degree[:, :], 1.0))
            ch.link(nc.vector.reciprocal(dinv[:, :], tmp_n[:, :]))
            dve_chain.close(ch.n)

        @block.tensor
        def _(pe):
            pe.wait_ge(c["pool_setup"].sem, c["pool_setup"].at(1))
            pe.wait_ge(c["x_turned_out"].sem, c["x_turned_out"].at(1))
            nc.tensor.matmul(bank(0)[0:NP, 0:1], before[:, :], held[:, :], start=True, stop=True
                             ).then_inc(c["x_turned"].sem, 1)

        @block.sync
        def _(sp):
            sp.dma_start(edge_before[0:1, :], zeros[0:1, 0:1]).then_inc(setup_dma.sem, 16)
            for n, k in enumerate((*stored, *tab_stored)):
                sp.dma_start(primed[n:n + 1, :], zeros[0:1, 0:1]).then_inc(k.sem, 16)
                k.close(16)
                sp.wait_ge(k.sem, k.at(0))
            sp.wait_ge(c["dve_setup"].sem, c["dve_setup"].at(1))
            sp.dma_start(edge_before[1:NP + 1, :], edge_end[:, NW - 1:NW], allow_slow_non_contiguous=True
                         ).then_inc(setup_dma.sem, 16)
            sp.wait_ge(setup_dma.sem, setup_dma.at(32))
            sp.dma_start(first_edge[:, 0:1], edge_before[0:NP, :], allow_slow_non_contiguous=True
                         ).then_inc(setup_dma.sem, 16)
            sp.wait_ge(setup_dma.sem, setup_dma.at(48))

    with nc.Block() as block:
        @block.scalar
        def _(act):
            nc.scalar.activation(dinv[:, :], dinv[:, :], ACT.Sqrt)
    setup_dma.close(48)
    for k in ("dve_setup", "pool_setup", "x_turned", "x_turned_out"):
        c[k].close(1)
    for s in range(2):
        idx_ready[s].close(NPAIR)
        gathered[s].close(16 * WB * NPAIR)
    work.close()
    setup.close()

    def nodes(t):
        return t.rearrange("(p w) f -> p w f", p=NP)

    def rows(t, wide=F):
        return t[0:NP, :].unsqueeze(1).to_broadcast([NP, WB, wide])

    def by_window(t, i, s):
        return t[:, bass.ds(i * 2 * WB + s * WB, WB)].unsqueeze(2).to_broadcast([NP, WB, F])

    def node_phase(kind, x_in, x_out, tab_in, tab_out, pre_only=False):
        buf = ExitStack()
        wide = RW if kind == "L3" else F
        run_rows = runs3 if kind == "L3" else runs
        xb = sb(kind + "_xb", [NP, 2, WB, F], at=buf)
        agg = sb(kind + "_agg", [NP, 2, WB, wide], at=buf)
        own = sb(kind + "_own", [NP, 2, WB, F], at=buf)
        res = sb(kind + "_res", [NP, WB, F], at=buf)
        nx = sb(kind + "_nx", [NP, 2, WB, F], at=buf)
        stats = sb(kind + "_stats", [NP, WB, 6], at=buf)
        mv = sb(kind + "_mv", [NP, WB, 2], at=buf)
        std = sb(kind + "_std", [NP, WB], at=buf)
        turned = sb(kind + "_turned", [F, 2, WB, NP], at=buf)
        tw = TW if kind == "L2b" else F
        tab = sb(kind + "_tab", [NP, 2, WB, tw], at=buf)
        fac = sb(kind + "_fac", [NP, WB, 3 * H], at=buf) if kind == "L3" else None
        pT = bank(0, 3)[:, 0:WB * 128].rearrange("p (w n) -> p w n", w=WB)
        pM = bank(3, 3)[:, 0:WB * 128].rearrange("p (w n) -> p w n", w=WB)
        pS = bank(6, 1)[:, 0:WB * 20].rearrange("p (w n) -> p w n", w=WB)
        has_agg = kind not in ("pre", "L0")
        parts = sb(kind + "_parts", [NP, 2, NACCS, WB, AW], at=buf) if kind == "L0" else None
        has_x = kind != "L2a"
        has_own = kind in ("L2a", "L2b")
        has_norm = kind in ("L0", "L1", "L2b", "L3")
        has_table = kind != "L3"
        n_loads = 16 * (has_x + has_own + NACCS * (kind == "L0"))
        dve_per = 0

        def window(i, s):
            return bass.ds(i * 2 * WB + s * WB, WB)

        with nc.Block() as block:
            @block.sync
            def _(sp):
                def load(i, s):
                    if has_x:
                        sp.dma_start(xb[:, s, :, :], nodes(x_in)[:, window(i, s), :]).then_inc(loaded[s].sem, 16)
                    if kind == "L0":
                        for k in range(NACCS):
                            sp.dma_start(parts[:, s, k, :, :], nodes(acc[k][0:N, :])[:, window(i, s), :]
                                         ).then_inc(loaded[s].sem, 16)
                    if has_own:
                        sp.dma_start(own[:, s, :, :], nodes(tab_in)[:, window(i, s), :]).then_inc(loaded[s].sem, 16)

                def store(i, s):
                    if has_norm:
                        sp.wait_ge(c["normed"].sem, c["normed"].at(2 * i + s + 1))
                        sp.dma_start(nodes(x_out)[:, window(i, s), :], nx[:, s, :, :]).then_inc(stored[s].sem, 16)
                    if has_table and kind != "pre":
                        sp.wait_ge(c["table_out"].sem, c["table_out"].at(2 * i + s + 1))
                        sp.dma_start(nodes(tab_out)[:, window(i, s), :], tab[:, s, :, :]).then_inc(tab_stored[s].sem, 16)

                load(0, 0)
                load(0, 1)
                with sp.Fori(0, NPAIR - 1) as i:
                    for s in range(2):
                        store(i, s)
                        sp.wait_ge(c["batch_done"].sem, c["batch_done"].at(2 * i + s + 1))
                        load(i + 1, s)
                store(NPAIR - 1, 0)
                store(NPAIR - 1, 1)
                for s in range(2):
                    if has_norm:
                        sp.wait_ge(stored[s].sem, stored[s].at(16 * NPAIR))
                    if has_table and kind != "pre":
                        sp.wait_ge(tab_stored[s].sem, tab_stored[s].at(16 * NPAIR))

            if kind == "pre":
                @block.gpsimd
                def _(pool):
                    with pool.Fori(0, NPAIR) as i:
                        for s in range(2):
                            pool.wait_ge(idx_ready[s].sem, idx_ready[s].at(i + 1))
                            pool.wait_ge(c["table_out"].sem, c["table_out"].at(2 * i + s + 1))
                            pool.sem_inc(pause.sem, 1)
                            for j in range(WB):
                                nc.gpsimd.indirect_dma_start(
                                    by_run, bass.IndirectOffsetOnAxis(ap=row_buf[:, s, j:j + 1], axis=0),
                                    tab[:, s, j, :], None, bounds_check=NACC - 1, oob_is_err=False
                                ).then_inc(gathered[s].sem, 16)
                    for s in range(2):
                        pool.wait_ge(gathered[s].sem, gathered[s].at(16 * WB * NPAIR))

            if has_agg:
                @block.gpsimd
                def _(pool):
                    with pool.Fori(0, NPAIR) as i:
                        for s in range(2):
                            pool.wait_ge(idx_ready[s].sem, idx_ready[s].at(i + 1))
                            pool.sem_inc(pause.sem, 1)
                            for j in range(WB):
                                nc.gpsimd.indirect_dma_start(
                                    agg[:, s, j, :], None, run_rows,
                                    bass.IndirectOffsetOnAxis(ap=row_buf[:, s, j:j + 1], axis=0)
                                ).then_inc(gathered[s].sem, 16)

            @block.tensor
            def _(pe):
                def turn(source, s, ready, n, done):
                    pe.wait_ge(c[ready].sem, c[ready].at(n))
                    for j in range(WB):
                        ins = nc.tensor.transpose(pT[:, j, 0:NP], source[:, s, j, 0:F] if s is not None else source[:, j, 0:F],
                                                  ident[0:NP, 0:NP])
                    ins.then_inc(c[done].sem, 1)

                with pe.Fori(0, NPAIR) as i:
                    for s in range(2):
                        n = 2 * i + s
                        if kind in ("pre", "L0"):
                            pe.wait_ge(loaded[s].sem, loaded[s].at(n_loads * (i + 1)))
                            turn(xb, s, "normed_turned_out" if kind == "L0" else "x_turned_out", n, "x_turned")
                        if kind not in ("pre", "L2b"):
                            if kind == "L0":
                                pe.wait_ge(c["x_turned_out"].sem, c["x_turned_out"].at(n + 1))
                            elif kind == "L1":
                                pe.wait_ge(c["normed_turned_out"].sem, c["normed_turned_out"].at(n))
                            if kind == "L1":
                                pe.wait_ge(gathered[s].sem, gathered[s].at(16 * WB * (i + 1)))
                            turn(agg, s, "agg_scaled" if kind != "L1" else "agg_turned_out", n + 1 if kind != "L1" else n,
                                 "agg_turned")
                            pe.wait_ge(c["agg_turned_out"].sem, c["agg_turned_out"].at(n + 1))
                        elif kind == "pre":
                            pe.wait_ge(c["x_turned_out"].sem, c["x_turned_out"].at(n + 1))
                        if kind in ("L0", "L1", "L3"):
                            if has_table:
                                pe.wait_ge(c["table_out"].sem, c["table_out"].at(n))
                            w = {"L0": None, "L1": m["Wn2"], "L3": m["Wout"]}[kind]
                            if not has_table:
                                pe.wait_ge(c["residual"].sem, c["residual"].at(n))
                            for j in range(WB):
                                if kind == "L0":
                                    nc.tensor.matmul(pM[0:NP, j, :], turned[:, 0, j, :], m["W2"][:, 0, :], start=True, stop=False)
                                    ins = nc.tensor.matmul(pM[0:NP, j, :], turned[:, 1, j, :], m["W2"][:, 1, :], start=False, stop=True)
                                else:
                                    ins = nc.tensor.matmul(pM[0:NP, j, :], turned[:, 1, j, :], w[:, :], start=True, stop=True)
                            ins.then_inc(c["product"].sem, 1)
                        if has_norm and has_table:
                            turn(nx, s, "normed", n + 1, "normed_turned")
                            pe.wait_ge(c["normed_turned_out"].sem, c["normed_turned_out"].at(n + 1))
                        if has_table:
                            slot = 0 if kind not in ("L2a",) else 1
                            if kind in ("pre", "L2a"):
                                pe.wait_ge(c["table_out"].sem, c["table_out"].at(n))
                            elif kind in ("L0", "L1"):
                                pe.wait_ge(c["product_out"].sem, c["product_out"].at(n + 1))
                            else:
                                pe.wait_ge(c["table_out"].sem, c["table_out"].at(n))
                            w = {"pre": m["W1"][:, :], "L0": m["Wn1"][:, 0, :], "L1": m["gcn_W1"][:, :],
                                 "L2a": m["gcn_W2"][:, :], "L2b": m["Wv"][:, :]}[kind]
                            for j in range(WB):
                                ins = nc.tensor.matmul(pM[0:NP, j, :], turned[:, slot, j, :], w, start=True, stop=True)
                                if kind == "L2b":
                                    ins = nc.tensor.matmul(pS[0:NP, j, :], turned[:, slot, j, :], score_w[:, :], start=True, stop=True)
                            ins.then_inc(c["table_product"].sem, 1)

            @block.scalar
            def _(act):
                with act.Fori(0, NPAIR) as i:
                    for s in range(2):
                        n = 2 * i + s
                        if kind in ("pre", "L0"):
                            sc, sh = (bn1_scale[:, 0:1], bn1_shift[:, 0:1]) if kind == "pre" else (bn2_scale[:, 0:1], bn2_shift[:, 0:1])
                            act.wait_ge(c["x_turned"].sem, c["x_turned"].at(n + 1))
                            act.wait_ge(c["table_product"].sem, c["table_product"].at(n))
                            nc.scalar.activation(turned[:, 0, :, :], pT[:, :, 0:NP], ACT.Identity, bias=sh, scale=sc
                                                 ).then_inc(c["x_turned_out"].sem, 1)
                        if kind == "L3":
                            act.wait_ge(c["exponent"].sem, c["exponent"].at(n + 1))
                            nc.scalar.activation(fac[:, :, H:2 * H], fac[:, :, H:2 * H], ACT.Exp).then_inc(c["exponent_out"].sem, 1)
                        if kind not in ("pre", "L2b"):
                            act.wait_ge(c["agg_turned"].sem, c["agg_turned"].at(n + 1))
                            if kind == "L0":
                                nc.scalar.activation(turned[:, 1, :, :], pT[:, :, 0:NP], ACT.Identity, bias=bn2_shift[:, 1:2],
                                                     scale=bn2_scale[:, 1:2]).then_inc(c["agg_turned_out"].sem, 1)
                            elif kind == "L2a":
                                act.wait_ge(c["table_product"].sem, c["table_product"].at(n))
                                nc.scalar.activation(turned[:, 1, :, :], pT[:, :, 0:NP], ACT.Relu, bias=m["gcn_b1"][:, 0:1]
                                                     ).then_inc(c["agg_turned_out"].sem, 1)
                            elif kind in ("L1", "L3"):
                                nc.scalar.activation(turned[:, 1, :, :], pT[:, :, 0:NP], ACT.Copy
                                                     ).then_inc(c["agg_turned_out"].sem, 1)
                        if kind == "L0":
                            act.wait_ge(c["product_out"].sem, c["product_out"].at(n + 1))
                            nc.scalar.activation(res[:, :, :], res[:, :, :], ACT.Gelu).then_inc(c["activated"].sem, 1)
                        if kind == "L2b":
                            act.wait_ge(c["product_out"].sem, c["product_out"].at(n + 1))
                            nc.scalar.activation(res[:, :, :], res[:, :, :], ACT.Relu).then_inc(c["activated"].sem, 1)
                        if has_norm:
                            act.wait_ge(c["variance"].sem, c["variance"].at(n + 1))
                            nc.scalar.activation(std[:, :], mv[:, :, 1], ACT.Sqrt, bias=eps_ln[0:NP, :]
                                                 ).then_inc(c["deviation"].sem, 1)
                        if has_norm and has_table:
                            act.wait_ge(c["normed_turned"].sem, c["normed_turned"].at(n + 1))
                            nc.scalar.activation(turned[:, 0, :, :], pT[:, :, 0:NP], ACT.Copy
                                                 ).then_inc(c["normed_turned_out"].sem, 1)
                        if kind == "pre":
                            act.wait_ge(c["residual"].sem, c["residual"].at(n + 1))
                            nc.scalar.activation(tab[:, s, :, :], tab[:, s, :, :], ACT.Gelu).then_inc(c["table_out"].sem, 1)

            @block.vector
            def _(dve):
                per = {"pre": 0, "L0": 7, "L1": 4, "L2a": 1, "L2b": 6, "L3": 8}[kind]
                numbers = place if kind == "pre" else node_row
                if has_agg:
                    for s in range(2):
                        nc.vector.tensor_copy(row_buf[:, s, :], node_row[:, s * WB:(s + 1) * WB]).then_inc(idx_ready[s].sem, 1)
                with dve.Fori(0, NPAIR) as i:
                    for s in range(2):
                        n = 2 * i + s
                        ch = Chain(dve, dve_chain, per, n)
                        if kind == "pre":
                            dve.wait_ge(gathered[s].sem, gathered[s].at(16 * WB * i))
                            dve.sem_inc(pause.sem, 1)
                            nc.vector.tensor_copy(row_buf[:, s, :], place[:, window(i, s)]).then_inc(idx_ready[s].sem, 1)
                        if has_agg:
                            dve.wait_ge(gathered[s].sem, gathered[s].at(16 * WB * (i + 1)))
                            if kind != "L0" and n_loads:
                                dve.wait_ge(loaded[s].sem, loaded[s].at(n_loads * (i + 1)))
                        if kind == "L0":
                            dve.wait_ge(loaded[s].sem, loaded[s].at(n_loads * (i + 1)))
                            dve.sem_inc(pause.sem, 1)
                            whole = parts[:, s, :, :, :].rearrange("p k w f -> p k (w f)")
                            nc.vector.tensor_tensor(whole[:, 0:2, :], whole[:, 0:2, :], whole[:, 2:4, :], ALU.add
                                                    ).then_inc(dve_chain.sem, 1)
                            ch.n += 1
                            dve.wait_ge(dve_chain.sem, dve_chain.at(per * n + ch.n))
                            ch.link(nc.vector.tensor_tensor(whole[:, 0, :], whole[:, 0, :], whole[:, 1, :], ALU.add))
                            ch.link(nc.vector.tensor_scalar(std[:, :], parts[:, s, 0, :, F], 1.0, None, ALU.max))
                            ch.link(nc.vector.reciprocal(std[:, :], std[:, :]))
                            nc.vector.tensor_tensor(agg[:, s, :, :], parts[:, s, 0, :, 0:F],
                                                    std[:, :].unsqueeze(2).to_broadcast([NP, WB, F]), ALU.mult
                                                    ).then_inc(c["agg_scaled"].sem, 1)
                            dve.wait_ge(c["product"].sem, c["product"].at(n + 1))
                            nc.vector.tensor_tensor(res[:, :, :], pM[0:NP, :, :], rows(m["b2_rows"]), ALU.add
                                                    ).then_inc(c["product_out"].sem, 1)
                            dve.wait_ge(c["activated"].sem, c["activated"].at(n + 1))
                            ch.link(nc.vector.tensor_tensor(res[:, :, :], res[:, :, :], xb[:, s, :, :], ALU.add))
                        if kind == "L1":
                            ch.link(nc.vector.tensor_tensor(res[:, :, :], by_window(degree, i, s), rows(m["nb2_rows"]), ALU.mult))
                            ch.link(nc.vector.scalar_tensor_tensor(res[:, :, :], xb[:, s, :, :], 2.0, res[:, :, :], ALU.mult, ALU.add))
                            dve.wait_ge(c["product"].sem, c["product"].at(n + 1))
                            ins = nc.vector.tensor_tensor(res[:, :, :], res[:, :, :], pM[0:NP, :, :], ALU.add)
                            ins.then_inc(c["product_out"].sem, 1)
                            dve.wait_ge(c["product_out"].sem, c["product_out"].at(n + 1))
                        if kind == "L2a":
                            ch.link(nc.vector.tensor_tensor(agg[:, s, :, :], agg[:, s, :, :], own[:, s, :, :], ALU.add))
                            nc.vector.tensor_tensor(agg[:, s, :, :], agg[:, s, :, :], by_window(dinv, i, s), ALU.mult
                                                    ).then_inc(c["agg_scaled"].sem, 1)
                        if kind == "L2b":
                            ch.link(nc.vector.tensor_tensor(res[:, :, :], agg[:, s, :, :], own[:, s, :, :], ALU.add))
                            ch.link(nc.vector.tensor_tensor(res[:, :, :], res[:, :, :], by_window(dinv, i, s), ALU.mult))
                            ch.link(nc.vector.tensor_tensor(res[:, :, :], res[:, :, :], rows(m["gcn_b2_rows"]), ALU.add))
                            nc.vector.tensor_tensor(res[:, :, :], res[:, :, :], xb[:, s, :, :], ALU.add
                                                    ).then_inc(c["product_out"].sem, 1)
                            dve.wait_ge(c["activated"].sem, c["activated"].at(n + 1))
                            ch.link(nc.vector.tensor_tensor(res[:, :, :], res[:, :, :], xb[:, s, :, :], ALU.add))
                        if kind == "L3":
                            top, f, den = fac[:, :, 0:H], fac[:, :, H:2 * H], fac[:, :, 2 * H:3 * H]
                            got_m, got_d = agg[:, s, :, F + H:F + 2 * H], agg[:, s, :, F:F + H]
                            ch.link(nc.vector.tensor_scalar(top, got_m, MAX_FLOOR, None, ALU.max))
                            nc.vector.tensor_tensor(f, got_m, top, ALU.subtract).then_inc(c["exponent"].sem, 1)
                            dve.wait_ge(c["exponent_out"].sem, c["exponent_out"].at(n + 1))
                            ch.link(nc.vector.tensor_tensor(den, got_d, f, ALU.mult))
                            ch.link(nc.vector.tensor_scalar_add(den, den, DEN_EPS))
                            ch.link(nc.vector.reciprocal(den, den))
                            ch.link(nc.vector.tensor_tensor(f, f, den, ALU.mult))
                            for j in range(WB):
                                hj = agg[:, s, j, 0:F].rearrange("p (h d) -> p h d", h=H)
                                ins = nc.vector.tensor_tensor(hj, hj, fac[:, j, H:2 * H].unsqueeze(2).to_broadcast([NP, H, HD]), ALU.mult)
                            ins.then_inc(c["agg_scaled"].sem, 1)
                            ch.link(nc.vector.tensor_tensor(res[:, :, :], xb[:, s, :, :], rows(m["bout_rows"]), ALU.add))
                            dve.wait_ge(c["product"].sem, c["product"].at(n + 1))
                            nc.vector.tensor_tensor(res[:, :, :], res[:, :, :], pM[0:NP, :, :], ALU.add
                                                    ).then_inc(c["residual"].sem, 1)
                            dve.wait_ge(c["residual"].sem, c["residual"].at(n + 1))
                        if has_norm:
                            for j in range(WB):
                                ins = nc.vector.bn_stats(stats[:, j, :], res[:, j, :])
                            ch.link(ins)
                            dve.sem_inc(pause.sem, 1)
                            for j in range(WB):
                                ins = nc.vector.bn_aggr(mv[:, j, :], stats[:, j, :])
                            ins.then_inc(c["variance"].sem, 1)
                            dve.wait_ge(c["deviation"].sem, c["deviation"].at(n + 1))
                            dve.wait_ge(stored[s].sem, stored[s].at(16 * i))
                            ch.link(nc.vector.reciprocal(std[:, :], std[:, :]))
                            for j in range(WB):
                                ins = nc.vector.tensor_scalar(nx[:, s, j, :], res[:, j, :], mv[:, j, 0:1], std[:, j:j + 1],
                                                              ALU.subtract, ALU.mult)
                            ins.then_inc(c["normed"].sem, 1)
                        if has_table:
                            dve.wait_ge(c["table_product"].sem, c["table_product"].at(n + 1))
                            if kind != "pre":
                                dve.wait_ge(tab_stored[s].sem, tab_stored[s].at(16 * i))
                            if kind == "pre":
                                nc.vector.tensor_tensor(tab[:, s, :, :], pM[0:NP, :, :], rows(m["b1_rows"]), ALU.add
                                                        ).then_inc(c["residual"].sem, 1)
                                dve.wait_ge(c["table_out"].sem, c["table_out"].at(n + 1))
                            if kind == "L0":
                                nc.vector.tensor_tensor(tab[:, s, :, :], pM[0:NP, :, :], rows(m["nb1_rows"]), ALU.add
                                                        ).then_inc(c["table_out"].sem, 1)
                            if kind in ("L1", "L2a"):
                                nc.vector.tensor_tensor(tab[:, s, :, :], pM[0:NP, :, :], by_window(dinv, i, s), ALU.mult
                                                        ).then_inc(c["table_out"].sem, 1)
                            if kind == "L2b":
                                nc.vector.tensor_copy(tab[:, s, :, 0:F], pM[0:NP, :, :])
                                nc.vector.tensor_copy(kd_node[:, window(i, s), :], pS[0:NP, :, (1 + KINDS) * H:(2 + KINDS) * H])
                                nc.vector.tensor_copy(tab[:, s, :, F:TW], pS[0:NP, :, 0:(1 + KINDS) * H]
                                                      ).then_inc(c["table_out"].sem, 1)
                        if has_agg:
                            ahead = bass.ds((i * 2 + 2) * WB + s * WB, WB)
                            nc.vector.tensor_copy(row_buf[:, s, :], node_row[:, ahead]).then_inc(idx_ready[s].sem, 1)
                        dve.sem_inc(c["batch_done"].sem, 1)
                        assert ch.n == per or per == 0, (kind, ch.n)
                dve_chain.close(per * 2 * NPAIR)
        buf.close()
        n = 2 * NPAIR
        if has_agg or kind == "pre":
            for s in range(2):
                gathered[s].close(16 * WB * NPAIR)
                idx_ready[s].close(NPAIR + has_agg)
        for s in range(2):
            loaded[s].close(n_loads * NPAIR)
            stored[s].close(16 * NPAIR * has_norm)
            tab_stored[s].close(16 * NPAIR * (has_table and kind != "pre"))
        ran = ["batch_done"]
        ran += {"pre": ["x_turned", "x_turned_out", "residual"],
                "L0": ["x_turned", "x_turned_out", "agg_scaled", "agg_turned", "agg_turned_out", "product", "product_out", "activated"],
                "L1": ["agg_turned", "agg_turned_out", "product", "product_out"],
                "L2a": ["agg_scaled", "agg_turned", "agg_turned_out"],
                "L2b": ["product_out", "activated"],
                "L3": ["exponent", "exponent_out", "agg_scaled", "agg_turned", "agg_turned_out", "product", "residual"]}[kind]
        ran += ["variance", "deviation", "normed"] * has_norm + ["normed_turned", "normed_turned_out"] * (has_norm and has_table)
        ran += ["table_product", "table_out"] * has_table
        for k in ran:
            c[k].close(n)

    def node_layer(kind, x_in, x_out, tab_in, tab_out):
        buf = ExitStack()
        has_agg, has_own = kind != "L0", kind == "L2b"
        has_product, has_table = kind != "L2b", kind != "L3"
        wide = RW if kind == "L3" else F
        run_rows = runs3 if kind == "L3" else runs
        xb = sb(kind + "_xb", [NP, 2, WB, F], at=buf)
        agg = sb(kind + "_agg", [NP, 2, WB, wide], at=buf)
        own = sb(kind + "_own", [NP, 2, WB, F], at=buf) if has_own else None
        res = sb(kind + "_res", [NP, 2, WB, F], at=buf)
        nx = sb(kind + "_nx", [NP, 2, WB, F], at=buf)
        stats = sb(kind + "_stats", [NP, WB, 6], at=buf)
        mv = sb(kind + "_mv", [NP, WB, 2], at=buf)
        std = sb(kind + "_std", [NP, WB], at=buf)
        turned = sb(kind + "_turned", [F, 2, WB, NP], at=buf)
        tab = sb(kind + "_tab", [NP, 2, WB, TW if kind == "L2b" else F], at=buf) if has_table else None
        parts = sb(kind + "_parts", [NP, 2, NACCS, WB, AW], at=buf) if kind == "L0" else None
        shared = sb(kind + "_shared", [NP, WB], at=buf)
        fac = sb(kind + "_fac", [NP, WB, 3 * H], at=buf)
        pT = bank(0, 3)[:, 0:WB * 128].rearrange("p (w n) -> p w n", w=WB)
        pM = bank(3, 3)[:, 0:WB * 128].rearrange("p (w n) -> p w n", w=WB)
        pS = bank(6, 1)[:, 0:WB * 20].rearrange("p (w n) -> p w n", w=WB)
        n_loads = 16 * (1 + has_own)
        LAST = NPAIR - 1
        update_chain, norm_chain = stage_chains
        per_update = {"L0": 3, "L1": 1, "L2b": 3, "L3": 5}[kind]
        per_norm = {"L0": 3, "L1": 2, "L2b": 3, "L3": 2}[kind]

        def window(i, s):
            return bass.ds(i * 2 * WB + s * WB, WB)

        def steps(eng, step):
            step(0, 0, None, (0, 1))
            step(0, 1, (0, 0), (1, 0))
            with eng.Fori(1, LAST) as i:
                step(i, 0, (i - 1, 1), (i, 1))
                step(i, 1, (i, 0), (i + 1, 0))
            step(LAST, 0, (LAST - 1, 1), (LAST, 1))
            step(LAST, 1, (LAST, 0), None)

        with nc.Block() as block:
            @block.sync
            def _(sp):
                def load(i, s):
                    sp.dma_start(xb[:, s, :, :], nodes(x_in)[:, window(i, s), :]).then_inc(loaded[s].sem, 16)
                    if has_own:
                        sp.dma_start(own[:, s, :, :], nodes(tab_in)[:, window(i, s), :]).then_inc(loaded[s].sem, 16)

                def load_parts(i, s):
                    for k in range(NACCS):
                        sp.dma_start(parts[:, s, k, :, :], nodes(acc[k][0:N, :])[:, window(i, s), :]
                                     ).then_inc(window_in[s].sem, 16)

                def store_table(i, s):
                    sp.wait_ge(c["table_out"].sem, c["table_out"].at(2 * i + s + 1))
                    sp.dma_start(nodes(tab_out)[:, window(i, s), :], tab[:, s, :, :]).then_inc(tab_stored[s].sem, 16)

                def step(i, s, before, after):
                    n = 2 * i + s
                    ends = isinstance(i, int) and i == LAST
                    if kind == "L0" and not ends:
                        sp.wait_ge(c["agg_scaled"].sem, c["agg_scaled"].at(n + 1))
                        load_parts(i + 1, s)
                    if before and has_table:
                        store_table(*before)
                    if not ends:
                        sp.wait_ge(c["batch_done"].sem, c["batch_done"].at(n + 1))
                        load(i + 1, s)
                    sp.wait_ge(c["normed"].sem, c["normed"].at(n + 1))
                    sp.dma_start(nodes(x_out)[:, window(i, s), :], nx[:, s, :, :]).then_inc(stored[s].sem, 16)
                    if not after and has_table:
                        store_table(i, s)

                for s in range(2):
                    load(0, s)
                    if kind == "L0":
                        load_parts(0, s)
                steps(sp, step)
                for s in range(2):
                    sp.wait_ge(stored[s].sem, stored[s].at(16 * NPAIR))
                    if has_table:
                        sp.wait_ge(tab_stored[s].sem, tab_stored[s].at(16 * NPAIR))

            if has_agg:
                @block.gpsimd
                def _(pool):
                    with pool.Fori(0, NPAIR) as i:
                        for s in range(2):
                            pool.wait_ge(idx_ready[s].sem, idx_ready[s].at(i + 1))
                            pool.sem_inc(pause.sem, 1)
                            for j in range(WB):
                                nc.gpsimd.indirect_dma_start(
                                    agg[:, s, j, :], None, run_rows,
                                    bass.IndirectOffsetOnAxis(ap=row_buf[:, s, j:j + 1], axis=0)
                                ).then_inc(gathered[s].sem, 16)

            @block.tensor
            def _(pe):
                def turn(source, s, done):
                    for j in range(WB):
                        ins = nc.tensor.transpose(pT[:, j, 0:NP], source[:, s, j, 0:F], ident[0:NP, 0:NP])
                    ins.then_inc(c[done].sem, 1)

                def update(i, s):
                    n = 2 * i + s
                    if kind == "L0":
                        pe.wait_ge(loaded[s].sem, loaded[s].at(n_loads * (i + 1)))
                        turn(xb, s, "x_turned")
                        pe.wait_ge(c["x_turned_out"].sem, c["x_turned_out"].at(n + 1))
                    if kind == "L1":
                        pe.wait_ge(gathered[s].sem, gathered[s].at(16 * WB * (i + 1)))
                    else:
                        pe.wait_ge(c["agg_scaled"].sem, c["agg_scaled"].at(n + 1))
                    pe.sem_inc(pause.sem, 1)
                    turn(agg, s, "agg_turned")
                    pe.wait_ge(c["agg_turned_out"].sem, c["agg_turned_out"].at(n + 1))
                    wait(pe, c["product_out"], n)
                    if has_table:
                        wait(pe, c["table_out"], n - 1)
                    pe.sem_inc(pause.sem, 1)
                    w = {"L0": None, "L1": m["Wn2"], "L3": m["Wout"]}[kind]
                    for j in range(WB):
                        if kind == "L0":
                            nc.tensor.matmul(pM[0:NP, j, :], turned[:, 0, j, :], m["W2"][:, 0, :], start=True, stop=False)
                            ins = nc.tensor.matmul(pM[0:NP, j, :], turned[:, 1, j, :], m["W2"][:, 1, :], start=False, stop=True)
                        else:
                            ins = nc.tensor.matmul(pM[0:NP, j, :], turned[:, 1, j, :], w[:, :], start=True, stop=True)
                    ins.then_inc(c["product"].sem, 1)

                def table(i, s, after):
                    n = 2 * i + s
                    pe.wait_ge(c["normed"].sem, c["normed"].at(n + 1))
                    pe.sem_inc(pause.sem, 1)
                    turn(nx, s, "normed_turned")
                    pe.wait_ge(c["normed_turned_out"].sem, c["normed_turned_out"].at(n + 1))
                    if has_product:
                        pe.wait_ge(c["product_out"].sem, c["product_out"].at(n + 2 if after else n + 1))
                    else:
                        wait(pe, c["table_out"], n)
                    pe.sem_inc(pause.sem, 1)
                    w = {"L0": m["Wn1"][:, 0, :], "L1": m["gcn_W1"][:, :], "L2b": m["Wv"][:, :]}[kind]
                    for j in range(WB):
                        ins = nc.tensor.matmul(pM[0:NP, j, :], turned[:, 0, j, :], w, start=True, stop=True)
                        if kind == "L2b":
                            ins = nc.tensor.matmul(pS[0:NP, j, :], turned[:, 0, j, :], score_w[:, :], start=True, stop=True)
                    ins.then_inc(c["table_product"].sem, 1)

                def step(i, s, before, after):
                    if has_product and not before:
                        update(i, s)
                    if has_product and after:
                        update(*after)
                    if has_table:
                        table(i, s, after)

                steps(pe, step)

            @block.scalar
            def _(act):
                def update(i, s):
                    n = 2 * i + s
                    if kind == "L3":
                        act.wait_ge(c["exponent"].sem, c["exponent"].at(n + 1))
                        nc.scalar.activation(fac[:, :, H:2 * H], fac[:, :, H:2 * H], ACT.Exp).then_inc(c["exponent_out"].sem, 1)
                    if kind == "L0":
                        act.wait_ge(c["x_turned"].sem, c["x_turned"].at(n + 1))
                        nc.scalar.activation(turned[:, 0, :, :], pT[:, :, 0:NP], ACT.Identity, bias=bn2_shift[:, 0:1],
                                             scale=bn2_scale[:, 0:1]).then_inc(c["x_turned_out"].sem, 1)
                    act.wait_ge(c["agg_turned"].sem, c["agg_turned"].at(n + 1))
                    if kind == "L0":
                        nc.scalar.activation(turned[:, 1, :, :], pT[:, :, 0:NP], ACT.Identity, bias=bn2_shift[:, 1:2],
                                             scale=bn2_scale[:, 1:2]).then_inc(c["agg_turned_out"].sem, 1)
                    else:
                        nc.scalar.activation(turned[:, 1, :, :], pT[:, :, 0:NP], ACT.Copy).then_inc(c["agg_turned_out"].sem, 1)

                def step(i, s, before, after):
                    n = 2 * i + s
                    if has_product and not before:
                        update(i, s)
                    if kind in ("L0", "L2b"):
                        act.wait_ge(c["product_out"].sem, c["product_out"].at(n + 1))
                        nc.scalar.activation(res[:, s, :, :], res[:, s, :, :], ACT.Gelu if kind == "L0" else ACT.Relu
                                             ).then_inc(c["activated"].sem, 1)
                    if has_product and after:
                        update(*after)
                    act.wait_ge(c["variance"].sem, c["variance"].at(n + 1))
                    nc.scalar.activation(std[:, :], mv[:, :, 1], ACT.Sqrt, bias=eps_ln[0:NP, :]).then_inc(c["deviation"].sem, 1)
                    if has_table:
                        act.wait_ge(c["normed_turned"].sem, c["normed_turned"].at(n + 1))
                        nc.scalar.activation(turned[:, 0, :, :], pT[:, :, 0:NP], ACT.Copy).then_inc(c["normed_turned_out"].sem, 1)

                steps(act, step)

            @block.vector
            def _(dve):
                def next_rows(i, s):
                    ahead = bass.ds((i * 2 + 2 + s) * WB, WB)
                    nc.vector.tensor_copy(row_buf[:, s, :], node_row[:, ahead]).then_inc(idx_ready[s].sem, 1)

                def update(i, s):
                    n = 2 * i + s
                    ch = Chain(dve, update_chain, per_update, n)
                    wait(dve, c["normed"], n - 1)
                    if has_agg:
                        dve.wait_ge(gathered[s].sem, gathered[s].at(16 * WB * (i + 1)))
                        dve.wait_ge(loaded[s].sem, loaded[s].at(n_loads * (i + 1)))
                    else:
                        dve.wait_ge(window_in[s].sem, window_in[s].at(16 * NACCS * (i + 1)))
                    dve.sem_inc(pause.sem, 1)
                    if kind == "L0":
                        whole = parts[:, s, :, :, :].rearrange("p k w f -> p k (w f)")
                        ch.link(nc.vector.tensor_tensor(whole[:, 0:2, :], whole[:, 0:2, :], whole[:, 2:4, :], ALU.add))
                        ch.link(nc.vector.tensor_tensor(whole[:, 0, :], whole[:, 0, :], whole[:, 1, :], ALU.add))
                        ch.link(nc.vector.tensor_scalar(shared[:, :], parts[:, s, 0, :, F], 1.0, None, ALU.max))
                        nc.vector.reciprocal(shared[:, :], shared[:, :]).then_inc(c["exponent"].sem, 1)
                        dve.wait_ge(c["exponent"].sem, c["exponent"].at(n + 1))
                        nc.vector.tensor_tensor(agg[:, s, :, :], parts[:, s, 0, :, 0:F],
                                                shared[:, :].unsqueeze(2).to_broadcast([NP, WB, F]), ALU.mult
                                                ).then_inc(c["agg_scaled"].sem, 1)
                    if kind == "L1":
                        ch.link(nc.vector.tensor_tensor(res[:, s, :, :], by_window(degree, i, s), rows(m["nb2_rows"]), ALU.mult))
                        nc.vector.scalar_tensor_tensor(res[:, s, :, :], xb[:, s, :, :], 2.0, res[:, s, :, :], ALU.mult, ALU.add
                                                       ).then_inc(c["batch_done"].sem, 1)
                    if kind == "L2b":
                        ch.link(nc.vector.tensor_tensor(res[:, s, :, :], agg[:, s, :, :], own[:, s, :, :], ALU.add))
                        next_rows(i, s)
                        ch.link(nc.vector.tensor_tensor(res[:, s, :, :], res[:, s, :, :], by_window(dinv, i, s), ALU.mult))
                        ch.link(nc.vector.tensor_tensor(res[:, s, :, :], res[:, s, :, :], rows(m["gcn_b2_rows"]), ALU.add))
                        nc.vector.tensor_tensor(res[:, s, :, :], res[:, s, :, :], xb[:, s, :, :], ALU.add
                                                ).then_inc(c["product_out"].sem, 1)
                    if kind == "L3":
                        top, f, den = fac[:, :, 0:H], fac[:, :, H:2 * H], fac[:, :, 2 * H:3 * H]
                        got_m, got_d = agg[:, s, :, F + H:F + 2 * H], agg[:, s, :, F:F + H]
                        ch.link(nc.vector.tensor_scalar(top, got_m, MAX_FLOOR, None, ALU.max))
                        nc.vector.tensor_tensor(f, got_m, top, ALU.subtract).then_inc(c["exponent"].sem, 1)
                        nc.vector.tensor_tensor(res[:, s, :, :], xb[:, s, :, :], rows(m["bout_rows"]), ALU.add
                                                ).then_inc(c["batch_done"].sem, 1)
                        dve.wait_ge(c["exponent_out"].sem, c["exponent_out"].at(n + 1))
                        ch.link(nc.vector.tensor_tensor(den, got_d, f, ALU.mult))
                        ch.link(nc.vector.tensor_scalar_add(den, den, DEN_EPS))
                        ch.link(nc.vector.reciprocal(den, den))
                        ch.link(nc.vector.tensor_tensor(f, f, den, ALU.mult))
                        for j in range(WB):
                            hj = agg[:, s, j, 0:F].rearrange("p (h d) -> p h d", h=H)
                            ins = nc.vector.tensor_tensor(hj, hj, fac[:, j, H:2 * H].unsqueeze(2).to_broadcast([NP, H, HD]), ALU.mult)
                        ins.then_inc(c["agg_scaled"].sem, 1)
                    assert ch.n == per_update, (kind, ch.n)

                def add_product(i, s):
                    n = 2 * i + s
                    dve.wait_ge(c["product"].sem, c["product"].at(n + 1))
                    if kind == "L0":
                        ins = nc.vector.tensor_tensor(res[:, s, :, :], pM[0:NP, :, :], rows(m["b2_rows"]), ALU.add)
                    else:
                        if kind == "L1":
                            dve.wait_ge(c["batch_done"].sem, c["batch_done"].at(n + 1))
                        dve.sem_inc(pause.sem, 1)
                        ins = nc.vector.tensor_tensor(res[:, s, :, :], res[:, s, :, :], pM[0:NP, :, :], ALU.add)
                    ins.then_inc(c["product_out"].sem, 1)
                    dve.wait_ge(c["product_out"].sem, c["product_out"].at(n + 1))
                    if has_agg:
                        next_rows(i, s)

                def norm(i, s):
                    n = 2 * i + s
                    ch = Chain(dve, norm_chain, per_norm, n)
                    if kind in ("L0", "L2b"):
                        dve.wait_ge(c["activated"].sem, c["activated"].at(n + 1))
                        if kind == "L0":
                            dve.wait_ge(loaded[s].sem, loaded[s].at(n_loads * (i + 1)))
                        dve.sem_inc(pause.sem, 1)
                        ch.link(nc.vector.tensor_tensor(res[:, s, :, :], res[:, s, :, :], xb[:, s, :, :], ALU.add))
                        dve.sem_inc(c["batch_done"].sem, 1)
                    for j in range(WB):
                        ins = nc.vector.bn_stats(stats[:, j, :], res[:, s, j, :])
                    ch.link(ins)
                    dve.sem_inc(pause.sem, 1)
                    for j in range(WB):
                        ins = nc.vector.bn_aggr(mv[:, j, :], stats[:, j, :])
                    ins.then_inc(c["variance"].sem, 1)
                    dve.wait_ge(c["deviation"].sem, c["deviation"].at(n + 1))
                    dve.wait_ge(stored[s].sem, stored[s].at(16 * i))
                    ch.link(nc.vector.reciprocal(std[:, :], std[:, :]))
                    for j in range(WB):
                        ins = nc.vector.tensor_scalar(nx[:, s, j, :], res[:, s, j, :], mv[:, j, 0:1], std[:, j:j + 1],
                                                      ALU.subtract, ALU.mult)
                    ins.then_inc(c["normed"].sem, 1)
                    assert ch.n == per_norm, (kind, ch.n)

                def table(i, s):
                    n = 2 * i + s
                    dve.wait_ge(c["table_product"].sem, c["table_product"].at(n + 1))
                    dve.wait_ge(tab_stored[s].sem, tab_stored[s].at(16 * i))
                    if kind == "L0":
                        ins = nc.vector.tensor_tensor(tab[:, s, :, :], pM[0:NP, :, :], rows(m["nb1_rows"]), ALU.add)
                    if kind == "L1":
                        ins = nc.vector.tensor_tensor(tab[:, s, :, :], pM[0:NP, :, :], by_window(dinv, i, s), ALU.mult)
                    if kind == "L2b":
                        dve.sem_inc(pause.sem, 1)
                        nc.vector.tensor_copy(tab[:, s, :, 0:F], pM[0:NP, :, :])
                        nc.vector.tensor_copy(kd_node[:, window(i, s), :], pS[0:NP, :, (1 + KINDS) * H:(2 + KINDS) * H])
                        ins = nc.vector.tensor_copy(tab[:, s, :, F:TW], pS[0:NP, :, 0:(1 + KINDS) * H])
                    ins.then_inc(c["table_out"].sem, 1)

                def step(i, s, before, after):
                    if not before:
                        update(i, s)
                    if has_product:
                        add_product(i, s)
                    if after:
                        update(*after)
                    if before and has_table:
                        table(*before)
                    norm(i, s)
                    if not after and has_table:
                        table(i, s)

                if has_agg:
                    for s in range(2):
                        nc.vector.tensor_copy(row_buf[:, s, :], node_row[:, s * WB:(s + 1) * WB]).then_inc(idx_ready[s].sem, 1)
                steps(dve, step)
        buf.close()
        n = 2 * NPAIR
        for s in range(2):
            if has_agg:
                gathered[s].close(16 * WB * NPAIR)
                idx_ready[s].close(NPAIR + 1)
            else:
                window_in[s].close(16 * NACCS * NPAIR)
            loaded[s].close(n_loads * NPAIR)
            stored[s].close(16 * NPAIR)
            tab_stored[s].close(16 * NPAIR * has_table)
        ran = ["batch_done", "variance", "deviation", "normed"]
        ran += {"L0": ["x_turned", "x_turned_out", "agg_scaled", "activated", "exponent"], "L1": [], "L2b": ["activated"],
                "L3": ["exponent", "exponent_out", "agg_scaled"]}[kind]
        ran += ["agg_turned", "agg_turned_out", "product"] * has_product + ["product_out"]
        ran += ["normed_turned", "normed_turned_out", "table_product", "table_out"] * has_table
        for k in ran:
            c[k].close(n)
        update_chain.close(per_update * n)
        norm_chain.close(per_norm * n)

    run_view = runs.rearrange("(r t) f -> r t f", t=NT)

    def halves(i, s):
        return bass.ds((2 * i + s) * HB, HB)

    def edge_pass(name, tab_in):
        buf = ExitStack()
        got = sb(name + "_got", [TE, 2, HB, F], at=buf)
        onehot = sb(name + "_onehot", [TE, 2, HB, TE], at=buf)
        sums = sb(name + "_sums", [TE, 2, HB, F], at=buf)
        with nc.Block() as block:
            @block.gpsimd
            def _(pool):
                with pool.Fori(0, NPASS) as i:
                    for s in range(2):
                        pool.wait_ge(idx_ready[s].sem, idx_ready[s].at(i + 1))
                        pool.sem_inc(pause.sem, 1)
                        for t in range(HB):
                            nc.gpsimd.indirect_dma_start(got[:, s, t, :], None, tab_in, bass.IndirectOffsetOnAxis(
                                ap=idx_buf[:, s, t:t + 1], axis=0)).then_inc(gathered[s].sem, 16)

            @block.vector
            def _(dve):
                with dve.Fori(0, NPASS) as i:
                    for s in range(2):
                        dve.wait_ge(sums_ready[s].sem, sums_ready[s].at(4 * i))
                        dve.sem_inc(pause.sem, 1)
                        nc.vector.tensor_copy(idx_buf[:, s, :], src_T[:, halves(i, s)]).then_inc(idx_ready[s].sem, 1)
                        nc.vector.tensor_copy(rank_buf[:, s, :], rank_T[:, halves(i, s)]).then_inc(dve_chain.sem, 1)
                        dve.wait_ge(dve_chain.sem, dve_chain.at(2 * i + s + 1))
                        for t in range(HB):
                            ins = nc.vector.tensor_scalar(onehot[:, s, t, :], iota_run[:, :], rank_buf[:, s, t:t + 1],
                                                          None, ALU.is_equal)
                        ins.then_inc(onehot_ready[s].sem, 1)

            @block.tensor
            def _(pe):
                with pe.Fori(0, NPASS) as i:
                    for s in range(2):
                        pe.wait_ge(onehot_ready[s].sem, onehot_ready[s].at(i + 1))
                        pe.wait_ge(gathered[s].sem, gathered[s].at(16 * HB * (i + 1)))
                        pe.wait_ge(evacuated[s].sem, evacuated[s].at(4 * i))
                        for t in range(HB):
                            b = bank(4 * s + t // 4)
                            ins = nc.tensor.matmul(b[:, (t % 4) * F:(t % 4 + 1) * F], onehot[:, s, t, :], got[:, s, t, :],
                                                   start=True, stop=True)
                            if t % 4 == 3:
                                ins.then_inc(sums_ready[s].sem, 1)

            @block.scalar
            def _(act):
                with act.Fori(0, NPASS) as i:
                    for s in range(2):
                        act.wait_ge(stored[s].sem, stored[s].at(16 * i))
                        for q in range(4):
                            act.wait_ge(sums_ready[s].sem, sums_ready[s].at(4 * i + q + 1))
                            nc.scalar.activation(sums[:, s, 4 * q:4 * q + 4, :].rearrange("p t f -> p (t f)"),
                                                 bank(4 * s + q), ACT.Copy).then_inc(evacuated[s].sem, 1)

            @block.sync
            def _(sp):
                with sp.Fori(0, NPASS) as i:
                    for s in range(2):
                        sp.wait_ge(evacuated[s].sem, evacuated[s].at(4 * (i + 1)))
                        sp.dma_start(run_view[:, halves(i, s), :], sums[:, s, :, :]).then_inc(stored[s].sem, 16)
                for s in range(2):
                    sp.wait_ge(stored[s].sem, stored[s].at(16 * NPASS))
        for s in range(2):
            idx_ready[s].close(NPASS)
            onehot_ready[s].close(NPASS)
            gathered[s].close(16 * HB * NPASS)
            sums_ready[s].close(4 * NPASS)
            evacuated[s].close(4 * NPASS)
            stored[s].close(16 * NPASS)
        dve_chain.close(2 * NPASS)
        buf.close()

    def scatter_pass():
        buf = ExitStack()
        rows_in = sb("rows_in", [TE, 2, HB, AW], at=buf)
        src_bc = sb("src_bc", [TE, 2, HB, TE], I32, at=buf)
        onehot = sb("s_onehot", [TE, 2, HB, TE], BF16, at=buf)
        same = sb("same", [TE, 2, HB, TE], BF16, at=buf)
        earlier = sb("earlier", [TE, 2, HB, TE], BF16, at=buf)
        tri = sb("tri", [TE, TE], BF16, at=buf)
        ones_b = sb("ones_b", [TE, 1], BF16, at=buf)
        counts = sb("counts", [TE, 2, 4, TE], at=buf)
        to_add = sb("to_add", [TE, 2, HB, AW], at=buf)
        src_f = sb("src_f", [TE, HB], at=buf)
        spare = sb("spare", [TE, HB], at=buf)
        spare_base = sb("spare_base", [TE, 1], at=buf)
        with nc.Block() as block:
            @block.gpsimd
            def _(pool):
                ch = Chain(pool, pool_chain)
                nc.gpsimd.iota(spare_base[:, :], pattern=[[0, 1]], base=N, channel_multiplier=1,
                               allow_small_or_imprecise_dtypes=True)
                ch.link(nc.gpsimd.memset(tri[:, :], 1.0))
                nc.gpsimd.affine_select(out=tri[:, :], in_=tri[:, :], compare_op=ALU.is_gt, fill=0.0, base=0,
                                        pattern=[[1, TE]], channel_multiplier=-1)
                nc.gpsimd.memset(ones_b[:, :], 1.0)
                nc.gpsimd.memset(rows_in[:, :, :, F:AW], 1.0)
                pool_chain.close(ch.n)

        def tile_loads(eng, odd, i, s):
            for t in range(odd, HB, 2):
                at = eng.value_load(tile_place[0:1, bass.ds((2 * i + s) * HB + t, 1)], min_val=0, max_val=N)
                eng.dma_start(rows_in[:, s, t, 0:F], by_run[bass.ds(at, TE), :]).then_inc(window_in[s].sem, 16)

        def source_load(eng, i, s):
            eng.dma_start(src_bc[:, s, :, :].rearrange("p t e -> p (t e)"),
                          src_rows[0, bass.ds((2 * i + s) * HB * TE, HB * TE)].partition_broadcast(TE)
                          ).then_inc(loaded[s].sem, 16)

        with nc.Block() as block:
            @block.sync
            def _(sp):
                with sp.Fori(0, NPASS) as i:
                    for s in range(2):
                        sp.wait_ge(sums_ready[s].sem, sums_ready[s].at(HB * i))
                        sp.sem_inc(pause.sem, 1)
                        source_load(sp, i, s)
                        tile_loads(sp, 0, i, s)

            @block.vector
            def _(dve):
                PER = 6
                with dve.Fori(0, NPASS) as i:
                    for s in range(2):
                        n = 2 * i + s
                        ch = Chain(dve, dve_chain, PER, n)
                        dve.wait_ge(sums_ready[s].sem, sums_ready[s].at(HB * i))
                        dve.sem_inc(pause.sem, 1)
                        nc.vector.tensor_copy(src_f[:, :], src_T[:, halves(i, s)]).then_inc(dve_chain.sem, 1)
                        nc.vector.tensor_copy(rank_buf[:, s, :], rank_T[:, halves(i, s)]).then_inc(dve_chain.sem, 1)
                        ch.n += 2
                        dve.wait_ge(dve_chain.sem, dve_chain.at(PER * n + 2))
                        for t in range(HB):
                            nc.vector.tensor_scalar(onehot[:, s, t, :], iota_run[:, :], rank_buf[:, s, t:t + 1], None,
                                                    ALU.is_equal)
                        dve.wait_ge(loaded[s].sem, loaded[s].at(16 * (i + 1)))
                        for t in range(HB):
                            ins = nc.vector.tensor_scalar(same[:, s, t, :], src_bc[:, s, t, :], src_f[:, t:t + 1], None,
                                                          ALU.is_equal)
                        ch.link(ins)
                        nc.vector.tensor_tensor(earlier[:, s, :, :], same[:, s, :, :],
                                                tri[:, :].unsqueeze(1).to_broadcast([TE, HB, TE]), ALU.mult
                                                ).then_inc(onehot_ready[s].sem, 1)
                        ch.link(nc.vector.tensor_scalar(spare[:, :], src_f[:, :], -1.0, spare_base[:, :], ALU.mult, ALU.add))
                        dve.wait_ge(scatter_idx.sem, scatter_idx.at(n + 1))
                        ch.link(nc.vector.scalar_tensor_tensor(spare[:, :], bank(7)[:, 0:HB], 0.5, spare[:, :], ALU.is_gt, ALU.mult))
                        ch.link(nc.vector.tensor_tensor(spare[:, :], spare[:, :], src_f[:, :], ALU.add))
                        for k in range(NACCS):
                            dve.wait_ge(scattered[k].sem, scattered[k].at(16 * (HB // NACCS) * (n - 1)))
                        nc.vector.tensor_copy(idx_buf[:, s, :], spare[:, :]).then_inc(idx_ready[s].sem, 1)
                        dve.wait_ge(idx_ready[s].sem, idx_ready[s].at(i + 1))
                        assert ch.n == PER
                dve_chain.close(PER * 2 * NPASS)

            @block.tensor
            def _(pe):
                with pe.Fori(0, NPASS) as i:
                    for s in range(2):
                        n = 2 * i + s
                        pe.wait_ge(onehot_ready[s].sem, onehot_ready[s].at(i + 1))
                        pe.wait_ge(idx_ready[1 - s].sem, idx_ready[1 - s].at(i + s))
                        for t in range(HB):
                            ins = nc.tensor.matmul(bank(7)[:, t:t + 1], earlier[:, s, t, :], ones_b[:, :], start=True, stop=True)
                        ins.then_inc(scatter_idx.sem, 1)
                        pe.wait_ge(window_in[s].sem, window_in[s].at(16 * HB * (i + 1)))

                        def count_edges(q):
                            pe.wait_ge(counts_out.sem, counts_out.at(n * 4 + q) if q else counts_out.at(n * 4))
                            for t in range(4 * q, 4 * q + 4):
                                ins = nc.tensor.matmul(bank(q % 2)[:, (t % 4) * TE:(t % 4 + 1) * TE], onehot[:, s, t, :],
                                                       same[:, s, t, :], start=True, stop=True)
                            ins.then_inc(counts_ready.sem, 1)

                        count_edges(0)
                        for q in range(4):
                            pe.wait_ge(counts_out.sem, counts_out.at(n * 4 + q + 1))
                            if q < 3:
                                count_edges(q + 1)
                            for t in range(4 * q, 4 * q + 4):
                                if t == 0:
                                    pe.wait_ge(evacuated[0].sem, evacuated[0].at(n * 2 * (HB // 4)))
                                if t == 8:
                                    pe.wait_ge(evacuated[0].sem, evacuated[0].at(n * 2 * (HB // 4) + 4))
                                b = bank(2 + (t // 2) % 4)
                                ins = nc.tensor.matmul(b[:, (t % 2) * AW:(t % 2 + 1) * AW], counts[:, q % 2, t % 4, :],
                                                       rows_in[:, s, t, :], start=True, stop=True)
                                ins.then_inc(sums_ready[s].sem, 1)

            @block.scalar
            def _(act):
                for s in range(2):
                    tile_loads(act, 1, 0, s)
                with act.Fori(0, NPASS) as i:
                    for s in range(2):
                        n = 2 * i + s

                        def counts_copy(q):
                            act.wait_ge(counts_ready.sem, counts_ready.at(4 * n + q + 1))
                            nc.scalar.activation(counts[:, q % 2, :, :].rearrange("p t e -> p (t e)"), bank(q % 2),
                                                 ACT.Copy).then_inc(counts_out.sem, 1)

                        for k in range(NACCS):
                            act.wait_ge(scattered[k].sem, scattered[k].at(16 * (HB // NACCS) * (n - 1)))
                        counts_copy(0)
                        for q in range(4):
                            if q < 3:
                                if q >= 1:
                                    act.wait_ge(sums_ready[s].sem, sums_ready[s].at(HB * i + 4 * q))
                                counts_copy(q + 1)
                            for h in range(2):
                                t = 4 * q + 2 * h
                                act.wait_ge(sums_ready[s].sem, sums_ready[s].at(HB * i + t + 2))
                                nc.scalar.activation(to_add[:, s, t:t + 2, :].rearrange("p t f -> p (t f)"),
                                                     bank(2 + (t // 2) % 4)[:, 0:2 * AW], ACT.Copy
                                                     ).then_inc(evacuated[0].sem, 1)
                        tile_loads(act, 1, i + 1, s)
                for s in range(2):
                    act.wait_ge(window_in[s].sem, window_in[s].at(16 * HB * NPASS + 16 * (HB // 2)))

            @block.gpsimd
            def _(pool):
                with pool.Fori(0, NPASS) as i:
                    for s in range(2):
                        pool.wait_ge(idx_ready[s].sem, idx_ready[s].at(i + 1))
                        for t in range(HB):
                            k = t % NACCS
                            if t % 2 == 0:
                                pool.wait_ge(evacuated[0].sem, evacuated[0].at((2 * i + s) * 8 + t // 2 + 1))
                            pool.wait_ge(scattered[k].sem, scattered[k].at(16 * ((2 * i + s) * (HB // NACCS) + t // NACCS)))
                            pool.sem_inc(pause.sem, 1)
                            nc.gpsimd.indirect_dma_start(acc[k], bass.IndirectOffsetOnAxis(ap=idx_buf[:, s, t:t + 1], axis=0),
                                                         to_add[:, s, t, :], None, compute_op=ALU.add
                                                         ).then_inc(scattered[k].sem, 16)
                for k in range(NACCS):
                    pool.wait_ge(scattered[k].sem, scattered[k].at(16 * (HB // NACCS) * 2 * NPASS))
        for k in scattered:
            k.close(16 * (HB // NACCS) * 2 * NPASS)
        for s in range(2):
            sums_ready[s].close(HB * NPASS)
            loaded[s].close(16 * NPASS)
            window_in[s].close(16 * HB * NPASS + 16 * (HB // 2))
            onehot_ready[s].close(NPASS)
            idx_ready[s].close(NPASS)
        scatter_idx.close(2 * NPASS)
        counts_ready.close(8 * NPASS)
        counts_out.close(8 * NPASS)
        evacuated[0].close(8 * 2 * NPASS)
        buf.close()

    def border_pass(name):
        buf = ExitStack()
        lasts = sb(name + "_lasts", [BP, BC, F], at=buf)
        firsts = sb(name + "_firsts", [BP, BC, F], at=buf)
        last_T = sb(name + "_last_T", [F, NT + 1], at=buf)
        inflow = sb(name + "_inflow", [F, NT], at=buf)
        carried = sb(name + "_carried", [F, NT], at=buf)
        first_rows = runs[0:NT, :].rearrange("(c p) f -> p c f", p=BP)
        pT = ps[:, 0:4 * 512]
        with nc.Block() as block:
            @block.gpsimd
            def _(pool):
                for k in range(BC):
                    nc.gpsimd.indirect_dma_start(lasts[:, k, :], None, runs, bass.IndirectOffsetOnAxis(
                        ap=last_row[:, k:k + 1], axis=0)).then_inc(gathered[0].sem, 16)

            @block.sync
            def _(sp):
                sp.dma_start(firsts[:, :, :], first_rows).then_inc(loaded[0].sem, 16)
                sp.wait_ge(c["residual"].sem, c["residual"].at(1))
                sp.dma_start(first_rows, firsts[:, :, :]).then_inc(stored[0].sem, 16)
                sp.wait_ge(stored[0].sem, stored[0].at(16))

            @block.tensor
            def _(pe):
                pe.wait_ge(gathered[0].sem, gathered[0].at(16 * BC))
                for k in range(BC):
                    ins = nc.tensor.transpose(bank(k // 4)[:, (k % 4) * BP:(k % 4 + 1) * BP], lasts[:, k, :], ident[0:BP, 0:BP])
                ins.then_inc(c["x_turned"].sem, 1)
                pe.wait_ge(c["normed"].sem, c["normed"].at(1))
                for k in range(BC):
                    ins = nc.tensor.transpose(bank(4 + k // 4)[0:BP, (k % 4) * F:(k % 4 + 1) * F],
                                              carried[:, k * BP:(k + 1) * BP], ident[:, :])
                ins.then_inc(c["normed_turned"].sem, 1)

            @block.vector
            def _(dve):
                ch = Chain(dve, dve_chain)
                nc.vector.memset(last_T[:, 0:1], 0.0)
                dve.wait_ge(c["x_turned"].sem, c["x_turned"].at(1))
                for k in range(4):
                    wide = min(4 * BP, NT - k * 4 * BP)
                    ins = nc.vector.tensor_copy(last_T[:, 1 + k * 4 * BP:1 + k * 4 * BP + wide], bank(k)[:, 0:wide])
                ch.link(ins)
                ch.link(nc.vector.tensor_tensor(inflow[:, :], last_T[:, 0:NT], carries[:, :], ALU.mult))
                nc.vector.tensor_tensor_scan(carried[:, :], through[:, :], inflow[:, :], 0.0, ALU.mult, ALU.add
                                             ).then_inc(c["normed"].sem, 1)
                dve.wait_ge(c["normed_turned"].sem, c["normed_turned"].at(1))
                dve.wait_ge(loaded[0].sem, loaded[0].at(16))
                whole = firsts[:, :, :].rearrange("p c f -> p (c f)")
                nc.vector.tensor_tensor(whole, whole, ps[0:BP, 4 * 512:4 * 512 + BC * F], ALU.add
                                        ).then_inc(c["residual"].sem, 1)
                dve_chain.close(ch.n)
        gathered[0].close(16 * BC)
        loaded[0].close(16)
        stored[0].close(16)
        for k in ("residual", "x_turned", "normed", "normed_turned"):
            c[k].close(1)
        buf.close()

    GT, GROUPS = 4, NT // 4
    UT = 8

    def wait(eng, semaphore, n):
        if not isinstance(n, int) or n > 0:
            eng.wait_ge(semaphore.sem, semaphore.at(n))

    def message_pass(tab_in):
        buf = ExitStack()
        prep = ExitStack()
        time_parts = nc.dram_tensor("time_parts", [3, NCH * TE * TE], BF16, kind="Internal").ap()
        wt_parts = nc.dram_tensor("wt_parts", [3, F], BF16, kind="Internal").ap()
        wt9 = sb("wt9", [9, F], BF16, at=buf)
        time_f = sb("time_f", [128, NCH, TE], at=prep)
        time_b = sb("time_b", [128, 3, NCH, TE], BF16, at=prep)
        wt_f = sb("wt_f", [1, F], at=prep)
        wt_b = sb("wt_b", [1, 3, F], BF16, at=prep)
        with nc.Block() as block:
            @block.vector
            def _(dve):
                nc.vector.memset(time_f[:, CHT:NCH, :], 0.0)
        with nc.Block() as block:
            @block.sync
            def _(sp):
                v = a["edge_weight"]
                whole, rest = CHT * TE * TE, CHR * TE
                sp.dma_start(time_f[:, 0:CHT, :], v[0:whole].rearrange("(c p e) -> p c e", c=CHT, p=128)).then_inc(loaded[0].sem, 16)
                sp.dma_start(time_f[0:CHR, CHT, :], v[whole:whole + rest].rearrange("(p e) -> p e", e=TE)).then_inc(loaded[0].sem, 16)
                sp.dma_start(time_f[CHR:CHR + 1, CHT, 0:REM], v[FULL * TE:E].rearrange("(p e) -> p e", p=1)).then_inc(loaded[0].sem, 16)
                sp.wait_ge(c["dve_setup"].sem, c["dve_setup"].at(1))
                sp.dma_start(time_parts.rearrange("k (c p e) -> p k c e", p=128, e=TE)[:, 0, :, :], time_b[:, 0, :, :]).then_inc(stored[0].sem, 16)
                sp.dma_start(time_parts.rearrange("k (c p e) -> p k c e", p=128, e=TE)[:, 1, :, :], time_b[:, 1, :, :]).then_inc(stored[0].sem, 16)
                sp.dma_start(time_parts.rearrange("k (c p e) -> p k c e", p=128, e=TE)[:, 2, :, :], time_b[:, 2, :, :]).then_inc(stored[0].sem, 16)
                sp.dma_start(wt_parts.rearrange("k f -> (k f)").unsqueeze(0), wt_b[:, :, :].rearrange("p k f -> p (k f)")).then_inc(stored[0].sem, 16)
                sp.wait_ge(stored[0].sem, stored[0].at(64))
                for k in range(3):
                    sp.dma_start(wt9[3 * k:3 * k + 3, :], wt_parts).then_inc(loaded[1].sem, 16)
                sp.wait_ge(loaded[1].sem, loaded[1].at(48))

            @block.vector
            def _(dve):
                ch = Chain(dve, dve_chain)
                dve.wait_ge(loaded[0].sem, loaded[0].at(48))
                ch.link(nc.vector.tensor_copy(wt_f[:, :], m["Wt"][:, :]))
                for full, part in ((time_f[:, :, :], lambda k: time_b[:, k, :, :]), (wt_f[:, :], lambda k: wt_b[:, k, :])):
                    for k in range(3):
                        ch.link(nc.vector.tensor_copy(part(k), full))
                        if k < 2:
                            ch.link(nc.vector.tensor_tensor(full, full, part(k), ALU.subtract))
                nc.vector.memset(wt_f[:, :], 0.0).then_inc(c["dve_setup"].sem, 1)
                dve_chain.close(ch.n)
        loaded[0].close(48)
        loaded[1].close(48)
        stored[0].close(64)
        c["dve_setup"].close(1)
        prep.close()

        got = sb("m_got", [TE, 4, UT, F], at=buf)
        onehot = sb("m_onehot", [TE, 8, GT, TE], at=buf)
        sums = sb("m_sums", [TE, 8, GT, F], at=buf)
        ea = sb("ea", [TE, 2, HB, EC], at=buf)
        times = sb("times", [9, 2, HB * TE], BF16, at=buf)
        ea_T = sb("ea_T", [EC, 2, GT * TE], at=buf)
        gate = sb("gate", [F, 4, GT * TE], at=buf)
        hid = sb("hid", [F, 2, GT * TE], at=buf)
        ef = sb("ef", [F, 2, GT * TE], at=buf)
        idx4 = sb("idx4", [TE, 4, UT], I32, at=buf)
        rank4 = sb("rank4", [TE, 4, UT], at=buf)
        attr = a["edge_attr_64"]
        LAST = NPASS - 1

        def group(i, u, back):
            return 8 * i + u - back, (u - back) % 8

        def drive(eng, step):
            for u in range(8):
                step(0, u)
            with eng.Fori(1, LAST) as i:
                for u in range(8):
                    step(i, u)
            for u in range(8):
                step(LAST, u)
            for u in range(4):
                step(NPASS, u)

        def there(i, u, back):
            g = 8 * i + u - back
            return not isinstance(g, int) or 0 <= g < GROUPS

        with nc.Block() as block:
            @block.gpsimd
            def _(pool):
                with pool.Fori(0, NPASS) as i:
                    for v in range(4):
                        pool.wait_ge(idx_ready[v].sem, idx_ready[v].at(i + 1))
                        pool.sem_inc(pause.sem, 1)
                        for t in range(UT):
                            nc.gpsimd.indirect_dma_start(got[:, v, t, :], None, tab_in, bass.IndirectOffsetOnAxis(
                                ap=idx4[:, v, t:t + 1], axis=0)).then_inc(gathered[v].sem, 16)

            @block.tensor
            def _(pe):
                def step(i, u):
                    if there(i, u, 4):
                        g, r = group(i, u, 4)
                        wait(pe, onehot_ready[0], g + 1)
                        wait(pe, c["msg_out"], g + 1)
                        wait(pe, evacuated[0], g - 1)
                        for t in range(GT):
                            ins = nc.tensor.matmul(bank(5 + r % 2)[:, t * F:(t + 1) * F], onehot[:, r, t, :],
                                                   got[:, r // 2, (r % 2) * GT + t, :], start=True, stop=True)
                        ins.then_inc(sums_ready[0].sem, 1)
                    if there(i, u, 3):
                        g, r = group(i, u, 3)
                        wait(pe, c["ef_out"], g + 1)
                        wait(pe, c["z_out"], g - 1)
                        for t in range(GT):
                            ins = nc.tensor.matmul(bank((4, 7)[r % 2])[:, t * F:(t + 1) * F], ef[:, r % 2, t * TE:(t + 1) * TE],
                                                   m["Wn1"][:, 1, :], start=True, stop=True)
                        ins.then_inc(c["z_ready"].sem, 1)
                    if there(i, u, 2):
                        g, r = group(i, u, 2)
                        wait(pe, c["hid_out"], g + 1)
                        wait(pe, c["ef_out"], g)
                        nc.tensor.matmul(bank(3), m["We2"][:, :], hid[:, r % 2, :], start=True, stop=True
                                         ).then_inc(c["ef_ready"].sem, 1)
                    if there(i, u, 1):
                        g, r = group(i, u, 1)
                        wait(pe, c["ea_out"], g + 1)
                        wait(pe, c["hid_out"], g)
                        nc.tensor.matmul(bank(2), m["We1"][:, :], ea_T[:, r % 2, :], start=True, stop=True
                                         ).then_inc(c["hid_ready"].sem, 1)
                    if there(i, u, 0):
                        g, r = group(i, u, 0)
                        s = r // 4
                        if r % 4 == 0:
                            pe.wait_ge(loaded[s].sem, loaded[s].at(32 * (i + 1)))
                            if isinstance(i, int) and i == LAST and s == 1:
                                pe.wait_ge(setup_dma.sem, setup_dma.at(16))
                        wait(pe, c["ea_out"], g)
                        pe.sem_inc(pause.sem, 1)
                        for t in range(GT):
                            ins = nc.tensor.transpose(bank(0)[0:EC, t * TE:(t + 1) * TE], ea[:, s, (r % 4) * GT + t, :], ident[:, :])
                        ins.then_inc(c["ea_turned"].sem, 1)
                        wait(pe, c["gate_out"], g)
                        nc.tensor.matmul(bank(1), wt9[:, :], times[:, s, (r % 4) * GT * TE:(r % 4 + 1) * GT * TE],
                                         start=True, stop=True).then_inc(c["gate_ready"].sem, 1)
                drive(pe, step)

            @block.scalar
            def _(act):
                def step(i, u):
                    if there(i, u, 4):
                        g, r = group(i, u, 4)
                        if r % 4 == 0:
                            s = r // 4
                            act.wait_ge(stored[s].sem, stored[s].at(16 * ((i if u >= 4 else i - 1))))
                        wait(act, sums_ready[0], g + 1)
                        nc.scalar.activation(sums[:, r, :, :].rearrange("p t f -> p (t f)"), bank(5 + r % 2), ACT.Copy
                                             ).then_inc(evacuated[0].sem, 1)
                    if there(i, u, 3):
                        g, r = group(i, u, 3)
                        wait(act, c["z_out"], g + 1)
                        rows_ = got[:, r // 2, (r % 2) * GT:(r % 2 + 1) * GT, :].rearrange("p t f -> p (t f)")
                        nc.scalar.activation(rows_, rows_, ACT.Relu).then_inc(c["msg_out"].sem, 1)
                    if there(i, u, 1):
                        g, r = group(i, u, 1)
                        wait(act, c["hid_ready"], g + 1)
                        wait(act, c["ef_ready"], g - 1)
                        nc.scalar.activation(hid[:, r % 2, :], bank(2), ACT.Relu, bias=m["be1"][:, 0:1]
                                             ).then_inc(c["hid_out"].sem, 1)
                    if there(i, u, 0):
                        g, r = group(i, u, 0)
                        wait(act, c["gate_ready"], g + 1)
                        wait(act, c["ef_out"], g - 3)
                        nc.scalar.activation(gate[:, r % 4, :], bank(1), ACT.Sigmoid, bias=m["bt"][:, 0:1]
                                             ).then_inc(c["gate_out"].sem, 1)
                drive(act, step)

            @block.vector
            def _(dve):
                def numbers(i, v, unit):
                    wait(dve, sums_ready[0], 2 * unit - 6)
                    dve.sem_inc(pause.sem, 1)
                    nc.vector.tensor_copy(idx4[:, v, :], src_T[:, bass.ds(unit * UT, UT)]).then_inc(idx_ready[v].sem, 1)

                def step(i, u):
                    if u % 2 == 0 and there(i, u, 0):
                        unit = 4 * i + u // 2
                        if not (isinstance(unit, int) and unit + 1 >= 4 * NPASS):
                            numbers(i, (u // 2 + 1) % 4, unit + 1)
                    if u % 2 == 0 and there(i, u, 2):
                        unit = 4 * i + (u - 2) // 2
                        wait(dve, onehot_ready[0], 2 * unit - 6)
                        dve.sem_inc(pause.sem, 1)
                        nc.vector.tensor_copy(rank4[:, (u // 2 - 1) % 4, :], rank_T[:, bass.ds(unit * UT, UT)]
                                              ).then_inc(dve_chain.sem, 1)
                        dve.wait_ge(dve_chain.sem, dve_chain.at(unit + 1))
                    if there(i, u, 3):
                        g, r = group(i, u, 3)
                        if r % 2 == 0:
                            dve.wait_ge(gathered[r // 2].sem, gathered[r // 2].at(16 * UT * ((i + 1) if u >= 3 else i)))
                        wait(dve, c["z_ready"], g + 1)
                        rows_ = got[:, r // 2, (r % 2) * GT:(r % 2 + 1) * GT, :].rearrange("p t f -> p (t f)")
                        nc.vector.tensor_tensor(rows_, rows_, bank((4, 7)[r % 2]), ALU.add).then_inc(c["z_out"].sem, 1)
                    if there(i, u, 2):
                        g, r = group(i, u, 2)
                        wait(dve, c["ef_ready"], g + 1)
                        wait(dve, c["gate_out"], g + 1)
                        wait(dve, c["z_ready"], g - 1)
                        nc.vector.scalar_tensor_tensor(ef[:, r % 2, :], bank(3), m["be2"][:, 0:1], gate[:, r % 4, :],
                                                       ALU.add, ALU.mult).then_inc(c["ef_out"].sem, 1)
                        wait(dve, sums_ready[0], g - 7)
                        for t in range(GT):
                            ins = nc.vector.tensor_scalar(onehot[:, r, t, :], iota_run[:, :],
                                                          rank4[:, r // 2, (r % 2) * GT + t:(r % 2) * GT + t + 1], None, ALU.is_equal)
                        ins.then_inc(onehot_ready[0].sem, 1)
                    if there(i, u, 0):
                        g, r = group(i, u, 0)
                        wait(dve, c["ea_turned"], g + 1)
                        wait(dve, c["hid_ready"], g - 1)
                        nc.vector.tensor_copy(ea_T[:, r % 2, :], bank(0)[0:EC, :]).then_inc(c["ea_out"].sem, 1)
                numbers(0, 0, 0)
                drive(dve, step)

            @block.sync
            def _(sp):
                def load(i, s):
                    h = 2 * i + s
                    wait(sp, c["gate_ready"], 4 * h - 4)
                    if isinstance(h, int) and h == 2 * NPASS - 1:
                        whole = FULL - h * HB
                        sp.dma_start(ea[:, s, 0:whole, :], attr[h * HB * TE:FULL * TE, :].rearrange("(t p) c -> p t c", p=TE)
                                     ).then_inc(loaded[s].sem, 16)
                        sp.dma_start(ea[0:REM, s, whole, :], attr[FULL * TE:E, :]).then_inc(setup_dma.sem, 16)
                    else:
                        sp.dma_start(ea[:, s, :, :], attr[bass.ds(h * HB * TE, HB * TE), :].rearrange("(t p) c -> p t c", p=TE)
                                     ).then_inc(loaded[s].sem, 16)
                    sp.dma_start(times[:, s, :], time_parts[:, bass.ds(h * HB * TE, HB * TE)].unsqueeze(1).to_broadcast([3, 3, HB * TE])
                                 ).then_inc(loaded[s].sem, 16)

                def store(i, s):
                    h = 2 * i + s
                    sp.wait_ge(evacuated[0].sem, evacuated[0].at(4 * (h + 1)))
                    sp.dma_start(run_view[:, bass.ds(h * HB, HB), :], sums[:, 4 * s:4 * s + 4, :, :].rearrange("p g t f -> p (g t) f")
                                 ).then_inc(stored[s].sem, 16)

                load(0, 0)
                load(0, 1)
                load(1, 0)
                load(1, 1)
                store(0, 0)
                with sp.Fori(1, LAST - 1) as i:
                    load(i + 1, 0)
                    store(i - 1, 1)
                    load(i + 1, 1)
                    store(i, 0)
                load(LAST, 0)
                store(LAST - 2, 1)
                load(LAST, 1)
                for h in range(2 * LAST - 2, 2 * NPASS):
                    store(h // 2, h % 2)
                for s in range(2):
                    sp.wait_ge(stored[s].sem, stored[s].at(16 * NPASS))
        for k in ("ea_turned", "ea_out", "gate_ready", "gate_out", "hid_ready", "hid_out", "ef_ready", "ef_out", "z_ready",
                  "z_out", "msg_out"):
            c[k].close(GROUPS)
        for k in (onehot_ready[0], sums_ready[0], evacuated[0]):
            k.close(GROUPS)
        for v in range(4):
            gathered[v].close(16 * UT * NPASS)
            idx_ready[v].close(NPASS)
        loaded[0].close(32 * NPASS)
        loaded[1].close(32 * NPASS)
        setup_dma.close(16)
        dve_chain.close(4 * NPASS)
        for s in range(2):
            stored[s].close(16 * NPASS)
        buf.close()

    att = ExitStack()

    def attention_setup():
        kd_T = sb("kd_T", [TE, H, NT], at=att)
        kind_T = sb("kind_T", [TE, KINDS, NT], at=att)
        buf = ExitStack()
        blank = sb("a_blank", [128, NCH * TE * H], at=buf)
        natural = sb("natural", [128, NCH, TE, H], at=buf)
        held_kd = sb("held_kd", [128, 2, H, TE], at=buf)
        kinds = sb("kinds", [128, 2, TE], at=buf)
        keep = sb("keep", [128, NCH, SW], at=buf)
        first_kd = sb("first_kd", [128, NCH, H], at=buf)
        key_in = sb("key_in", [128, NCH], at=buf)
        first_i = sb("first_i", [128, NCH], I32, at=buf)
        spot = sb("spot", [NP, NW], at=buf)
        spot_i = sb("spot_i", [NP, NW], I32, at=buf)
        spare = sb("a_spare", [NP, NW], at=buf)
        some = sb("some", [NP, NW], at=buf)
        tab_kd = sb("tab_kd", [NP, WB, H], at=buf)
        type_i = sb("type_i", [128, NCH, TE], I32, at=buf)
        type_f = sb("type_f", [128, NCH, TE], at=buf)
        with nc.Block() as block:
            @block.gpsimd
            def _(pool):
                nc.gpsimd.memset(blank[:, :], 0.0).then_inc(c["pool_setup"].sem, 1)
                nc.gpsimd.iota(spare[:, :], pattern=[[1, NW]], base=NCH * TE * TE, channel_multiplier=NW,
                               allow_small_or_imprecise_dtypes=True).then_inc(c["pool_setup"].sem, 1)

            @block.vector
            def _(dve):
                nc.vector.memset(type_i[:, CHT:NCH, :], 0).then_inc(c["dve_setup"].sem, 1)
                ch = Chain(dve, dve_chain)
                dve.wait_ge(c["pool_setup"].sem, c["pool_setup"].at(2))
                ch.link(nc.vector.tensor_scalar(some[:, :], degree[:, :], 0.5, None, ALU.is_gt))
                ch.link(nc.vector.tensor_tensor(spot[:, :], first_edge[:, :], spare[:, :], ALU.subtract))
                ch.link(nc.vector.tensor_tensor(spot[:, :], spot[:, :], some[:, :], ALU.mult))
                ch.link(nc.vector.tensor_tensor(spot[:, :], spot[:, :], spare[:, :], ALU.add))
                nc.vector.tensor_copy(spot_i[:, :], spot[:, :])
                dve.wait_ge(loaded[0].sem, loaded[0].at(16))
                ch.link(nc.vector.tensor_scalar(key_in[:, :], key_in[:, :], float(N - 1), None, ALU.min))
                nc.vector.tensor_copy(first_i[:, :], key_in[:, :])
                dve_chain.close(ch.n)

            @block.sync
            def _(sp):
                sp.dma_start(key_in[:, :].unsqueeze(2), keys.rearrange("(c p) k -> p c k", p=128)[:, :, 0:1],
                             allow_slow_non_contiguous=True).then_inc(loaded[0].sem, 16)
                sp.dma_start(keep[:, :, :], starts_d.rearrange("(c p) k -> p c k", p=128)).then_inc(setup_dma.sem, 16)
                sp.dma_start(nodes(kd_rows), kd_node[:, :, :]).then_inc(setup_dma.sem, 16)
                sp.wait_ge(c["pool_setup"].sem, c["pool_setup"].at(1))
                sp.dma_start(kd_edge[0:NCH * TE * TE, :].rearrange("(p e) h -> p (e h)", p=128), blank[:, :]).then_inc(setup_dma.sem, 16)
                sp.wait_ge(c["dve_setup"].sem, c["dve_setup"].at(1))
                v = a["edge_type_3"]
                whole, rest = CHT * TE * TE, CHR * TE
                sp.dma_start(type_i[:, 0:CHT, :], v[0:whole].rearrange("(c p e) -> p c e", c=CHT, p=128)).then_inc(setup_dma.sem, 16)
                sp.dma_start(type_i[0:CHR, CHT, :], v[whole:whole + rest].rearrange("(p e) -> p e", e=TE)).then_inc(setup_dma.sem, 16)
                sp.dma_start(type_i[CHR:CHR + 1, CHT, 0:REM], v[FULL * TE:E].rearrange("(p e) -> p e", p=1)).then_inc(setup_dma.sem, 16)
                setup_dma.close(96)
                sp.wait_ge(setup_dma.sem, setup_dma.at(0))
        c["pool_setup"].close(2)
        c["dve_setup"].close(1)
        loaded[0].close(16)

        with nc.Block() as block:
            @block.gpsimd
            def _(pool):
                for k in range(NCH):
                    nc.gpsimd.indirect_dma_start(first_kd[:, k, :], None, kd_rows, bass.IndirectOffsetOnAxis(
                        ap=first_i[:, k:k + 1], axis=0)).then_inc(gathered[0].sem, 16)
                pool.wait_ge(gathered[0].sem, gathered[0].at(16 * NCH))
                with pool.Fori(0, NW // WB) as i:
                    pool.wait_ge(idx_ready[0].sem, idx_ready[0].at(i + 1))
                    pool.sem_inc(pause.sem, 1)
                    for j in range(WB):
                        nc.gpsimd.indirect_dma_start(kd_edge, bass.IndirectOffsetOnAxis(ap=row_buf[:, 0, j:j + 1], axis=0),
                                                     tab_kd[:, j, :], None).then_inc(gathered[1].sem, 16)
                pool.wait_ge(gathered[1].sem, gathered[1].at(16 * NW))

            @block.vector
            def _(dve):
                with dve.Fori(0, NW // WB) as i:
                    dve.wait_ge(gathered[1].sem, gathered[1].at(16 * WB * i))
                    dve.sem_inc(pause.sem, 1)
                    nc.vector.tensor_copy(tab_kd[:, :, :], kd_node[:, bass.ds(i * WB, WB), :]).then_inc(dve_chain.sem, 1)
                    dve.wait_ge(dve_chain.sem, dve_chain.at(i + 1))
                    dve.sem_inc(pause.sem, 1)
                    nc.vector.tensor_copy(row_buf[:, 0, :], spot_i[:, bass.ds(i * WB, WB)]).then_inc(idx_ready[0].sem, 1)
                dve_chain.close(NW // WB)
                ch = Chain(dve, dve_chain)
                ch.link(nc.vector.tensor_copy(type_f[:, :, :], type_i[:, :, :]))
                nc.vector.tensor_scalar(keep[:, :, :], keep[:, :, :], 1.0 / FAR, 1.0, ALU.mult, ALU.add
                                        ).then_inc(c["dve_setup"].sem, 1)
                dve_chain.close(ch.n)
        gathered[0].close(16 * NCH)
        gathered[1].close(16 * NW)
        idx_ready[0].close(NW // WB)
        c["dve_setup"].close(1)

        with nc.Block() as block:
            @block.sync
            def _(sp):
                sp.dma_start(natural[:, :, :, :], kd_edge[0:NCH * TE * TE, :].rearrange("(c p e) h -> p c e h", p=128, e=TE)
                             ).then_inc(loaded[0].sem, 16)

            @block.vector
            def _(dve):
                ch = Chain(dve, dve_chain)
                dve.wait_ge(loaded[0].sem, loaded[0].at(16))
                ch.link(nc.vector.tensor_copy(natural[:, :, 0, :], first_kd[:, :, :]))
                for k in range(NCH):
                    wide = min(TE, NT - k * TE)
                    s = k % 2
                    wait(dve, c["x_turned"], k - 1)
                    for h in range(H):
                        ins = nc.vector.tensor_tensor_scan(held_kd[:, s, h, :], keep[:, k, 0:TE], natural[:, k, :, h], 0.0,
                                                           ALU.mult, ALU.add)
                    ins.then_inc(c["normed"].sem, 1)
                    dve.wait_ge(c["x_turned"].sem, c["x_turned"].at(k + 1))
                    nc.vector.tensor_copy(kd_T[:, :, k * TE:k * TE + wide],
                                          bank(2 * s).rearrange("p (h t) -> p h t", h=H)[:, :, 0:wide])
                    for j in range(KINDS):
                        ins = nc.vector.tensor_scalar(kind_T[:, j, k * TE:k * TE + wide], bank(2 * s + 1)[:, 0:wide], float(j), None,
                                                      ALU.is_equal)
                    ins.then_inc(c["x_turned_out"].sem, 1)
                dve_chain.close(ch.n)

            @block.tensor
            def _(pe):
                for k in range(NCH):
                    s = k % 2
                    pe.wait_ge(c["normed"].sem, c["normed"].at(k + 1))
                    wait(pe, c["x_turned_out"], k - 1)
                    for h in range(H):
                        nc.tensor.transpose(bank(2 * s)[:, h * TE:(h + 1) * TE], held_kd[:, s, h, :], ident[:, :])
                    nc.tensor.transpose(bank(2 * s + 1)[:, 0:TE], type_f[:, k, :], ident[:, :]).then_inc(c["x_turned"].sem, 1)
        loaded[0].close(16)
        for k in ("x_turned", "x_turned_out", "normed"):
            c[k].close(NCH)
        buf.close()
        return kd_T, kind_T

    def attention_pass(kd_T, kind_T):
        buf = ExitStack()
        HT = H * HB
        got = sb("a_got", [TE, 2, HB, TW], at=buf)
        msg = sb("a_msg", [TE, 2, HB, RW], at=buf)
        onehot = sb("a_onehot", [TE, 2, HB, TE], at=buf)
        sums = sb("a_sums", [TE, 2, HB, RW], at=buf)
        mark = sb("mark", [HT, 2, SW], at=buf)
        picked = sb("picked", [TE, KINDS, H, HB], at=buf)
        embed = sb("embed_score", [TE, H, HB], at=buf)
        score = sb("score", [TE, H, HB], at=buf)
        upward = sb("upward", [HT, TE], at=buf)
        top = sb("top", [HT, TE], at=buf)
        shifted = sb("shifted", [HT, TE], at=buf)
        ex = sb("ex", [HT, TE], at=buf)
        top_start = sb("top_start", [HT, TE], at=buf)
        runs3_view = runs3.rearrange("(r t) f -> r t f", t=NT)
        with nc.Block() as block:
            @block.gpsimd
            def _(pool):
                with pool.Fori(0, NPASS) as i:
                    for s in range(2):
                        pool.wait_ge(idx_ready[s].sem, idx_ready[s].at(i + 1))
                        pool.sem_inc(pause.sem, 1)
                        for t in range(HB):
                            nc.gpsimd.indirect_dma_start(got[:, s, t, :], None, table3, bass.IndirectOffsetOnAxis(
                                ap=idx_buf[:, s, t:t + 1], axis=0)).then_inc(gathered[s].sem, 16)

            @block.vector
            def _(dve):
                PER = 7
                for s in range(2):
                    nc.vector.tensor_copy(idx_buf[:, s, :], src_T[:, s * HB:(s + 1) * HB]).then_inc(idx_ready[s].sem, 1)
                with dve.Fori(0, NPASS) as i:
                    for s in range(2):
                        n = 2 * i + s
                        ch = Chain(dve, dve_chain, PER, n)
                        dve.wait_ge(sums_ready[s].sem, sums_ready[s].at(8 * i))
                        dve.sem_inc(pause.sem, 1)
                        ch.link(nc.vector.tensor_copy(rank_buf[:, s, :], rank_T[:, halves(i, s)]))
                        for t in range(HB):
                            ins = nc.vector.tensor_scalar(onehot[:, s, t, :], iota_run[:, :], rank_buf[:, s, t:t + 1],
                                                          None, ALU.is_equal)
                        ins.then_inc(onehot_ready[s].sem, 1)
                        dve.wait_ge(gathered[s].sem, gathered[s].at(16 * HB * (i + 1)))
                        dve.sem_inc(pause.sem, 1)
                        for k in range(KINDS):
                            ins = nc.vector.tensor_tensor(
                                picked[:, k, :, :], got[:, s, :, F + (1 + k) * H:F + (2 + k) * H].rearrange("p t h -> p h t"),
                                kind_T[:, k, halves(i, s)].unsqueeze(1).to_broadcast([TE, H, HB]), ALU.mult)
                        ch.link(ins)
                        nc.vector.tensor_reduce(embed[:, :, :], picked[:, :, :, :].rearrange("p k h t -> p h t k"), AX.X, ALU.add)
                        ch.link(nc.vector.tensor_tensor(score[:, :, :], got[:, s, :, F:F + H].rearrange("p t h -> p h t"),
                                                        kd_T[:, :, halves(i, s)], ALU.add))
                        ch.link(nc.vector.scalar_tensor_tensor(score[:, :, :], score[:, :, :], SLOPE, score[:, :, :], ALU.mult, ALU.max))
                        nc.vector.tensor_tensor(score[:, :, :], score[:, :, :], embed[:, :, :], ALU.add
                                                ).then_inc(c["ea_out"].sem, 1)
                        dve.wait_ge(c["ea_turned"].sem, c["ea_turned"].at(n + 1))
                        dve.wait_ge(loaded[s].sem, loaded[s].at(16 * H * (i + 1)))
                        turned = bank(0)[0:HT, 0:TE]
                        ch.link(nc.vector.tensor_tensor_scan(upward[:, :], mark[:, s, 0:TE], turned, -FAR, ALU.add, ALU.max))
                        ch.link(nc.vector.tensor_tensor_scan(top[:, ::-1], mark[:, s, TE:0:-1], upward[:, ::-1], -FAR,
                                                             ALU.add, ALU.max))
                        nc.vector.tensor_tensor(shifted[:, :], turned, top[:, :], ALU.subtract).then_inc(c["hid_ready"].sem, 1)
                        ch.link(nc.vector.scalar_tensor_tensor(top_start[:, :], mark[:, s, 0:TE], -1.0 / FAR, top[:, :],
                                                               ALU.mult, ALU.mult))
                        dve.sem_inc(c["hid_out"].sem, 1)
                        dve.wait_ge(c["ef_out"].sem, c["ef_out"].at(n + 1))
                        dve.sem_inc(pause.sem, 1)
                        for t in range(HB):
                            ins = nc.vector.tensor_tensor(
                                msg[:, s, t, 0:F].rearrange("p (h d) -> p h d", h=H), got[:, s, t, 0:F].rearrange("p (h d) -> p h d", h=H),
                                msg[:, s, t, F:F + H].unsqueeze(2).to_broadcast([TE, H, HD]), ALU.mult)
                        ins.then_inc(c["msg_out"].sem, 1)
                        dve.wait_ge(c["msg_out"].sem, c["msg_out"].at(n + 1))
                        dve.sem_inc(pause.sem, 1)
                        nc.vector.tensor_copy(idx_buf[:, s, :], src_T[:, bass.ds((2 * i + s + 2) * HB, HB)]
                                              ).then_inc(idx_ready[s].sem, 1)
                        assert ch.n == PER, ch.n
                dve_chain.close(PER * 2 * NPASS)

            @block.tensor
            def _(pe):
                with pe.Fori(0, NPASS) as i:
                    for s in range(2):
                        n = 2 * i + s
                        pe.wait_ge(c["ea_out"].sem, c["ea_out"].at(n + 1))
                        pe.sem_inc(pause.sem, 1)
                        nc.tensor.transpose(bank(0)[0:HT, 0:TE], score[:, :, :].rearrange("p h t -> p (h t)"), ident[:, :]
                                            ).then_inc(c["ea_turned"].sem, 1)
                        pe.wait_ge(c["hid_out"].sem, c["hid_out"].at(n + 1))
                        pe.wait_ge(c["ef_ready"].sem, c["ef_ready"].at(n + 1))
                        pe.sem_inc(pause.sem, 1)
                        nc.tensor.transpose(bank(1)[:, 0:HT], ex[:, :], ident[0:HT, 0:HT])
                        nc.tensor.transpose(bank(1)[:, HT:2 * HT], top_start[:, :], ident[0:HT, 0:HT]
                                            ).then_inc(c["z_ready"].sem, 1)
                        pe.wait_ge(onehot_ready[s].sem, onehot_ready[s].at(i + 1))
                        pe.wait_ge(c["msg_out"].sem, c["msg_out"].at(n + 1))
                        for q in range(8):
                            if q % 4 == 0:
                                pe.wait_ge(evacuated[0].sem, evacuated[0].at(8 * n + q))
                            for t in range(2 * q, 2 * q + 2):
                                ins = nc.tensor.matmul(bank(4 + q % 4)[:, (t % 2) * RW:(t % 2 + 1) * RW], onehot[:, s, t, :],
                                                       msg[:, s, t, :], start=True, stop=True)
                            ins.then_inc(sums_ready[s].sem, 1)

            @block.scalar
            def _(act):
                with act.Fori(0, NPASS) as i:
                    for s in range(2):
                        n = 2 * i + s
                        act.wait_ge(c["hid_ready"].sem, c["hid_ready"].at(n + 1))
                        nc.scalar.activation(ex[:, :], shifted[:, :], ACT.Exp).then_inc(c["ef_ready"].sem, 1)
                        act.wait_ge(c["z_ready"].sem, c["z_ready"].at(n + 1))
                        nc.scalar.activation(msg[:, s, :, F:RW].rearrange("p t (k h) -> p k h t", k=2),
                                             bank(1)[:, 0:2 * HT].rearrange("p (k h t) -> p k h t", k=2, h=H), ACT.Copy
                                             ).then_inc(c["ef_out"].sem, 1)
                        act.wait_ge(stored[s].sem, stored[s].at(16 * i))
                        for q in range(8):
                            act.wait_ge(sums_ready[s].sem, sums_ready[s].at(8 * i + q + 1))
                            nc.scalar.activation(sums[:, s, 2 * q:2 * q + 2, :].rearrange("p t f -> p (t f)"),
                                                 bank(4 + q % 4)[:, 0:2 * RW], ACT.Copy).then_inc(evacuated[0].sem, 1)

            @block.sync
            def _(sp):
                def load(i, s):
                    for h in range(H):
                        sp.dma_start(mark[h * HB:(h + 1) * HB, s, :], starts_d[halves(i, s), :]).then_inc(loaded[s].sem, 16)

                load(0, 0)
                load(0, 1)
                with sp.Fori(0, NPASS - 1) as i:
                    for s in range(2):
                        sp.wait_ge(c["z_ready"].sem, c["z_ready"].at(2 * i + s + 1))
                        load(i + 1, s)
                        sp.wait_ge(evacuated[0].sem, evacuated[0].at(8 * (2 * i + s + 1)))
                        sp.dma_start(runs3_view[:, halves(i, s), :], sums[:, s, :, :]).then_inc(stored[s].sem, 16)
                for s in range(2):
                    sp.wait_ge(evacuated[0].sem, evacuated[0].at(8 * (2 * NPASS - 1 + s)))
                    sp.dma_start(runs3_view[:, halves(NPASS - 1, s), :], sums[:, s, :, :]).then_inc(stored[s].sem, 16)
                for s in range(2):
                    sp.wait_ge(stored[s].sem, stored[s].at(16 * NPASS))
        for s in range(2):
            idx_ready[s].close(NPASS + 1)
            onehot_ready[s].close(NPASS)
            gathered[s].close(16 * HB * NPASS)
            sums_ready[s].close(8 * NPASS)
            stored[s].close(16 * NPASS)
            loaded[s].close(16 * H * NPASS)
        evacuated[0].close(16 * NPASS)
        for k in ("ea_out", "ea_turned", "hid_ready", "hid_out", "ef_ready", "ef_out", "z_ready", "msg_out"):
            c[k].close(2 * NPASS)
        buf.close()

    def attention_border():
        buf = ExitStack()
        lasts = sb("b_lasts", [BP, BC, RW], at=buf)
        firsts = sb("b_firsts", [BP, BC, RW], at=buf)
        last_T = sb("b_last_T", [F, NT + 1], at=buf)
        den_T = sb("b_den_T", [H, NT + 1], at=buf)
        max_T = sb("b_max_T", [H, NT + 1], at=buf)
        open_ = sb("b_open", [H, NT], at=buf)
        carried_m = sb("b_carried_m", [H, NT + 1], at=buf)
        alpha = sb("b_alpha", [H, NT], at=buf)
        beta = sb("b_beta", [H, NT], at=buf)
        carried_d = sb("b_carried_d", [H, NT], at=buf)
        wide_a = sb("b_wide_a", [F, NT], at=buf)
        wide_b = sb("b_wide_b", [F, NT], at=buf)
        carried = sb("b_carried", [F, NT], at=buf)
        head_of = sb("head_of", [H, F], at=buf)
        new_m = sb("b_new_m", [BP, BC, H], at=buf)
        own_f = sb("b_own_f", [BP, BC, H], at=buf)
        carry_f = sb("b_carry_f", [BP, BC, H], at=buf)
        tmp = sb("b_tmp", [BP, BC, H], at=buf)
        back = sb("b_back", [BP, BC, F], at=buf)
        first_rows = runs3[0:NT, :].rearrange("(c p) f -> p c f", p=BP)
        done = c["x_turned_out"]
        WIDE = NT // 4
        with nc.Block() as block:
            @block.gpsimd
            def _(pool):
                ch = Chain(pool, pool_chain)
                ch.link(nc.gpsimd.memset(head_of[:, :], 1.0))
                ch.link(nc.gpsimd.affine_select(out=head_of[:, :], in_=head_of[:, :], compare_op=ALU.is_ge, fill=0.0, base=0,
                                                pattern=[[1, F]], channel_multiplier=-HD))
                ch.link(nc.gpsimd.affine_select(out=head_of[:, :], in_=head_of[:, :], compare_op=ALU.is_gt, fill=0.0, base=HD,
                                                pattern=[[-1, F]], channel_multiplier=HD))
                pool_chain.close(ch.n)
                for k in range(BC):
                    nc.gpsimd.indirect_dma_start(lasts[:, k, :], None, runs3, bass.IndirectOffsetOnAxis(
                        ap=last_row[:, k:k + 1], axis=0)).then_inc(gathered[0].sem, 16)
                pool.wait_ge(gathered[0].sem, gathered[0].at(16 * BC))

            @block.sync
            def _(sp):
                sp.dma_start(firsts[:, :, :], first_rows).then_inc(loaded[0].sem, 16)
                sp.wait_ge(loaded[0].sem, loaded[0].at(16))
        gathered[0].close(16 * BC)
        loaded[0].close(16)

        def turn_all(pieces):
            with nc.Block() as block:
                @block.tensor
                def _(pe):
                    for first_bank, wide, f0, _ in pieces:
                        for k in range(BC):
                            ins = nc.tensor.transpose(bank(first_bank + k // 4)[0:wide, (k % 4) * BP:(k % 4 + 1) * BP],
                                                      lasts[:, k, f0:f0 + wide], ident[0:BP, 0:BP])
                        ins.then_inc(c["x_turned"].sem, 1)

                @block.vector
                def _(dve):
                    for n, (first_bank, wide, f0, dest) in enumerate(pieces):
                        dve.wait_ge(c["x_turned"].sem, c["x_turned"].at(n + 1))
                        nc.vector.memset(dest[:, 0:1], 0.0)
                        for k in range(4):
                            w = min(4 * BP, NT - k * 4 * BP)
                            nc.vector.tensor_copy(dest[:, 1 + k * 4 * BP:1 + k * 4 * BP + w], bank(first_bank + k)[0:wide, 0:w])
            c["x_turned"].close(len(pieces))

        turn_all([(0, F, 0, last_T), (4, H, F, den_T)])
        turn_all([(0, H, F + H, max_T)])
        with nc.Block() as block:
            @block.vector
            def _(dve):
                ch = Chain(dve, dve_chain)
                c4, t4 = carries[0:H, :], through[0:H, :]
                ch.link(nc.vector.tensor_scalar(open_[:, :], c4, -1.0, FAR, ALU.add, ALU.mult))
                ch.link(nc.vector.tensor_tensor(alpha[:, :], max_T[:, 0:NT], c4, ALU.mult))
                ch.link(nc.vector.tensor_tensor(alpha[:, :], alpha[:, :], open_[:, :], ALU.add))
                ch.link(nc.vector.tensor_scalar(open_[:, :], t4, -1.0, FAR, ALU.add, ALU.mult))
                ch.link(nc.vector.memset(carried_m[:, 0:1], -FAR))
                ch.link(nc.vector.tensor_tensor_scan(carried_m[:, 1:NT + 1], open_[:, :], alpha[:, :], -FAR, ALU.add, ALU.max))
                ch.link(nc.vector.tensor_tensor(alpha[:, :], carried_m[:, 0:NT], carried_m[:, 1:NT + 1], ALU.subtract))
                ch.link(nc.vector.tensor_scalar(alpha[:, :], alpha[:, :], 0.0, None, ALU.min))
                ch.link(nc.vector.tensor_tensor(beta[:, :], max_T[:, 0:NT], carried_m[:, 1:NT + 1], ALU.subtract))
                nc.vector.tensor_scalar(beta[:, :], beta[:, :], 0.0, None, ALU.min).then_inc(c["exponent"].sem, 1)
                dve.wait_ge(c["exponent_out"].sem, c["exponent_out"].at(1))
                ch.link(nc.vector.tensor_tensor(alpha[:, :], alpha[:, :], t4, ALU.mult))
                nc.vector.tensor_tensor(beta[:, :], beta[:, :], c4, ALU.mult).then_inc(c["normed"].sem, 1)
                dve.wait_ge(c["normed"].sem, c["normed"].at(1))
                ch.link(nc.vector.tensor_tensor(den_T[:, 0:NT], den_T[:, 0:NT], beta[:, :], ALU.mult))
                nc.vector.tensor_tensor_scan(carried_d[:, :], alpha[:, :], den_T[:, 0:NT], 0.0, ALU.mult, ALU.add)
                for k, dest in enumerate((wide_a, wide_b)):
                    for q in range(4):
                        dve.wait_ge(c["product"].sem, c["product"].at(4 * k + q + 1))
                        ins = nc.vector.tensor_copy(dest[:, q * WIDE:(q + 1) * WIDE], bank(4 * k + q)[:, 0:WIDE])
                ch.link(ins)
                ch.link(nc.vector.tensor_tensor(wide_b[:, :], wide_b[:, :], last_T[:, 0:NT], ALU.mult))
                ch.link(nc.vector.tensor_tensor_scan(carried[:, :], wide_a[:, :], wide_b[:, :], 0.0, ALU.mult, ALU.add))
                dve_chain.close(ch.n)

            @block.scalar
            def _(act):
                act.wait_ge(c["exponent"].sem, c["exponent"].at(1))
                nc.scalar.activation(alpha[:, :], alpha[:, :], ACT.Exp)
                nc.scalar.activation(beta[:, :], beta[:, :], ACT.Exp).then_inc(c["exponent_out"].sem, 1)

            @block.tensor
            def _(pe):
                pe.wait_ge(c["normed"].sem, c["normed"].at(1))
                for k, s_ in enumerate((alpha, beta)):
                    for q in range(4):
                        nc.tensor.matmul(bank(4 * k + q)[:, 0:WIDE], head_of[:, :], s_[:, q * WIDE:(q + 1) * WIDE],
                                         start=True, stop=True).then_inc(c["product"].sem, 1)
        for k, n in (("exponent", 1), ("exponent_out", 1), ("normed", 1), ("product", 8)):
            c[k].close(n)
        with nc.Block() as block:
            @block.tensor
            def _(pe):
                for k in range(BC):
                    nc.tensor.transpose(bank(k // 4)[0:BP, (k % 4) * F:(k % 4 + 1) * F], carried[:, k * BP:(k + 1) * BP], ident[:, :])
                    nc.tensor.transpose(bank(4)[0:BP, k * H:(k + 1) * H], carried_d[:, k * BP:(k + 1) * BP], ident[0:H, 0:H])
                    ins = nc.tensor.transpose(bank(5)[0:BP, k * H:(k + 1) * H], carried_m[:, 1 + k * BP:1 + (k + 1) * BP], ident[0:H, 0:H])
                ins.then_inc(c["x_turned"].sem, 1)

            @block.vector
            def _(dve):
                ch = Chain(dve, dve_chain)
                dve.wait_ge(c["x_turned"].sem, c["x_turned"].at(1))
                carry_s = ps[0:BP, 0:BC * F].rearrange("p (c f) -> p c f", f=F)
                carry_d = bank(4)[0:BP, 0:BC * H].rearrange("p (c h) -> p c h", h=H)
                carry_m = bank(5)[0:BP, 0:BC * H].rearrange("p (c h) -> p c h", h=H)
                own_s, own_d, own_m = firsts[:, :, 0:F], firsts[:, :, F:F + H], firsts[:, :, F + H:RW]
                ch.link(nc.vector.tensor_tensor(new_m[:, :, :], own_m, carry_m, ALU.max))
                nc.vector.tensor_tensor(own_f[:, :, :], own_m, new_m[:, :, :], ALU.subtract)
                nc.vector.tensor_tensor(carry_f[:, :, :], carry_m, new_m[:, :, :], ALU.subtract).then_inc(c["exponent"].sem, 1)
                dve.wait_ge(c["exponent_out"].sem, c["exponent_out"].at(1))
                ch.link(nc.vector.tensor_tensor(own_d, own_d, own_f[:, :, :], ALU.mult))
                ch.link(nc.vector.tensor_tensor(tmp[:, :, :], carry_d, carry_f[:, :, :], ALU.mult))
                ch.link(nc.vector.tensor_tensor(own_d, own_d, tmp[:, :, :], ALU.add))
                ch.link(nc.vector.tensor_copy(own_m, new_m[:, :, :]))
                for h in range(H):
                    part = slice(h * HD, (h + 1) * HD)
                    wide = lambda t: t[:, :, h:h + 1].to_broadcast([BP, BC, HD])
                    nc.vector.tensor_tensor(firsts[:, :, part], firsts[:, :, part], wide(own_f), ALU.mult)
                    ins = nc.vector.tensor_tensor(back[:, :, part], carry_s[:, :, part], wide(carry_f), ALU.mult)
                ch.link(ins)
                nc.vector.tensor_tensor(own_s, own_s, back[:, :, :], ALU.add).then_inc(c["residual"].sem, 1)
                dve_chain.close(ch.n)

            @block.scalar
            def _(act):
                act.wait_ge(c["exponent"].sem, c["exponent"].at(1))
                nc.scalar.activation(own_f[:, :, :], own_f[:, :, :], ACT.Exp)
                nc.scalar.activation(carry_f[:, :, :], carry_f[:, :, :], ACT.Exp).then_inc(c["exponent_out"].sem, 1)

            @block.sync
            def _(sp):
                sp.wait_ge(c["residual"].sem, c["residual"].at(1))
                sp.dma_start(first_rows, firsts[:, :, :]).then_inc(stored[0].sem, 16)
                sp.wait_ge(stored[0].sem, stored[0].at(16))
        stored[0].close(16)
        for k in ("x_turned", "exponent", "exponent_out", "residual"):
            c[k].close(1)
        buf.close()

    def show(x_dram):
        with nc.Block() as block:
            @block.sync
            def _(sp):
                sp.dma_start(nodes(out), nodes(x_dram)).then_inc(setup_dma.sem, 16)
                setup_dma.close(16)
                sp.wait_ge(setup_dma.sem, setup_dma.at(0))

    node_phase("pre", a["x"], None, None, None)
    scatter_pass()
    node_layer("L0", a["x"], x_state[0], None, table[0])
    if STOP_AFTER == 1:
        return show(x_state[0])
    message_pass(table[0])
    border_pass("B1")
    node_layer("L1", x_state[0], x_state[1], None, table[0])
    if STOP_AFTER == 2:
        return show(x_state[1])
    edge_pass("E2", table[0])
    border_pass("B2")
    node_phase("L2a", None, None, table[0], table[1])
    edge_pass("E3", table[1])
    border_pass("B3")
    node_layer("L2b", x_state[1], x_state[0], table[1], table3)
    if STOP_AFTER == 3:
        return show(x_state[0])
    attention_pass(*attention_setup())
    att.close()
    attention_border()
    node_layer("L3", x_state[0], out, None, None)


_INS = ("x src dst edge_attr_64 edge_type_3 edge_weight "
        "L0_gnn_bn1_gamma L0_gnn_bn1_beta L0_gnn_bn1_mean L0_gnn_bn1_var L0_gnn_W1 L0_gnn_b1 "
        "L0_gnn_bn2_gamma L0_gnn_bn2_beta L0_gnn_bn2_mean L0_gnn_bn2_var L0_gnn_W2 L0_gnn_b2 "
        "L1_gnn_We1 L1_gnn_be1 L1_gnn_We2 L1_gnn_be2 L1_gnn_Wt L1_gnn_bt L1_gnn_Wn1 L1_gnn_bn1 L1_gnn_Wn2 L1_gnn_bn2 "
        "L2_gnn_W1 L2_gnn_b1 L2_gnn_W2 L2_gnn_b2 "
        "L3_gnn_Wq L3_gnn_Wk L3_gnn_Wv L3_gnn_attn_lin L3_gnn_edge_embed_table L3_gnn_Wout L3_gnn_bout").split()


def kernel(**inputs):
    import numpy as np
    import concourse.bacc as bacc
    from concourse.bass_utils import run_bass_kernel_spmd as run

    nc = bacc.Bacc("TRN2", target_bir_lowering=False, num_devices=1)
    arrays = {n: np.ascontiguousarray(inputs[n]) for n in _INS}
    aps = {n: nc.dram_tensor(n, v.shape, mybir.dt.from_np(v.dtype), kind="ExternalInput").ap() for n, v in arrays.items()}
    out = nc.dram_tensor("out", (N, F), F32, kind="ExternalOutput").ap()
    gnn_kernel(nc, aps, out)
    return run(nc, [arrays], core_ids=[0]).results[0]["out"]
```

```python
import concourse.bass as bass
from concourse import mybir
from contextlib import ExitStack

F32, I32, BF16 = mybir.dt.float32, mybir.dt.int32, mybir.dt.bfloat16
ALU = mybir.AluOpType
ACT = mybir.ActivationFunctionType
AX = mybir.AxisListType

N, F, E = 12500, 128, 200000
H, HD, KINDS, EC = 4, 32, 3, 64

NP, NW, WB = 125, 100, 10
NPAIR = NW // (2 * WB)

TE = 128
FULL, REM = E // TE, E % TE
HB = 16
NPASS = -(-(FULL + 1) // (2 * HB))
NT = NPASS * 2 * HB
NCH = -(-(FULL + 1) // TE)
CHT, CHR = FULL // TE, FULL % TE

BP, BC = 112, NT // 112
PAD_DST, NO_KEY = 16000.0, 30000.0
ZERO_ROW = (TE - 1) * NT + NT - 1
SW = TE + 4
PAD_PLACE = 30000.0
BN_EPS, LN_EPS, DEN_EPS, MAX_FLOOR, FAR = 1e-3, 1e-5, 1e-10, -100.0, 2.0 ** 100
SLOPE = 0.2
RW = F + 2 * H
TW = F + H + KINDS * H
NACC = 99 * 128
AW = F + 4
NACCS = 4
DVE_WINDOWS = 2
CLEARS = 9


class Count:

    def __init__(self, sem):
        self.sem, self.base = sem, 0

    def at(self, n):
        return self.base + n

    def close(self, n):
        self.base += n


class Chain:

    def __init__(self, eng, count, per=0, i=0):
        self.eng, self.count, self.offset, self.n = eng, count, per * i if per else 0, 0

    def link(self, instruction):
        self.n += 1
        instruction.then_inc(self.count.sem, 1)
        self.eng.wait_ge(self.count.sem, self.count.base + self.n + self.offset)


def gnn_kernel(nc, a, out):
    ctx = ExitStack()
    with ctx:
        build(nc, a, out, ctx)


def build(nc, a, out, ctx):
    def sb(name, shape, dt=F32, at=ctx):
        return at.enter_context(nc.sbuf_tensor(name, shape, dt))

    def dram(name, shape):
        return nc.dram_tensor(name, shape, F32, kind="Internal").ap()

    def count(name):
        return Count(ctx.enter_context(nc.semaphore(name)))

    x_state = [dram(f"x_state{n}", [N, F]) for n in range(2)]
    table = [dram(f"table{n}", [N, F]) for n in range(2)]
    table3 = dram("table3", [N, TW])
    runs = dram("runs", [TE * NT, F])
    runs3 = dram("runs3", [TE * NT, RW])
    keys = dram("keys", [NCH * TE, 2 * TE])
    starts_d = dram("starts_d", [NCH * TE, SW])
    primed = dram("primed", [4 + HB + NACCS, 1])
    edge_before = dram("edge_before", [NP + 1, 1])
    by_run = dram("by_run", [NACC, F])
    acc = [dram(f"acc{k}", [NACC, AW]) for k in range(NACCS)]
    kd_edge = dram("kd_edge", [NCH * TE * TE + NP * TE, H])
    kd_rows = dram("kd_rows", [N, H])

    ident = sb("ident", [128, 128])
    iota_run = sb("iota_run", [128, 128])
    ones = sb("ones", [128, 128])
    kd_node = sb("kd_node", [NP, NW, H])
    zeros = sb("zeros", [128, AW])
    eps_ln = sb("eps_ln", [128, 1])
    src_T = sb("src_T", [128, NT + 2 * HB], I32)
    rank_T = sb("rank_T", [128, NT])
    carries = sb("carries", [128, NT])
    through = sb("through", [128, NT])
    last_row = sb("last_row", [BP, BC], I32)
    node_row = sb("node_row", [NP, NW + 2 * WB], I32)
    degree = sb("degree", [NP, NW])
    dinv = sb("dinv", [NP, NW])
    first_edge = sb("first_edge", [NP, NW])
    place = sb("place", [NP, NW + 2 * WB], I32)
    tile_place = sb("tile_place", [1, NT + 2 * HB], I32)
    spot = sb("spot", [NP, NW], I32)
    idx_buf = sb("idx_buf", [128, 2, HB], I32)
    rank_buf = sb("rank_buf", [128, 2, HB])
    row_buf = sb("row_buf", [NP, 2, WB], I32)

    ps = ctx.enter_context(nc.psum_tensor("ps", [128, 8 * 512], F32))

    def bank(n, k=1):
        return ps[:, n * 512:(n + k) * 512]

    loaded = [count(f"loaded{s}") for s in range(2)]
    stored = [count(f"stored{s}") for s in range(2)]
    tab_stored = [count(f"tab_stored{s}") for s in range(2)]
    gathered = [count(f"gathered{s}") for s in range(4)]
    idx_ready = [count(f"idx_ready{s}") for s in range(4)]
    onehot_ready = [count(f"onehot_ready{s}") for s in range(2)]
    sums_ready = [count(f"sums_ready{s}") for s in range(2)]
    evacuated = [count(f"evacuated{s}") for s in range(2)]
    scattered = [count(f"scattered{k}") for k in range(NACCS)]
    window_in = [count(f"window_in{s}") for s in range(2)]
    counts_ready, counts_out, scatter_idx = count("counts_ready"), count("counts_out"), count("scatter_idx")
    dve_chain, act_chain, pool_chain = count("dve_chain"), count("act_chain"), count("pool_chain")
    half_searched = count("half_searched")
    stage_chains = count("update_chain"), count("norm_chain")
    pause = count("pause")
    setup_dma = count("setup_dma")
    names = ("agg_scaled x_turned x_turned_out agg_turned agg_turned_out product product_out residual "
             "variance deviation normed normed_turned normed_turned_out table_product table_out "
             "ea_turned ea_out gate_ready gate_out hid_ready hid_out ef_ready ef_out z_ready z_out msg_out "
             "pe_setup act_setup dve_setup pool_setup batch_done activated exponent exponent_out").split()
    c = {n: count(n) for n in names}
    every = [half_searched, *stage_chains, counts_ready, counts_out, scatter_idx, *idx_ready, *onehot_ready, *sums_ready, *evacuated, *c.values()]

    mat = {}

    def weight(name, shape, src):
        t = sb("w_" + name, shape)
        mat[name] = t
        loads.append((t, src))
        return t

    loads = []
    for n in ("bn1_gamma", "bn1_beta", "bn1_mean", "bn1_var"):
        weight(n, [F, 1], a["L0_gnn_" + n].rearrange("(p o) -> p o", o=1))
    for n in ("bn2_gamma", "bn2_beta", "bn2_mean", "bn2_var"):
        weight(n, [F, 2], a["L0_gnn_" + n].rearrange("(o p) -> p o", o=2))
    for n, key in (("be1", "L1_gnn_be1"), ("be2", "L1_gnn_be2"), ("bt", "L1_gnn_bt"), ("gcn_b1", "L2_gnn_b1")):
        weight(n, [F, 1], a[key].rearrange("(p o) -> p o", o=1))
    for n, key in (("b1_rows", "L0_gnn_b1"), ("b2_rows", "L0_gnn_b2"), ("nb1_rows", "L1_gnn_bn1"),
                   ("nb2_rows", "L1_gnn_bn2"), ("gcn_b2_rows", "L2_gnn_b2"), ("bout_rows", "L3_gnn_bout")):
        weight(n, [128, F], a[key].partition_broadcast(128))
    weight("W1", [F, F], a["L0_gnn_W1"])
    weight("W2", [F, 2, F], a["L0_gnn_W2"].rearrange("(k p) n -> p k n", k=2))
    weight("We1", [EC, F], a["L1_gnn_We1"])
    weight("We2", [F, F], a["L1_gnn_We2"])
    weight("Wt", [1, F], a["L1_gnn_Wt"])
    weight("Wn1", [F, 2, F], a["L1_gnn_Wn1"].rearrange("(k p) n -> p k n", k=2))
    weight("Wn2", [F, F], a["L1_gnn_Wn2"])
    weight("gcn_W1", [F, F], a["L2_gnn_W1"])
    weight("gcn_W2", [F, F], a["L2_gnn_W2"])
    weight("Wq", [F, F], a["L3_gnn_Wq"])
    weight("Wk", [F, F], a["L3_gnn_Wk"])
    weight("Wv", [F, F], a["L3_gnn_Wv"])
    weight("Wout", [F, F], a["L3_gnn_Wout"])
    weight("a_q", [128, H, HD], a["L3_gnn_attn_lin"][0, :, 0:HD].partition_broadcast(128))
    weight("a_k", [128, H, HD], a["L3_gnn_attn_lin"][0, :, HD:2 * HD].partition_broadcast(128))
    weight("embed", [128, KINDS, F], a["L3_gnn_edge_embed_table"].partition_broadcast(128))
    bn1_scale, bn1_shift = sb("bn1_scale", [F, 1]), sb("bn1_shift", [F, 1])
    bn2_scale, bn2_shift = sb("bn2_scale", [F, 2]), sb("bn2_shift", [F, 2])
    score_w = sb("score_w", [F, (2 + KINDS) * H])
    score_tmp = sb("score_tmp", [F, F])
    m = mat

    setup = ExitStack()
    edge_i = sb("edge_i", [128, 2, NCH, TE], I32, at=setup)
    edge_f = sb("edge_f", [128, 2, NCH, TE], at=setup)
    with nc.Block() as block:
        @block.gpsimd
        def _(pool):
            ch = Chain(pool, pool_chain)
            nc.gpsimd.memset(zeros[:, :], 0.0)
            nc.gpsimd.memset(ones[:, :], 1.0)
            nc.gpsimd.memset(src_T[:, NT:NT + 2 * HB], 0)
            nc.gpsimd.memset(eps_ln[:, :], LN_EPS)
            ch.link(nc.gpsimd.memset(ident[:, :], 0.0))
            nc.gpsimd.affine_select(out=ident[:, :], in_=ident[:, :], compare_op=ALU.not_equal, fill=1.0, base=0,
                                    pattern=[[-1, 128]], channel_multiplier=1)
            nc.gpsimd.iota(iota_run[:, :], pattern=[[1, 128]], base=0, channel_multiplier=0,
                           allow_small_or_imprecise_dtypes=True)
            pool_chain.close(ch.n)
            for k in every:
                pool.sem_inc(k.sem, 1)
                k.close(1)

        @block.vector
        def _(dve):
            nc.vector.memset(edge_i[:, 0, CHT:NCH, :], int(PAD_DST))
            nc.vector.memset(edge_i[:, 1, CHT:NCH, :], 0)

        @block.sync
        def _(sp):
            for t, s in loads:
                full = t[:, :] if len(t.shape) == 2 else t[:, :, :]
                sp.dma_start(full, s, allow_slow_non_contiguous=True).then_inc(setup_dma.sem, 16)
            setup_dma.close(16 * len(loads))
            sp.wait_ge(setup_dma.sem, setup_dma.at(0))

    with nc.Block() as block:
        @block.gpsimd
        def _(pool):
            for r in range(HB // NACCS + 1):
                for k in range(NACCS):
                    row = 4 + r * NACCS + k
                    pool.dma_start(primed[row:row + 1, :], zeros[0:1, 0:1]).then_inc(scattered[k].sem, 16)
            for k in scattered:
                k.close(16 * (HB // NACCS + 1))
                pool.wait_ge(k.sem, k.at(0))

        @block.sync
        def _(sp):
            n = 0
            for k, key in enumerate(("dst", "src")):
                v = a[key]
                whole, rest = CHT * TE * TE, CHR * TE
                sp.dma_start(edge_i[:, k, 0:CHT, :], v[0:whole].rearrange("(c p e) -> p c e", c=CHT, p=128)
                             ).then_inc(setup_dma.sem, 16)
                sp.dma_start(edge_i[0:CHR, k, CHT, :], v[whole:whole + rest].rearrange("(p e) -> p e", e=TE)
                             ).then_inc(setup_dma.sem, 16)
                sp.dma_start(edge_i[CHR:CHR + 1, k, CHT, 0:REM], v[FULL * TE:E].rearrange("(p e) -> p e", p=1)
                             ).then_inc(setup_dma.sem, 16)
                n += 3
            setup_dma.close(16 * n)
            sp.wait_ge(setup_dma.sem, setup_dma.at(0))

        @block.scalar
        def _(act):
            act.wait_ge(c["dve_setup"].sem, c["dve_setup"].at(2))
            nc.scalar.activation(bn1_scale[:, :], bn1_shift[:, :], ACT.Sqrt)
            nc.scalar.activation(bn2_scale[:, :], bn2_shift[:, :], ACT.Sqrt).then_inc(c["act_setup"].sem, 1)

        @block.vector
        def _(dve):
            ch = Chain(dve, dve_chain)
            nc.vector.tensor_scalar_add(bn1_shift[:, :], m["bn1_var"][:, :], BN_EPS).then_inc(c["dve_setup"].sem, 1)
            nc.vector.tensor_scalar_add(bn2_shift[:, :], m["bn2_var"][:, :], BN_EPS).then_inc(c["dve_setup"].sem, 1)
            c["dve_setup"].close(2)
            cols = [("Wq", m["a_q"][:, :, :])] + [("Wq", m["embed"][:, k, :].rearrange("p (h d) -> p h d", h=H))
                                                 for k in range(KINDS)] + [("Wk", m["a_k"][:, :, :])]
            tmp = score_tmp[:, :].rearrange("p (h d) -> p h d", h=H)
            for k, (w, row) in enumerate(cols):
                ch.link(nc.vector.tensor_tensor(tmp, m[w][:, :].rearrange("p (h d) -> p h d", h=H), row, ALU.mult))
                ch.link(nc.vector.tensor_reduce(score_w[:, k * H:(k + 1) * H], tmp, AX.X, ALU.add))
            dve.wait_ge(c["act_setup"].sem, c["act_setup"].at(1))
            c["act_setup"].close(1)
            for scale, shift, g, b, mean in ((bn1_scale, bn1_shift, "bn1_gamma", "bn1_beta", "bn1_mean"),
                                             (bn2_scale, bn2_shift, "bn2_gamma", "bn2_beta", "bn2_mean")):
                ch.link(nc.vector.reciprocal(scale[:, :], scale[:, :]))
                ch.link(nc.vector.tensor_tensor(scale[:, :], scale[:, :], m[g][:, :], ALU.mult))
                ch.link(nc.vector.tensor_tensor(shift[:, :], scale[:, :], m[mean][:, :], ALU.mult))
                ch.link(nc.vector.tensor_tensor(shift[:, :], m[b][:, :], shift[:, :], ALU.subtract))
            dve_chain.close(ch.n)

    work = ExitStack()
    start = sb("start", [128, NCH, TE], at=work)
    ranks = sb("ranks", [128, NCH, TE], at=work)
    valid = sb("valid", [128, NCH, TE], at=work)
    key_out = sb("key_out", [128, NCH, 2 * TE], at=work)
    dst_T = sb("dst_T", [128, NT], at=work)
    marks = sb("marks", [128, NCH, SW], at=work)
    with nc.Block() as block:
        @block.vector
        def _(dve):
            ch = Chain(dve, dve_chain)
            dst = edge_f[:, 0, :, :]
            ch.link(nc.vector.tensor_copy(edge_f[:, :, :, :], edge_i[:, :, :, :]))
            nc.vector.memset(start[:, :, 0:1], 1.0)
            ch.link(nc.vector.tensor_tensor(start[:, :, 1:TE], dst[:, :, 1:TE], dst[:, :, 0:TE - 1], ALU.not_equal))
            ch.link(nc.vector.tensor_scalar(valid[:, :, :], dst, float(N), None, ALU.is_lt))
            for k in range(NCH):
                last = nc.vector.tensor_tensor_scan(ranks[:, k, :], start[:, k, :], zeros[:, 0:TE], 0.0, ALU.add, ALU.add)
            ch.link(last)
            ch.link(nc.vector.tensor_tensor(ranks[:, :, :], ranks[:, :, :], valid[:, :, :], ALU.mult))
            nc.vector.tensor_scalar_add(ranks[:, :, :], ranks[:, :, :], -1.0).then_inc(c["dve_setup"].sem, 1)
            ch.link(nc.vector.scalar_tensor_tensor(key_out[:, :, 0:TE], dst, -NO_KEY, start[:, :, :], ALU.add, ALU.mult))
            ch.link(nc.vector.tensor_scalar_add(key_out[:, :, 0:TE], key_out[:, :, 0:TE], NO_KEY))
            ch.link(nc.vector.memset(marks[:, :, :], 0.0))
            nc.vector.tensor_scalar(marks[:, :, 0:TE], start[:, :, :], -FAR, None, ALU.mult)
            ch.link(nc.vector.memset(marks[:, :, TE:TE + 1], -FAR))
            nc.vector.tensor_copy(key_out[:, :, TE:2 * TE], dst).then_inc(c["dve_setup"].sem, 1)
            for k in range(NCH):
                wide = min(TE, NT - k * TE)
                for j, dest in enumerate((dst_T, src_T, rank_T)):
                    n = 3 * k + j
                    dve.wait_ge(c["pe_setup"].sem, c["pe_setup"].at(n + 1))
                    nc.vector.tensor_copy(dest[:, k * TE:k * TE + wide], bank(n % 8)[:, 0:wide]
                                          ).then_inc(c["x_turned_out"].sem, 1)
            dve_chain.close(ch.n)

        @block.tensor
        def _(pe):
            pe.wait_ge(c["dve_setup"].sem, c["dve_setup"].at(1))
            for k in range(NCH):
                for j, s in enumerate((edge_f[:, 0, k, :], edge_f[:, 1, k, :], ranks[:, k, :])):
                    n = 3 * k + j
                    if n >= 8:
                        pe.wait_ge(c["x_turned_out"].sem, c["x_turned_out"].at(n - 7))
                    nc.tensor.transpose(bank(n % 8)[:, 0:128], s, ident[:, :]).then_inc(c["pe_setup"].sem, 1)

        @block.sync
        def _(sp):
            sp.wait_ge(c["dve_setup"].sem, c["dve_setup"].at(2))
            sp.dma_start(keys.rearrange("(c p) k -> p c k", p=128), key_out[:, :, :]).then_inc(setup_dma.sem, 16)
            sp.dma_start(starts_d.rearrange("(c p) k -> p c k", p=128), marks[:, :, :]).then_inc(setup_dma.sem, 16)
            setup_dma.close(32)
            sp.wait_ge(setup_dma.sem, setup_dma.at(0))
    c["dve_setup"].close(2)
    c["pe_setup"].close(3 * NCH)
    c["x_turned_out"].close(3 * NCH)

    pick = sb("pick", [128, 2, 128], at=work)
    first_bc = sb("first_bc", [128, NT], at=work)
    last_bc = sb("last_bc", [128, NT], at=work)
    node_id = sb("node_id", [NP, NW], at=work)
    tiles_at = sb("tiles_at", [NP, NW], at=work)
    tile_f = sb("tile_f", [NP, NW], at=work)
    node_half = sb("node_half", [NP, NW], at=work)
    junk = sb("junk", [128, NT], at=work)
    row_f = sb("row_f", [BP, BC], at=work)
    single = sb("single", [128, NT], at=work)
    rank_bc = sb("rank_bc", [128, NT], at=work)
    place_f = sb("place_f", [1, NT], at=work)
    zero_row = sb("zero_row", [1, NT], at=work)
    blank = valid[:, :, :].rearrange("p c e -> p (c e)")
    WIDE = NT // 4
    with nc.Block() as block:
        @block.gpsimd
        def _(pool):
            ch = Chain(pool, pool_chain)
            nc.gpsimd.memset(zero_row[:, :], 0.0)
            ch.link(nc.gpsimd.memset(pick[:, :, :], 0.0))
            for k, p in enumerate((0, TE - 1)):
                ins = nc.gpsimd.affine_select(out=pick[:, k, :], in_=pick[:, k, :], compare_op=ALU.not_equal,
                                              fill=1.0, base=-p, pattern=[[0, 128]], channel_multiplier=1)
            ins.then_inc(c["pool_setup"].sem, 1)
            nc.gpsimd.iota(node_id[:, :], pattern=[[1, NW]], base=0, channel_multiplier=NW,
                           allow_small_or_imprecise_dtypes=True).then_inc(c["pool_setup"].sem, 1)
            nc.gpsimd.iota(row_f[:, :], pattern=[[BP, BC]], base=0, channel_multiplier=1,
                           allow_small_or_imprecise_dtypes=True).then_inc(c["pool_setup"].sem, 1)
            ch.link(nc.gpsimd.memset(blank[:, :], 0.0))
            pool.sem_inc(c["pool_setup"].sem, 1)
            pool_chain.close(ch.n)

        @block.sync
        def _(sp):
            sp.wait_ge(c["pool_setup"].sem, c["pool_setup"].at(4))
            wide = NACC // 128 // CLEARS
            sp.dma_start(by_run.rearrange("(p a b) f -> p a (b f)", p=128, a=CLEARS),
                         blank[:, 0:wide * F].unsqueeze(1).to_broadcast([128, CLEARS, wide * F])).then_inc(setup_dma.sem, 16)
            for k in range(NACCS // 2):
                sp.dma_start(acc[k].rearrange("(p a b) f -> p a (b f)", p=128, a=CLEARS),
                             blank[:, 0:wide * AW].unsqueeze(1).to_broadcast([128, CLEARS, wide * AW])
                             ).then_inc(loaded[0].sem, 16)
            setup_dma.close(16)

        @block.tensor
        def _(pe):
            pe.wait_ge(c["pool_setup"].sem, c["pool_setup"].at(1))
            for k in range(2):
                for q in range(4):
                    nc.tensor.matmul(bank(4 * k + q)[:, 0:WIDE], pick[:, k, :], dst_T[:, q * WIDE:(q + 1) * WIDE],
                                     start=True, stop=True).then_inc(c["pe_setup"].sem, 1)
            for q in range(4):
                pe.wait_ge(c["x_turned_out"].sem, c["x_turned_out"].at(q + 1))
                nc.tensor.matmul(bank(4 + q)[:, 0:WIDE], pick[:, 1, :], rank_T[:, q * WIDE:(q + 1) * WIDE],
                                 start=True, stop=True).then_inc(c["normed_turned"].sem, 1)
            pe.wait_ge(c["dve_setup"].sem, c["dve_setup"].at(1))
            for k in range(BC):
                last = nc.tensor.matmul(bank(0)[0:BP, k:k + 1], rank_T[:, k * BP:(k + 1) * BP], pick[:, 1, 0:1],
                                        start=True, stop=True)
            last.then_inc(c["pe_setup"].sem, 1)

        @block.vector
        def _(dve):
            ch = Chain(dve, dve_chain)
            for k, dest in enumerate((first_bc, last_bc)):
                for q in range(4):
                    dve.wait_ge(c["pe_setup"].sem, c["pe_setup"].at(4 * k + q + 1))
                    ins = nc.vector.tensor_copy(dest[:, q * WIDE:(q + 1) * WIDE], bank(4 * k + q)[:, 0:WIDE])
                    if k == 1 and q < 3:
                        ins.then_inc(c["x_turned_out"].sem, 1)
            ins.then_inc(c["dve_setup"].sem, 1)
            dve.wait_ge(c["dve_setup"].sem, c["dve_setup"].at(1))
            dve.sem_inc(c["x_turned_out"].sem, 1)
            for q in range(4):
                dve.wait_ge(c["normed_turned"].sem, c["normed_turned"].at(q + 1))
                ins = nc.vector.tensor_copy(rank_bc[:, q * WIDE:(q + 1) * WIDE], bank(4 + q)[:, 0:WIDE])
            ch.link(ins)
            dve.wait_ge(c["dve_setup"].sem, c["dve_setup"].at(1))
            nc.vector.memset(carries[:, 0:1], 0.0)
            nc.vector.tensor_tensor(carries[:, 1:NT], first_bc[:, 1:NT], last_bc[:, 0:NT - 1], ALU.is_equal)
            ch.link(nc.vector.tensor_scalar(junk[:, :], first_bc[:, :], float(N), None, ALU.is_lt))
            ch.link(nc.vector.tensor_tensor(carries[:, :], carries[:, :], junk[:, :], ALU.mult))
            nc.vector.memset(through[:, 0:1], 0.0)
            ch.link(nc.vector.tensor_tensor(single[:, :], first_bc[:, :], last_bc[:, :], ALU.is_equal))
            ch.link(nc.vector.tensor_tensor(through[:, 1:NT], carries[:, 1:NT], single[:, 0:NT - 1], ALU.mult))
            row = rank_bc[0:1, :]
            ch.link(nc.vector.scalar_tensor_tensor(row, row, 1.0, carries[0:1, :], ALU.add, ALU.subtract))
            nc.vector.memset(place_f[0:1, 0:1], 0.0)
            ch.link(nc.vector.tensor_tensor_scan(place_f[0:1, 1:NT], row[:, 0:NT - 1], zero_row[0:1, 0:NT - 1], 0.0,
                                                 ALU.add, ALU.add))
            ch.link(nc.vector.tensor_tensor(place_f[0:1, :], place_f[0:1, :], carries[0:1, :], ALU.subtract))
            ch.link(nc.vector.tensor_scalar(place_f[0:1, :], place_f[0:1, :], 0.0, float(N), ALU.max, ALU.min))
            nc.vector.tensor_copy(tile_place[:, 0:NT], place_f[0:1, :])
            nc.vector.memset(tile_place[:, NT:NT + 2 * HB], 0)
            dve.wait_ge(c["pe_setup"].sem, c["pe_setup"].at(9))
            dve.wait_ge(c["pool_setup"].sem, c["pool_setup"].at(3))
            ch.link(nc.vector.tensor_scalar(junk[0:BP, 0:BC], bank(0)[0:BP, 0:BC], 0.0, float(NT), ALU.max, ALU.mult))
            ch.link(nc.vector.tensor_tensor(row_f[:, :], row_f[:, :], junk[0:BP, 0:BC], ALU.add))
            nc.vector.tensor_copy(last_row[:, :], row_f[:, :])
            nc.vector.tensor_scalar_add(node_half[:, :], node_id[:, :], 0.5)
            dve_chain.close(ch.n)
    c["pool_setup"].close(4)
    c["pe_setup"].close(9)
    c["dve_setup"].close(1)
    c["x_turned_out"].close(4)
    c["normed_turned"].close(4)

    found = sb("found", [NP, 2, WB, 2 * TE], at=work)
    found_junk = sb("found_junk", [NP, 3, TE], at=work)
    tally = sb("tally", [NP, 3, NW], at=work)
    edge_end = sb("edge_end", [NP, NW], at=work)
    tmp_n = sb("tmp_n", [NP, NW], at=work)
    held = sb("held", [NP, 1], at=work)
    spare = sb("spare_rows", [NP, NW], at=work)
    before = sb("before", [NP, NP], at=work)
    tile_buf = sb("tile_buf", [NP, 2, WB], I32, at=work)
    with nc.Block() as block:
        @block.gpsimd
        def _(pool):
            ch = Chain(pool, pool_chain)
            ch.link(nc.gpsimd.memset(before[:, :], 1.0))
            nc.gpsimd.iota(spare[:, :], pattern=[[1, NW]], base=NCH * TE * TE, channel_multiplier=NW,
                           allow_small_or_imprecise_dtypes=True)
            nc.gpsimd.affine_select(out=before[:, :], in_=before[:, :], compare_op=ALU.is_gt, fill=0.0, base=0,
                                    pattern=[[1, NP]], channel_multiplier=-1).then_inc(c["pool_setup"].sem, 1)
            pool_chain.close(ch.n)
            with pool.Fori(0, NPAIR) as i:
                for s in range(2):
                    pool.wait_ge(idx_ready[s].sem, idx_ready[s].at(i + 1))
                    pool.sem_inc(pause.sem, 1)
                    for j in range(WB):
                        nc.gpsimd.indirect_dma_start(found[:, s, j, :], None, keys, bass.IndirectOffsetOnAxis(
                            ap=tile_buf[:, s, j:j + 1], axis=0)).then_inc(gathered[s].sem, 16)

        @block.scalar
        def _(act):
            with act.Fori(0, NPAIR) as i:
                for s in range(2):
                    for j in range(DVE_WINDOWS, WB):
                        w = bass.ds((2 * i + s) * WB + j, 1)
                        ins = nc.scalar.activation(bank(4, 4)[0:NP, 0:NT], first_bc[0:NP, :], ACT.Sign, bias=node_half[:, w],
                                                   scale=-1.0, accum_out=tiles_at[:, w]).then_inc(act_chain.sem, 1)
                        act.wait_ge(act_chain.sem, act_chain.at((2 * i + s) * (WB - DVE_WINDOWS) + j - DVE_WINDOWS + 1))
                    act.sem_inc(half_searched.sem, 1)

        @block.vector
        def _(dve):
            search_chain, found_chain = stage_chains

            def search(i, s):
                n = 2 * i + s
                for j in range(DVE_WINDOWS):
                    w = bass.ds(n * WB + j, 1)
                    nc.vector.tensor_scalar(junk[0:NP, :], first_bc[0:NP, :], node_id[:, w], 0.0, ALU.is_le,
                                            ALU.add, accum_out=tiles_at[:, w]).then_inc(search_chain.sem, 1)
                    dve.wait_ge(search_chain.sem, search_chain.at((DVE_WINDOWS + 2) * n + j + 1))
                other = bass.ds(n * WB + DVE_WINDOWS, WB - DVE_WINDOWS)
                dve.wait_ge(half_searched.sem, half_searched.at(n + 1))
                dve.sem_inc(pause.sem, 1)
                nc.vector.tensor_scalar(tiles_at[:, other], tiles_at[:, other], float(NT), 0.5, ALU.add, ALU.mult
                                        ).then_inc(search_chain.sem, 1)
                dve.wait_ge(search_chain.sem, search_chain.at((DVE_WINDOWS + 2) * n + DVE_WINDOWS + 1))
                both = bass.ds(n * WB, WB)
                nc.vector.tensor_scalar(tile_f[:, both], tiles_at[:, both], -1.0, 0.0, ALU.add, ALU.max
                                        ).then_inc(search_chain.sem, 1)
                dve.wait_ge(search_chain.sem, search_chain.at((DVE_WINDOWS + 2) * (n + 1)))
                dve.sem_inc(pause.sem, 1)
                nc.vector.tensor_copy(tile_buf[:, s, :], tile_f[:, both]).then_inc(idx_ready[s].sem, 1)

            def compare(i, s):
                n = 2 * i + s
                dve.wait_ge(gathered[s].sem, gathered[s].at(16 * WB * (i + 1)))
                for j in range(WB):
                    w = bass.ds(n * WB + j, 1)
                    for k, (half, op) in enumerate(((0, ALU.is_le), (0, ALU.is_equal), (1, ALU.is_le))):
                        ins = nc.vector.tensor_scalar(found_junk[:, k, :], found[:, s, j, half * TE:(half + 1) * TE],
                                                      node_id[:, w], 0.0, op, ALU.add, accum_out=tally[:, k, w])
                    ins.then_inc(found_chain.sem, 1)
                    dve.wait_ge(found_chain.sem, found_chain.at(n * WB + j + 1))

            search(0, 0)
            with dve.Fori(0, NPAIR - 1) as i:
                search(i, 1)
                compare(i, 0)
                search(i + 1, 0)
                compare(i, 1)
            search(NPAIR - 1, 1)
            compare(NPAIR - 1, 0)
            compare(NPAIR - 1, 1)
            search_chain.close((DVE_WINDOWS + 2) * 2 * NPAIR)
            found_chain.close(NW)
            ch = Chain(dve, dve_chain)
            ch.link(nc.vector.tensor_scalar(tmp_n[:, :], tally[:, 0, :], -1.0, float(NT), ALU.add, ALU.mult))
            ch.link(nc.vector.tensor_tensor(tmp_n[:, :], tmp_n[:, :], tile_f[:, :], ALU.add))
            ch.link(nc.vector.scalar_tensor_tensor(tmp_n[:, :], tmp_n[:, :], -float(ZERO_ROW), tally[:, 1, :],
                                                   ALU.add, ALU.mult))
            ch.link(nc.vector.tensor_scalar_add(tmp_n[:, :], tmp_n[:, :], float(ZERO_ROW)))
            nc.vector.memset(node_row[:, NW:NW + 2 * WB], 0)
            ch.link(nc.vector.tensor_copy(node_row[:, 0:NW], tmp_n[:, :]))
            ch.link(nc.vector.tensor_tensor_scan(tmp_n[:, :], tally[:, 1, :], zeros[0:NP, 0:NW], 0.0, ALU.add, ALU.add))
            nc.vector.tensor_copy(held[:, :], tmp_n[:, NW - 1:NW]).then_inc(c["x_turned_out"].sem, 1)
            dve.wait_ge(c["x_turned"].sem, c["x_turned"].at(1))
            ch.link(nc.vector.tensor_copy(held[:, :], bank(0)[0:NP, 0:1]))
            ch.link(nc.vector.tensor_tensor(tmp_n[:, :], tmp_n[:, :], tally[:, 1, :], ALU.subtract))
            ch.link(nc.vector.tensor_scalar(tmp_n[:, :], tmp_n[:, :], held[:, 0:1], -PAD_PLACE, ALU.add, ALU.add))
            ch.link(nc.vector.tensor_tensor(tmp_n[:, :], tmp_n[:, :], tally[:, 1, :], ALU.mult))
            ch.link(nc.vector.tensor_scalar_add(tmp_n[:, :], tmp_n[:, :], PAD_PLACE))
            nc.vector.memset(place[:, NW:NW + 2 * WB], 0)
            ch.link(nc.vector.tensor_copy(place[:, 0:NW], tmp_n[:, :]))
            ch.link(nc.vector.scalar_tensor_tensor(edge_end[:, :], tile_f[:, :], float(TE), tally[:, 2, :],
                                                   ALU.mult, ALU.add))
            nc.vector.tensor_copy(first_edge[:, 1:NW], edge_end[:, 0:NW - 1]).then_inc(c["dve_setup"].sem, 1)
            dve.wait_ge(setup_dma.sem, setup_dma.at(48))
            ch.link(nc.vector.tensor_tensor(degree[:, :], edge_end[:, :], first_edge[:, :], ALU.subtract))
            ch.link(nc.vector.tensor_scalar_add(tmp_n[:, :], degree[:, :], 1.0))
            ch.link(nc.vector.reciprocal(dinv[:, :], tmp_n[:, :]))
            dve_chain.close(ch.n)

        @block.tensor
        def _(pe):
            pe.wait_ge(c["pool_setup"].sem, c["pool_setup"].at(1))
            pe.wait_ge(c["x_turned_out"].sem, c["x_turned_out"].at(1))
            nc.tensor.matmul(bank(0)[0:NP, 0:1], before[:, :], held[:, :], start=True, stop=True
                             ).then_inc(c["x_turned"].sem, 1)

        @block.sync
        def _(sp):
            sp.dma_start(edge_before[0:1, :], zeros[0:1, 0:1]).then_inc(setup_dma.sem, 16)
            for n, k in enumerate((*stored, *tab_stored)):
                sp.dma_start(primed[n:n + 1, :], zeros[0:1, 0:1]).then_inc(k.sem, 16)
                k.close(16)
                sp.wait_ge(k.sem, k.at(0))
            sp.wait_ge(c["dve_setup"].sem, c["dve_setup"].at(1))
            sp.dma_start(edge_before[1:NP + 1, :], edge_end[:, NW - 1:NW], allow_slow_non_contiguous=True
                         ).then_inc(setup_dma.sem, 16)
            sp.wait_ge(setup_dma.sem, setup_dma.at(32))
            sp.dma_start(first_edge[:, 0:1], edge_before[0:NP, :], allow_slow_non_contiguous=True
                         ).then_inc(setup_dma.sem, 16)
            sp.wait_ge(setup_dma.sem, setup_dma.at(48))
            sp.wait_ge(loaded[0].sem, loaded[0].at(16 * (NACCS // 2)))

    loaded[0].close(16 * (NACCS // 2))
    with nc.Block() as block:
        @block.scalar
        def _(act):
            nc.scalar.activation(dinv[:, :], dinv[:, :], ACT.Sqrt)

        @block.vector
        def _(dve):
            ch = Chain(dve, dve_chain)
            ch.link(nc.vector.tensor_scalar(tmp_n[:, :], degree[:, :], 0.5, None, ALU.is_gt))
            ch.link(nc.vector.tensor_tensor(tile_f[:, :], first_edge[:, :], spare[:, :], ALU.subtract))
            ch.link(nc.vector.tensor_tensor(tile_f[:, :], tile_f[:, :], tmp_n[:, :], ALU.mult))
            ch.link(nc.vector.tensor_tensor(tile_f[:, :], tile_f[:, :], spare[:, :], ALU.add))
            nc.vector.tensor_copy(spot[:, :], tile_f[:, :])
            dve_chain.close(ch.n)
    act_chain.close(2 * NPAIR * (WB - DVE_WINDOWS))
    half_searched.close(2 * NPAIR)
    setup_dma.close(48)
    for k in ("dve_setup", "pool_setup", "x_turned", "x_turned_out"):
        c[k].close(1)
    for s in range(2):
        idx_ready[s].close(NPAIR)
        gathered[s].close(16 * WB * NPAIR)
    work.close()
    setup.close()

    def nodes(t):
        return t.rearrange("(p w) f -> p w f", p=NP)

    def rows(t, wide=F):
        return t[0:NP, :].unsqueeze(1).to_broadcast([NP, WB, wide])

    def by_window(t, i, s):
        return t[:, bass.ds(i * 2 * WB + s * WB, WB)].unsqueeze(2).to_broadcast([NP, WB, F])

    def node_table(kind, x_in, tab_in, tab_out):
        buf = ExitStack()
        messages = kind == "L0 messages"
        key = "L0m" if messages else kind
        rows_in = sb(key + "_in", [NP, 2, WB, F], at=buf)
        agg = sb(key + "_agg", [NP, 2, WB, F], at=buf)
        turned = sb(key + "_turned", [F, WB, NP], at=buf)
        tab = sb(key + "_tab", [NP, 2, WB, F], at=buf)
        pT = bank(0, 3)[:, 0:WB * 128].rearrange("p (w n) -> p w n", w=WB)
        pM = bank(3, 3)[:, 0:WB * 128].rearrange("p (w n) -> p w n", w=WB)

        def window(i, s):
            return bass.ds(i * 2 * WB + s * WB, WB)

        with nc.Block() as block:
            @block.sync
            def _(sp):
                def load(i, s):
                    sp.dma_start(rows_in[:, s, :, :], nodes(x_in if messages else tab_in)[:, window(i, s), :]
                                 ).then_inc(loaded[s].sem, 16)

                def store(i, s):
                    if not messages:
                        sp.wait_ge(c["table_out"].sem, c["table_out"].at(2 * i + s + 1))
                        sp.dma_start(nodes(tab_out)[:, window(i, s), :], tab[:, s, :, :]).then_inc(tab_stored[s].sem, 16)

                load(0, 0)
                load(0, 1)
                with sp.Fori(0, NPAIR - 1) as i:
                    for s in range(2):
                        store(i, s)
                        sp.wait_ge(c["batch_done"].sem, c["batch_done"].at(2 * i + s + 1))
                        load(i + 1, s)
                store(NPAIR - 1, 0)
                store(NPAIR - 1, 1)
                if not messages:
                    for s in range(2):
                        sp.wait_ge(tab_stored[s].sem, tab_stored[s].at(16 * NPAIR))

            @block.gpsimd
            def _(pool):
                with pool.Fori(0, NPAIR) as i:
                    for s in range(2):
                        pool.wait_ge(idx_ready[s].sem, idx_ready[s].at(i + 1))
                        if messages:
                            pool.wait_ge(c["table_out"].sem, c["table_out"].at(2 * i + s + 1))
                        pool.sem_inc(pause.sem, 1)
                        for j in range(WB):
                            at = bass.IndirectOffsetOnAxis(ap=row_buf[:, s, j:j + 1], axis=0)
                            if messages:
                                ins = nc.gpsimd.indirect_dma_start(by_run, at, tab[:, s, j, :], None,
                                                                   bounds_check=NACC - 1, oob_is_err=False)
                            else:
                                ins = nc.gpsimd.indirect_dma_start(agg[:, s, j, :], None, runs, at)
                            ins.then_inc(gathered[s].sem, 16)
                if messages:
                    for s in range(2):
                        pool.wait_ge(gathered[s].sem, gathered[s].at(16 * WB * NPAIR))

            @block.tensor
            def _(pe):
                with pe.Fori(0, NPAIR) as i:
                    for s in range(2):
                        n = 2 * i + s
                        if messages:
                            pe.wait_ge(loaded[s].sem, loaded[s].at(16 * (i + 1)))
                            source = rows_in
                        else:
                            pe.wait_ge(c["agg_scaled"].sem, c["agg_scaled"].at(n + 1))
                            source = agg
                        for j in range(WB):
                            ins = nc.tensor.transpose(pT[:, j, 0:NP], source[:, s, j, :], ident[0:NP, 0:NP])
                        ins.then_inc(c["x_turned"].sem, 1)
                        pe.wait_ge(c["x_turned_out"].sem, c["x_turned_out"].at(n + 1))
                        pe.wait_ge(c["product_out"].sem, c["product_out"].at(n))
                        for j in range(WB):
                            ins = nc.tensor.matmul(pM[0:NP, j, :], turned[:, j, :], m["W1" if messages else "gcn_W2"][:, :],
                                                   start=True, stop=True)
                        ins.then_inc(c["table_product"].sem, 1)

            @block.scalar
            def _(act):
                clears = NACCS - NACCS // 2 + 1
                if messages:
                    rest = NCH * TE * H // TE
                    for k in range(NACCS // 2, NACCS):
                        act.dma_start(acc[k].rearrange("(p b) f -> p b f", p=128),
                                      zeros[:, :].unsqueeze(1).to_broadcast([128, NACC // 128, AW])).then_inc(window_in[0].sem, 16)
                    act.dma_start(kd_edge[0:NCH * TE * TE, :].rearrange("(p a e) h -> p a (e h)", p=128, a=rest),
                                  zeros[:, 0:TE].unsqueeze(1).to_broadcast([128, rest, TE])).then_inc(window_in[0].sem, 16)
                with act.Fori(0, NPAIR) as i:
                    for s in range(2):
                        n = 2 * i + s
                        act.wait_ge(c["x_turned"].sem, c["x_turned"].at(n + 1))
                        act.wait_ge(c["table_product"].sem, c["table_product"].at(n))
                        if messages:
                            ins = nc.scalar.activation(turned[:, :, :], pT[:, :, 0:NP], ACT.Identity, bias=bn1_shift[:, 0:1],
                                                       scale=bn1_scale[:, 0:1])
                        else:
                            ins = nc.scalar.activation(turned[:, :, :], pT[:, :, 0:NP], ACT.Relu, bias=m["gcn_b1"][:, 0:1])
                        ins.then_inc(c["x_turned_out"].sem, 1)
                        if messages:
                            act.wait_ge(c["product_out"].sem, c["product_out"].at(n + 1))
                            nc.scalar.activation(tab[:, s, :, :], tab[:, s, :, :], ACT.Gelu).then_inc(c["table_out"].sem, 1)
                if messages:
                    window_in[0].close(16 * clears)
                    act.wait_ge(window_in[0].sem, window_in[0].at(0))

            @block.vector
            def _(dve):
                if not messages:
                    for s in range(2):
                        nc.vector.tensor_copy(row_buf[:, s, :], node_row[:, s * WB:(s + 1) * WB]).then_inc(idx_ready[s].sem, 1)
                with dve.Fori(0, NPAIR) as i:
                    for s in range(2):
                        n = 2 * i + s
                        dve.wait_ge(gathered[s].sem, gathered[s].at(16 * WB * (i if messages else i + 1)))
                        if messages:
                            dve.sem_inc(pause.sem, 1)
                            nc.vector.tensor_copy(row_buf[:, s, :], place[:, window(i, s)]).then_inc(idx_ready[s].sem, 1)
                        else:
                            dve.wait_ge(loaded[s].sem, loaded[s].at(16 * (i + 1)))
                            ch = Chain(dve, dve_chain, 1, n)
                            ch.link(nc.vector.tensor_tensor(agg[:, s, :, :], agg[:, s, :, :], rows_in[:, s, :, :], ALU.add))
                            nc.vector.tensor_tensor(agg[:, s, :, :], agg[:, s, :, :], by_window(dinv, i, s), ALU.mult
                                                    ).then_inc(c["agg_scaled"].sem, 1)
                        dve.wait_ge(c["table_product"].sem, c["table_product"].at(n + 1))
                        if messages:
                            nc.vector.tensor_tensor(tab[:, s, :, :], pM[0:NP, :, :], rows(m["b1_rows"]), ALU.add
                                                    ).then_inc(c["product_out"].sem, 1)
                        else:
                            dve.wait_ge(tab_stored[s].sem, tab_stored[s].at(16 * i))
                            nc.vector.tensor_tensor(tab[:, s, :, :], pM[0:NP, :, :], by_window(dinv, i, s), ALU.mult
                                                    ).then_inc(c["product_out"].sem, 1)
                            ahead = bass.ds((i * 2 + 2) * WB + s * WB, WB)
                            nc.vector.tensor_copy(row_buf[:, s, :], node_row[:, ahead]).then_inc(idx_ready[s].sem, 1)
                            dve.wait_ge(c["product_out"].sem, c["product_out"].at(n + 1))
                            dve.sem_inc(c["table_out"].sem, 1)
                        dve.sem_inc(c["batch_done"].sem, 1)
        buf.close()
        n = 2 * NPAIR
        for s in range(2):
            gathered[s].close(16 * WB * NPAIR)
            idx_ready[s].close(NPAIR + (not messages))
            loaded[s].close(16 * NPAIR)
            tab_stored[s].close(16 * NPAIR * (not messages))
        for k in ["batch_done", "x_turned", "x_turned_out", "product_out", "table_product", "table_out"]:
            c[k].close(n)
        if not messages:
            c["agg_scaled"].close(n)
            dve_chain.close(n)

    def node_layer(kind, x_in, x_out, tab_in, tab_out):
        buf = ExitStack()
        has_agg, has_own = kind != "L0", kind == "L2b"
        has_product, has_table = kind != "L2b", kind != "L3"
        wide = RW if kind == "L3" else F
        run_rows = runs3 if kind == "L3" else runs
        xb = sb(kind + "_xb", [NP, 2, WB, F], at=buf)
        agg = sb(kind + "_agg", [NP, 2, WB, wide], at=buf)
        own = sb(kind + "_own", [NP, 2, WB, F], at=buf) if has_own else None
        res = sb(kind + "_res", [NP, 2, WB, F], at=buf)
        nx = sb(kind + "_nx", [NP, 2, WB, F], at=buf)
        stats = sb(kind + "_stats", [NP, WB, 6], at=buf)
        mv = sb(kind + "_mv", [NP, WB, 2], at=buf)
        std = sb(kind + "_std", [NP, WB], at=buf)
        turned = sb(kind + "_turned", [F, 2, WB, NP], at=buf)
        tab = sb(kind + "_tab", [NP, 2, WB, TW if kind == "L2b" else F], at=buf) if has_table else None
        parts = sb(kind + "_parts", [NP, 2, NACCS, WB, AW], at=buf) if kind == "L0" else None
        shared = sb(kind + "_shared", [NP, WB], at=buf)
        kd_buf = sb(kind + "_kd", [NP, 2, WB, H], at=buf)
        spot_buf = sb(kind + "_spot", [NP, 2, WB], I32, at=buf)
        fac = sb(kind + "_fac", [NP, WB, 3 * H], at=buf)
        pT = bank(0, 3)[:, 0:WB * 128].rearrange("p (w n) -> p w n", w=WB)
        pM = bank(3, 3)[:, 0:WB * 128].rearrange("p (w n) -> p w n", w=WB)
        pS = bank(6, 1)[:, 0:WB * 20].rearrange("p (w n) -> p w n", w=WB)
        n_loads = 16 * (1 + has_own)
        LAST = NPAIR - 1
        update_chain, norm_chain = stage_chains
        per_update = {"L0": 3, "L1": 1, "L2b": 3, "L3": 5}[kind]
        per_norm = {"L0": 3, "L1": 2, "L2b": 3, "L3": 2}[kind]

        def window(i, s):
            return bass.ds(i * 2 * WB + s * WB, WB)

        def steps(eng, step):
            step(0, 0, None, (0, 1))
            step(0, 1, (0, 0), (1, 0))
            with eng.Fori(1, LAST) as i:
                step(i, 0, (i - 1, 1), (i, 1))
                step(i, 1, (i, 0), (i + 1, 0))
            step(LAST, 0, (LAST - 1, 1), (LAST, 1))
            step(LAST, 1, (LAST, 0), None)

        with nc.Block() as block:
            @block.sync
            def _(sp):
                def load(i, s):
                    sp.dma_start(xb[:, s, :, :], nodes(x_in)[:, window(i, s), :]).then_inc(loaded[s].sem, 16)
                    if has_own:
                        sp.dma_start(own[:, s, :, :], nodes(tab_in)[:, window(i, s), :]).then_inc(loaded[s].sem, 16)

                def load_parts(i, s):
                    for k in range(NACCS):
                        sp.dma_start(parts[:, s, k, :, :], nodes(acc[k][0:N, :])[:, window(i, s), :]
                                     ).then_inc(window_in[s].sem, 16)

                def store_table(i, s):
                    sp.wait_ge(c["table_out"].sem, c["table_out"].at(2 * i + s + 1))
                    sp.dma_start(nodes(tab_out)[:, window(i, s), :], tab[:, s, :, :]).then_inc(tab_stored[s].sem, 16)

                def step(i, s, before, after):
                    n = 2 * i + s
                    ends = isinstance(i, int) and i == LAST
                    if kind == "L0" and not ends:
                        sp.wait_ge(c["agg_scaled"].sem, c["agg_scaled"].at(n + 1))
                        load_parts(i + 1, s)
                    if before and has_table:
                        store_table(*before)
                    if not ends:
                        sp.wait_ge(c["batch_done"].sem, c["batch_done"].at(n + 1))
                        load(i + 1, s)
                    sp.wait_ge(c["normed"].sem, c["normed"].at(n + 1))
                    sp.dma_start(nodes(x_out)[:, window(i, s), :], nx[:, s, :, :]).then_inc(stored[s].sem, 16)
                    if not after and has_table:
                        store_table(i, s)

                for s in range(2):
                    load(0, s)
                    if kind == "L0":
                        load_parts(0, s)
                steps(sp, step)
                for s in range(2):
                    sp.wait_ge(stored[s].sem, stored[s].at(16 * NPAIR))
                    if has_table:
                        sp.wait_ge(tab_stored[s].sem, tab_stored[s].at(16 * NPAIR))

            if has_agg:
                @block.gpsimd
                def _(pool):
                    def gather(i, s):
                        pool.wait_ge(idx_ready[s].sem, idx_ready[s].at(i + 1))
                        pool.sem_inc(pause.sem, 1)
                        for j in range(WB):
                            nc.gpsimd.indirect_dma_start(
                                agg[:, s, j, :], None, run_rows,
                                bass.IndirectOffsetOnAxis(ap=row_buf[:, s, j:j + 1], axis=0)
                            ).then_inc(gathered[s].sem, 16)

                    def scatter_kd(i, s):
                        pool.wait_ge(idx_ready[2 + s].sem, idx_ready[2 + s].at(i + 1))
                        pool.sem_inc(pause.sem, 1)
                        for j in range(WB):
                            nc.gpsimd.indirect_dma_start(
                                kd_edge, bass.IndirectOffsetOnAxis(ap=spot_buf[:, s, j:j + 1], axis=0),
                                kd_buf[:, s, j, :], None).then_inc(gathered[2 + s].sem, 16)

                    if kind != "L2b":
                        with pool.Fori(0, NPAIR) as i:
                            gather(i, 0)
                            gather(i, 1)
                    else:
                        for i in range(2):
                            gather(i, 0)
                            gather(i, 1)
                        with pool.Fori(2, NPAIR) as i:
                            for s in range(2):
                                gather(i, s)
                                scatter_kd(i - 2, s)
                        for i in range(NPAIR - 2, NPAIR):
                            scatter_kd(i, 0)
                            scatter_kd(i, 1)
                        for s in range(2):
                            pool.wait_ge(gathered[2 + s].sem, gathered[2 + s].at(16 * WB * NPAIR))

            @block.tensor
            def _(pe):
                def turn(source, s, done):
                    for j in range(WB):
                        ins = nc.tensor.transpose(pT[:, j, 0:NP], source[:, s, j, 0:F], ident[0:NP, 0:NP])
                    ins.then_inc(c[done].sem, 1)

                def update(i, s):
                    n = 2 * i + s
                    if kind == "L0":
                        pe.wait_ge(loaded[s].sem, loaded[s].at(n_loads * (i + 1)))
                        turn(xb, s, "x_turned")
                        pe.wait_ge(c["x_turned_out"].sem, c["x_turned_out"].at(n + 1))
                    if kind == "L1":
                        pe.wait_ge(gathered[s].sem, gathered[s].at(16 * WB * (i + 1)))
                    else:
                        pe.wait_ge(c["agg_scaled"].sem, c["agg_scaled"].at(n + 1))
                    pe.sem_inc(pause.sem, 1)
                    turn(agg, s, "agg_turned")
                    pe.wait_ge(c["agg_turned_out"].sem, c["agg_turned_out"].at(n + 1))
                    wait(pe, c["product_out"], n)
                    if has_table:
                        wait(pe, c["table_out"], n - 1)
                    pe.sem_inc(pause.sem, 1)
                    w = {"L0": None, "L1": m["Wn2"], "L3": m["Wout"]}[kind]
                    for j in range(WB):
                        if kind == "L0":
                            nc.tensor.matmul(pM[0:NP, j, :], turned[:, 0, j, :], m["W2"][:, 0, :], start=True, stop=False)
                            ins = nc.tensor.matmul(pM[0:NP, j, :], turned[:, 1, j, :], m["W2"][:, 1, :], start=False, stop=True)
                        else:
                            ins = nc.tensor.matmul(pM[0:NP, j, :], turned[:, 1, j, :], w[:, :], start=True, stop=True)
                    ins.then_inc(c["product"].sem, 1)

                def table(i, s, after):
                    n = 2 * i + s
                    pe.wait_ge(c["normed"].sem, c["normed"].at(n + 1))
                    pe.sem_inc(pause.sem, 1)
                    turn(nx, s, "normed_turned")
                    pe.wait_ge(c["normed_turned_out"].sem, c["normed_turned_out"].at(n + 1))
                    if has_product:
                        pe.wait_ge(c["product_out"].sem, c["product_out"].at(n + 2 if after else n + 1))
                    else:
                        wait(pe, c["table_out"], n)
                    pe.sem_inc(pause.sem, 1)
                    w = {"L0": m["Wn1"][:, 0, :], "L1": m["gcn_W1"][:, :], "L2b": m["Wv"][:, :]}[kind]
                    for j in range(WB):
                        ins = nc.tensor.matmul(pM[0:NP, j, :], turned[:, 0, j, :], w, start=True, stop=True)
                        if kind == "L2b":
                            ins = nc.tensor.matmul(pS[0:NP, j, :], turned[:, 0, j, :], score_w[:, :], start=True, stop=True)
                    ins.then_inc(c["table_product"].sem, 1)

                def step(i, s, before, after):
                    if has_product and not before:
                        update(i, s)
                    if has_product and after:
                        update(*after)
                    if has_table:
                        table(i, s, after)

                steps(pe, step)

            @block.scalar
            def _(act):
                def update(i, s):
                    n = 2 * i + s
                    if kind == "L3":
                        act.wait_ge(c["exponent"].sem, c["exponent"].at(n + 1))
                        nc.scalar.activation(fac[:, :, H:2 * H], fac[:, :, H:2 * H], ACT.Exp).then_inc(c["exponent_out"].sem, 1)
                    if kind == "L0":
                        act.wait_ge(c["x_turned"].sem, c["x_turned"].at(n + 1))
                        nc.scalar.activation(turned[:, 0, :, :], pT[:, :, 0:NP], ACT.Identity, bias=bn2_shift[:, 0:1],
                                             scale=bn2_scale[:, 0:1]).then_inc(c["x_turned_out"].sem, 1)
                    act.wait_ge(c["agg_turned"].sem, c["agg_turned"].at(n + 1))
                    if kind == "L0":
                        nc.scalar.activation(turned[:, 1, :, :], pT[:, :, 0:NP], ACT.Identity, bias=bn2_shift[:, 1:2],
                                             scale=bn2_scale[:, 1:2]).then_inc(c["agg_turned_out"].sem, 1)
                    else:
                        nc.scalar.activation(turned[:, 1, :, :], pT[:, :, 0:NP], ACT.Copy).then_inc(c["agg_turned_out"].sem, 1)

                def step(i, s, before, after):
                    n = 2 * i + s
                    if has_product and not before:
                        update(i, s)
                    if kind in ("L0", "L2b"):
                        act.wait_ge(c["product_out"].sem, c["product_out"].at(n + 1))
                        nc.scalar.activation(res[:, s, :, :], res[:, s, :, :], ACT.Gelu if kind == "L0" else ACT.Relu
                                             ).then_inc(c["activated"].sem, 1)
                    if has_product and after:
                        update(*after)
                    act.wait_ge(c["variance"].sem, c["variance"].at(n + 1))
                    nc.scalar.activation(std[:, :], mv[:, :, 1], ACT.Sqrt, bias=eps_ln[0:NP, :]).then_inc(c["deviation"].sem, 1)
                    if has_table:
                        act.wait_ge(c["normed_turned"].sem, c["normed_turned"].at(n + 1))
                        nc.scalar.activation(turned[:, 0, :, :], pT[:, :, 0:NP], ACT.Copy).then_inc(c["normed_turned_out"].sem, 1)

                steps(act, step)

            @block.vector
            def _(dve):
                def next_rows(i, s):
                    ahead = bass.ds((i * 2 + 2 + s) * WB, WB)
                    nc.vector.tensor_copy(row_buf[:, s, :], node_row[:, ahead]).then_inc(idx_ready[s].sem, 1)

                def update(i, s):
                    n = 2 * i + s
                    ch = Chain(dve, update_chain, per_update, n)
                    wait(dve, c["normed"], n - 1)
                    if has_agg:
                        dve.wait_ge(gathered[s].sem, gathered[s].at(16 * WB * (i + 1)))
                        dve.wait_ge(loaded[s].sem, loaded[s].at(n_loads * (i + 1)))
                    else:
                        dve.wait_ge(window_in[s].sem, window_in[s].at(16 * NACCS * (i + 1)))
                    dve.sem_inc(pause.sem, 1)
                    if kind == "L0":
                        whole = parts[:, s, :, :, :].rearrange("p k w f -> p k (w f)")
                        ch.link(nc.vector.tensor_tensor(whole[:, 0:2, :], whole[:, 0:2, :], whole[:, 2:4, :], ALU.add))
                        ch.link(nc.vector.tensor_tensor(whole[:, 0, :], whole[:, 0, :], whole[:, 1, :], ALU.add))
                        ch.link(nc.vector.tensor_scalar(shared[:, :], parts[:, s, 0, :, F], 1.0, None, ALU.max))
                        nc.vector.reciprocal(shared[:, :], shared[:, :]).then_inc(c["exponent"].sem, 1)
                        dve.wait_ge(c["exponent"].sem, c["exponent"].at(n + 1))
                        nc.vector.tensor_tensor(agg[:, s, :, :], parts[:, s, 0, :, 0:F],
                                                shared[:, :].unsqueeze(2).to_broadcast([NP, WB, F]), ALU.mult
                                                ).then_inc(c["agg_scaled"].sem, 1)
                    if kind == "L1":
                        ch.link(nc.vector.tensor_tensor(res[:, s, :, :], by_window(degree, i, s), rows(m["nb2_rows"]), ALU.mult))
                        nc.vector.scalar_tensor_tensor(res[:, s, :, :], xb[:, s, :, :], 2.0, res[:, s, :, :], ALU.mult, ALU.add
                                                       ).then_inc(c["batch_done"].sem, 1)
                    if kind == "L2b":
                        ch.link(nc.vector.tensor_tensor(res[:, s, :, :], agg[:, s, :, :], own[:, s, :, :], ALU.add))
                        next_rows(i, s)
                        ch.link(nc.vector.tensor_tensor(res[:, s, :, :], res[:, s, :, :], by_window(dinv, i, s), ALU.mult))
                        ch.link(nc.vector.tensor_tensor(res[:, s, :, :], res[:, s, :, :], rows(m["gcn_b2_rows"]), ALU.add))
                        nc.vector.tensor_tensor(res[:, s, :, :], res[:, s, :, :], xb[:, s, :, :], ALU.add
                                                ).then_inc(c["product_out"].sem, 1)
                    if kind == "L3":
                        top, f, den = fac[:, :, 0:H], fac[:, :, H:2 * H], fac[:, :, 2 * H:3 * H]
                        got_m, got_d = agg[:, s, :, F + H:F + 2 * H], agg[:, s, :, F:F + H]
                        ch.link(nc.vector.tensor_scalar(top, got_m, MAX_FLOOR, None, ALU.max))
                        nc.vector.tensor_tensor(f, got_m, top, ALU.subtract).then_inc(c["exponent"].sem, 1)
                        nc.vector.tensor_tensor(res[:, s, :, :], xb[:, s, :, :], rows(m["bout_rows"]), ALU.add
                                                ).then_inc(c["batch_done"].sem, 1)
                        dve.wait_ge(c["exponent_out"].sem, c["exponent_out"].at(n + 1))
                        ch.link(nc.vector.tensor_tensor(den, got_d, f, ALU.mult))
                        ch.link(nc.vector.tensor_scalar_add(den, den, DEN_EPS))
                        ch.link(nc.vector.reciprocal(den, den))
                        ch.link(nc.vector.tensor_tensor(f, f, den, ALU.mult))
                        for j in range(WB):
                            hj = agg[:, s, j, 0:F].rearrange("p (h d) -> p h d", h=H)
                            ins = nc.vector.tensor_tensor(hj, hj, fac[:, j, H:2 * H].unsqueeze(2).to_broadcast([NP, H, HD]), ALU.mult)
                        ins.then_inc(c["agg_scaled"].sem, 1)
                    assert ch.n == per_update, (kind, ch.n)

                def add_product(i, s):
                    n = 2 * i + s
                    dve.wait_ge(c["product"].sem, c["product"].at(n + 1))
                    if kind == "L0":
                        ins = nc.vector.tensor_tensor(res[:, s, :, :], pM[0:NP, :, :], rows(m["b2_rows"]), ALU.add)
                    else:
                        if kind == "L1":
                            dve.wait_ge(c["batch_done"].sem, c["batch_done"].at(n + 1))
                        dve.sem_inc(pause.sem, 1)
                        ins = nc.vector.tensor_tensor(res[:, s, :, :], res[:, s, :, :], pM[0:NP, :, :], ALU.add)
                    ins.then_inc(c["product_out"].sem, 1)
                    dve.wait_ge(c["product_out"].sem, c["product_out"].at(n + 1))
                    if has_agg:
                        next_rows(i, s)

                def norm(i, s):
                    n = 2 * i + s
                    ch = Chain(dve, norm_chain, per_norm, n)
                    if kind in ("L0", "L2b"):
                        dve.wait_ge(c["activated"].sem, c["activated"].at(n + 1))
                        if kind == "L0":
                            dve.wait_ge(loaded[s].sem, loaded[s].at(n_loads * (i + 1)))
                        dve.sem_inc(pause.sem, 1)
                        ch.link(nc.vector.tensor_tensor(res[:, s, :, :], res[:, s, :, :], xb[:, s, :, :], ALU.add))
                        dve.sem_inc(c["batch_done"].sem, 1)
                    for j in range(WB):
                        ins = nc.vector.bn_stats(stats[:, j, :], res[:, s, j, :])
                    ch.link(ins)
                    dve.sem_inc(pause.sem, 1)
                    for j in range(WB):
                        ins = nc.vector.bn_aggr(mv[:, j, :], stats[:, j, :])
                    ins.then_inc(c["variance"].sem, 1)
                    dve.wait_ge(c["deviation"].sem, c["deviation"].at(n + 1))
                    dve.wait_ge(stored[s].sem, stored[s].at(16 * i))
                    ch.link(nc.vector.reciprocal(std[:, :], std[:, :]))
                    for j in range(WB):
                        ins = nc.vector.tensor_scalar(nx[:, s, j, :], res[:, s, j, :], mv[:, j, 0:1], std[:, j:j + 1],
                                                      ALU.subtract, ALU.mult)
                    ins.then_inc(c["normed"].sem, 1)
                    assert ch.n == per_norm, (kind, ch.n)

                def table(i, s):
                    n = 2 * i + s
                    dve.wait_ge(c["table_product"].sem, c["table_product"].at(n + 1))
                    dve.wait_ge(tab_stored[s].sem, tab_stored[s].at(16 * i))
                    if kind == "L0":
                        ins = nc.vector.tensor_tensor(tab[:, s, :, :], pM[0:NP, :, :], rows(m["nb1_rows"]), ALU.add)
                    if kind == "L1":
                        ins = nc.vector.tensor_tensor(tab[:, s, :, :], pM[0:NP, :, :], by_window(dinv, i, s), ALU.mult)
                    if kind == "L2b":
                        dve.sem_inc(pause.sem, 1)
                        nc.vector.tensor_copy(tab[:, s, :, 0:F], pM[0:NP, :, :])
                        nc.vector.tensor_copy(kd_node[:, window(i, s), :], pS[0:NP, :, (1 + KINDS) * H:(2 + KINDS) * H])
                        dve.wait_ge(gathered[2 + s].sem, gathered[2 + s].at(16 * WB * i))
                        dve.sem_inc(pause.sem, 1)
                        nc.vector.tensor_copy(kd_buf[:, s, :, :], pS[0:NP, :, (1 + KINDS) * H:(2 + KINDS) * H])
                        nc.vector.tensor_copy(spot_buf[:, s, :], spot[:, window(i, s)]).then_inc(idx_ready[2 + s].sem, 1)
                        ins = nc.vector.tensor_copy(tab[:, s, :, F:TW], pS[0:NP, :, 0:(1 + KINDS) * H])
                    ins.then_inc(c["table_out"].sem, 1)

                def step(i, s, before, after):
                    if not before:
                        update(i, s)
                    if has_product:
                        add_product(i, s)
                    if after:
                        update(*after)
                    if before and has_table:
                        table(*before)
                    norm(i, s)
                    if not after and has_table:
                        table(i, s)

                if has_agg:
                    for s in range(2):
                        nc.vector.tensor_copy(row_buf[:, s, :], node_row[:, s * WB:(s + 1) * WB]).then_inc(idx_ready[s].sem, 1)
                steps(dve, step)
        buf.close()
        n = 2 * NPAIR
        for s in range(2):
            if has_agg:
                gathered[s].close(16 * WB * NPAIR)
                idx_ready[s].close(NPAIR + 1)
            if kind == "L2b":
                gathered[2 + s].close(16 * WB * NPAIR)
                idx_ready[2 + s].close(NPAIR)
            if not has_agg:
                window_in[s].close(16 * NACCS * NPAIR)
            loaded[s].close(n_loads * NPAIR)
            stored[s].close(16 * NPAIR)
            tab_stored[s].close(16 * NPAIR * has_table)
        ran = ["batch_done", "variance", "deviation", "normed"]
        ran += {"L0": ["x_turned", "x_turned_out", "agg_scaled", "activated", "exponent"], "L1": [], "L2b": ["activated"],
                "L3": ["exponent", "exponent_out", "agg_scaled"]}[kind]
        ran += ["agg_turned", "agg_turned_out", "product"] * has_product + ["product_out"]
        ran += ["normed_turned", "normed_turned_out", "table_product", "table_out"] * has_table
        for k in ran:
            c[k].close(n)
        update_chain.close(per_update * n)
        norm_chain.close(per_norm * n)

    run_view = runs.rearrange("(r t) f -> r t f", t=NT)

    def halves(i, s):
        return bass.ds((2 * i + s) * HB, HB)

    def edge_pass(name, tab_in):
        buf = ExitStack()
        got = sb(name + "_got", [TE, 2, HB, F], at=buf)
        onehot = sb(name + "_onehot", [TE, 2, HB, TE], at=buf)
        sums = sb(name + "_sums", [TE, 2, HB, F], at=buf)
        with nc.Block() as block:
            @block.gpsimd
            def _(pool):
                with pool.Fori(0, NPASS) as i:
                    for s in range(2):
                        pool.wait_ge(idx_ready[s].sem, idx_ready[s].at(i + 1))
                        pool.sem_inc(pause.sem, 1)
                        for t in range(HB):
                            nc.gpsimd.indirect_dma_start(got[:, s, t, :], None, tab_in, bass.IndirectOffsetOnAxis(
                                ap=idx_buf[:, s, t:t + 1], axis=0)).then_inc(gathered[s].sem, 16)

            @block.vector
            def _(dve):
                with dve.Fori(0, NPASS) as i:
                    for s in range(2):
                        dve.wait_ge(sums_ready[s].sem, sums_ready[s].at(4 * i))
                        dve.sem_inc(pause.sem, 1)
                        nc.vector.tensor_copy(idx_buf[:, s, :], src_T[:, halves(i, s)]).then_inc(idx_ready[s].sem, 1)
                        nc.vector.tensor_copy(rank_buf[:, s, :], rank_T[:, halves(i, s)]).then_inc(dve_chain.sem, 1)
                        dve.wait_ge(dve_chain.sem, dve_chain.at(2 * i + s + 1))
                        for t in range(HB):
                            ins = nc.vector.tensor_scalar(onehot[:, s, t, :], iota_run[:, :], rank_buf[:, s, t:t + 1],
                                                          None, ALU.is_equal)
                        ins.then_inc(onehot_ready[s].sem, 1)

            @block.tensor
            def _(pe):
                with pe.Fori(0, NPASS) as i:
                    for s in range(2):
                        pe.wait_ge(onehot_ready[s].sem, onehot_ready[s].at(i + 1))
                        pe.wait_ge(gathered[s].sem, gathered[s].at(16 * HB * (i + 1)))
                        pe.wait_ge(evacuated[s].sem, evacuated[s].at(4 * i))
                        for t in range(HB):
                            b = bank(4 * s + t // 4)
                            ins = nc.tensor.matmul(b[:, (t % 4) * F:(t % 4 + 1) * F], onehot[:, s, t, :], got[:, s, t, :],
                                                   start=True, stop=True)
                            if t % 4 == 3:
                                ins.then_inc(sums_ready[s].sem, 1)

            @block.scalar
            def _(act):
                with act.Fori(0, NPASS) as i:
                    for s in range(2):
                        act.wait_ge(stored[s].sem, stored[s].at(16 * i))
                        for q in range(4):
                            act.wait_ge(sums_ready[s].sem, sums_ready[s].at(4 * i + q + 1))
                            nc.scalar.activation(sums[:, s, 4 * q:4 * q + 4, :].rearrange("p t f -> p (t f)"),
                                                 bank(4 * s + q), ACT.Copy).then_inc(evacuated[s].sem, 1)

            @block.sync
            def _(sp):
                with sp.Fori(0, NPASS) as i:
                    for s in range(2):
                        sp.wait_ge(evacuated[s].sem, evacuated[s].at(4 * (i + 1)))
                        sp.dma_start(run_view[:, halves(i, s), :], sums[:, s, :, :]).then_inc(stored[s].sem, 16)
                for s in range(2):
                    sp.wait_ge(stored[s].sem, stored[s].at(16 * NPASS))
        for s in range(2):
            idx_ready[s].close(NPASS)
            onehot_ready[s].close(NPASS)
            gathered[s].close(16 * HB * NPASS)
            sums_ready[s].close(4 * NPASS)
            evacuated[s].close(4 * NPASS)
            stored[s].close(16 * NPASS)
        dve_chain.close(2 * NPASS)
        buf.close()

    def scatter_pass():
        buf = ExitStack()
        rows_in = sb("rows_in", [TE, 2, HB, AW], at=buf)
        onehot = sb("s_onehot", [TE, 2, HB, TE], BF16, at=buf)
        same = sb("same", [TE, 2, HB, TE], BF16, at=buf)
        earlier = sb("earlier", [TE, 2, HB, TE], BF16, at=buf)
        tri = sb("tri", [TE, TE], BF16, at=buf)
        ones_b = sb("ones_b", [TE, 1], BF16, at=buf)
        counts = sb("counts", [TE, 2, 4, TE], at=buf)
        to_add = sb("to_add", [TE, 2, HB, AW], at=buf)
        src_f = sb("src_f", [TE, 2, HB], at=buf)
        spread, spread_read, src_ready = c["ea_turned"], c["ea_out"], c["hid_ready"]
        spare = sb("spare", [TE, HB], at=buf)
        spare_base = sb("spare_base", [TE, 1], at=buf)
        with nc.Block() as block:
            @block.gpsimd
            def _(pool):
                ch = Chain(pool, pool_chain)
                nc.gpsimd.iota(spare_base[:, :], pattern=[[0, 1]], base=N, channel_multiplier=1,
                               allow_small_or_imprecise_dtypes=True)
                ch.link(nc.gpsimd.memset(tri[:, :], 1.0))
                nc.gpsimd.affine_select(out=tri[:, :], in_=tri[:, :], compare_op=ALU.is_gt, fill=0.0, base=0,
                                        pattern=[[1, TE]], channel_multiplier=-1)
                nc.gpsimd.memset(ones_b[:, :], 1.0)
                nc.gpsimd.memset(rows_in[:, :, :, F:AW], 1.0)
                pool_chain.close(ch.n)

        def tile_loads(eng, odd, i, s):
            for t in range(odd, HB, 2):
                at = eng.value_load(tile_place[0:1, bass.ds((2 * i + s) * HB + t, 1)], min_val=0, max_val=N)
                eng.dma_start(rows_in[:, s, t, 0:F], by_run[bass.ds(at, TE), :]).then_inc(window_in[s].sem, 16)

        with nc.Block() as block:
            @block.sync
            def _(sp):
                with sp.Fori(0, NPASS) as i:
                    for s in range(2):
                        sp.wait_ge(sums_ready[s].sem, sums_ready[s].at(HB * i))
                        sp.sem_inc(pause.sem, 1)
                        tile_loads(sp, 0, i, s)

            @block.vector
            def _(dve):
                PER = 4
                with dve.Fori(0, NPASS) as i:
                    for s in range(2):
                        n = 2 * i + s
                        ch = Chain(dve, dve_chain, PER, n)
                        dve.wait_ge(sums_ready[s].sem, sums_ready[s].at(HB * i))
                        dve.sem_inc(pause.sem, 1)
                        nc.vector.tensor_copy(src_f[:, s, :], src_T[:, halves(i, s)]).then_inc(src_ready.sem, 1)
                        nc.vector.tensor_copy(rank_buf[:, s, :], rank_T[:, halves(i, s)]).then_inc(dve_chain.sem, 1)
                        ch.n += 1
                        dve.wait_ge(dve_chain.sem, dve_chain.at(PER * n + 1))
                        for t in range(HB):
                            nc.vector.tensor_scalar(onehot[:, s, t, :], iota_run[:, :], rank_buf[:, s, t:t + 1], None,
                                                    ALU.is_equal)
                        dve.wait_ge(src_ready.sem, src_ready.at(n + 1))
                        for q in range(4):
                            dve.wait_ge(spread.sem, spread.at(4 * n + q + 1))
                            dve.sem_inc(pause.sem, 1)
                            for t in range(4 * q, 4 * q + 4):
                                ins = nc.vector.tensor_scalar(same[:, s, t, :], bank(4 + q % 2)[:, (t % 4) * TE:(t % 4 + 1) * TE],
                                                              src_f[:, s, t:t + 1], None, ALU.is_equal)
                            ins.then_inc(spread_read.sem, 1)
                        dve.wait_ge(spread_read.sem, spread_read.at(4 * (n + 1)))
                        nc.vector.tensor_tensor(earlier[:, s, :, :], same[:, s, :, :],
                                                tri[:, :].unsqueeze(1).to_broadcast([TE, HB, TE]), ALU.mult
                                                ).then_inc(onehot_ready[s].sem, 1)
                        ch.link(nc.vector.tensor_scalar(spare[:, :], src_f[:, s, :], -1.0, spare_base[:, :], ALU.mult, ALU.add))
                        dve.wait_ge(scatter_idx.sem, scatter_idx.at(n + 1))
                        ch.link(nc.vector.scalar_tensor_tensor(spare[:, :], bank(7)[:, 0:HB], 0.5, spare[:, :], ALU.is_gt, ALU.mult))
                        ch.link(nc.vector.tensor_tensor(spare[:, :], spare[:, :], src_f[:, s, :], ALU.add))
                        for k in range(NACCS):
                            dve.wait_ge(scattered[k].sem, scattered[k].at(16 * (HB // NACCS) * (n - 1)))
                        nc.vector.tensor_copy(idx_buf[:, s, :], spare[:, :]).then_inc(idx_ready[s].sem, 1)
                        dve.wait_ge(idx_ready[s].sem, idx_ready[s].at(i + 1))
                        assert ch.n == PER
                dve_chain.close(PER * 2 * NPASS)

            @block.tensor
            def _(pe):
                with pe.Fori(0, NPASS) as i:
                    for s in range(2):
                        n = 2 * i + s
                        pe.wait_ge(src_ready.sem, src_ready.at(n + 1))
                        for q in range(4):
                            pe.wait_ge(spread_read.sem, spread_read.at(4 * n + max(q - 1, 0)))
                            pe.sem_inc(pause.sem, 1)
                            for t in range(4 * q, 4 * q + 4):
                                ins = nc.tensor.transpose(bank(4 + q % 2)[:, (t % 4) * TE:(t % 4 + 1) * TE],
                                                          src_f[:, s, t:t + 1].to_broadcast([TE, TE]), ident[:, :])
                            ins.then_inc(spread.sem, 1)
                        pe.wait_ge(onehot_ready[s].sem, onehot_ready[s].at(i + 1))
                        pe.wait_ge(idx_ready[1 - s].sem, idx_ready[1 - s].at(i + s))
                        for t in range(HB):
                            ins = nc.tensor.matmul(bank(7)[:, t:t + 1], earlier[:, s, t, :], ones_b[:, :], start=True, stop=True)
                        ins.then_inc(scatter_idx.sem, 1)
                        pe.wait_ge(window_in[s].sem, window_in[s].at(16 * HB * (i + 1)))

                        def count_edges(q):
                            pe.wait_ge(counts_out.sem, counts_out.at(n * 4 + q) if q else counts_out.at(n * 4))
                            for t in range(4 * q, 4 * q + 4):
                                ins = nc.tensor.matmul(bank(q % 2)[:, (t % 4) * TE:(t % 4 + 1) * TE], onehot[:, s, t, :],
                                                       same[:, s, t, :], start=True, stop=True)
                            ins.then_inc(counts_ready.sem, 1)

                        count_edges(0)
                        for q in range(4):
                            pe.wait_ge(counts_out.sem, counts_out.at(n * 4 + q + 1))
                            if q < 3:
                                count_edges(q + 1)
                            for t in range(4 * q, 4 * q + 4):
                                if t % 2 == 0:
                                    pe.wait_ge(evacuated[0].sem, evacuated[0].at(n * (HB // 2) + max(t // 2 - 1, 0)))
                                b = bank(2 + (t // 2) % 2)
                                ins = nc.tensor.matmul(b[:, (t % 2) * AW:(t % 2 + 1) * AW], counts[:, q % 2, t % 4, :],
                                                       rows_in[:, s, t, :], start=True, stop=True)
                                ins.then_inc(sums_ready[s].sem, 1)

            @block.scalar
            def _(act):
                for s in range(2):
                    tile_loads(act, 1, 0, s)
                with act.Fori(0, NPASS) as i:
                    for s in range(2):
                        n = 2 * i + s

                        def counts_copy(q):
                            act.wait_ge(counts_ready.sem, counts_ready.at(4 * n + q + 1))
                            nc.scalar.activation(counts[:, q % 2, :, :].rearrange("p t e -> p (t e)"), bank(q % 2),
                                                 ACT.Copy).then_inc(counts_out.sem, 1)

                        for k in range(NACCS):
                            act.wait_ge(scattered[k].sem, scattered[k].at(16 * (HB // NACCS) * (n - 1)))
                        counts_copy(0)
                        for q in range(4):
                            if q < 3:
                                if q >= 1:
                                    act.wait_ge(sums_ready[s].sem, sums_ready[s].at(HB * i + 4 * q))
                                counts_copy(q + 1)
                            for h in range(2):
                                t = 4 * q + 2 * h
                                act.wait_ge(sums_ready[s].sem, sums_ready[s].at(HB * i + t + 2))
                                nc.scalar.activation(to_add[:, s, t:t + 2, :].rearrange("p t f -> p (t f)"),
                                                     bank(2 + (t // 2) % 2)[:, 0:2 * AW], ACT.Copy
                                                     ).then_inc(evacuated[0].sem, 1)
                        tile_loads(act, 1, i + 1, s)
                for s in range(2):
                    act.wait_ge(window_in[s].sem, window_in[s].at(16 * HB * NPASS + 16 * (HB // 2)))

            @block.gpsimd
            def _(pool):
                with pool.Fori(0, NPASS) as i:
                    for s in range(2):
                        pool.wait_ge(idx_ready[s].sem, idx_ready[s].at(i + 1))
                        for t in range(HB):
                            k = t % NACCS
                            if t % 2 == 0:
                                pool.wait_ge(evacuated[0].sem, evacuated[0].at((2 * i + s) * 8 + t // 2 + 1))
                            pool.wait_ge(scattered[k].sem, scattered[k].at(16 * ((2 * i + s) * (HB // NACCS) + t // NACCS)))
                            pool.sem_inc(pause.sem, 1)
                            nc.gpsimd.indirect_dma_start(acc[k], bass.IndirectOffsetOnAxis(ap=idx_buf[:, s, t:t + 1], axis=0),
                                                         to_add[:, s, t, :], None, compute_op=ALU.add
                                                         ).then_inc(scattered[k].sem, 16)
                for k in range(NACCS):
                    pool.wait_ge(scattered[k].sem, scattered[k].at(16 * (HB // NACCS) * 2 * NPASS))
        for k in scattered:
            k.close(16 * (HB // NACCS) * 2 * NPASS)
        for s in range(2):
            sums_ready[s].close(HB * NPASS)
            window_in[s].close(16 * HB * NPASS + 16 * (HB // 2))
            onehot_ready[s].close(NPASS)
            idx_ready[s].close(NPASS)
        scatter_idx.close(2 * NPASS)
        spread.close(8 * NPASS)
        spread_read.close(8 * NPASS)
        src_ready.close(2 * NPASS)
        counts_ready.close(8 * NPASS)
        counts_out.close(8 * NPASS)
        evacuated[0].close(8 * 2 * NPASS)
        buf.close()

    def border_pass(name):
        buf = ExitStack()
        lasts = sb(name + "_lasts", [BP, BC, F], at=buf)
        firsts = sb(name + "_firsts", [BP, BC, F], at=buf)
        last_T = sb(name + "_last_T", [F, NT + 1], at=buf)
        inflow = sb(name + "_inflow", [F, NT], at=buf)
        carried = sb(name + "_carried", [F, NT], at=buf)
        first_rows = runs[0:NT, :].rearrange("(c p) f -> p c f", p=BP)
        pT = ps[:, 0:4 * 512]
        with nc.Block() as block:
            @block.gpsimd
            def _(pool):
                for k in range(BC):
                    nc.gpsimd.indirect_dma_start(lasts[:, k, :], None, runs, bass.IndirectOffsetOnAxis(
                        ap=last_row[:, k:k + 1], axis=0)).then_inc(gathered[0].sem, 16)

            @block.sync
            def _(sp):
                sp.dma_start(firsts[:, :, :], first_rows).then_inc(loaded[0].sem, 16)
                sp.wait_ge(c["residual"].sem, c["residual"].at(1))
                sp.dma_start(first_rows, firsts[:, :, :]).then_inc(stored[0].sem, 16)
                sp.wait_ge(stored[0].sem, stored[0].at(16))

            @block.tensor
            def _(pe):
                pe.wait_ge(gathered[0].sem, gathered[0].at(16 * BC))
                for k in range(BC):
                    ins = nc.tensor.transpose(bank(k // 4)[:, (k % 4) * BP:(k % 4 + 1) * BP], lasts[:, k, :], ident[0:BP, 0:BP])
                ins.then_inc(c["x_turned"].sem, 1)
                pe.wait_ge(c["normed"].sem, c["normed"].at(1))
                for k in range(BC):
                    ins = nc.tensor.transpose(bank(4 + k // 4)[0:BP, (k % 4) * F:(k % 4 + 1) * F],
                                              carried[:, k * BP:(k + 1) * BP], ident[:, :])
                ins.then_inc(c["normed_turned"].sem, 1)

            @block.vector
            def _(dve):
                ch = Chain(dve, dve_chain)
                nc.vector.memset(last_T[:, 0:1], 0.0)
                dve.wait_ge(c["x_turned"].sem, c["x_turned"].at(1))
                for k in range(4):
                    wide = min(4 * BP, NT - k * 4 * BP)
                    ins = nc.vector.tensor_copy(last_T[:, 1 + k * 4 * BP:1 + k * 4 * BP + wide], bank(k)[:, 0:wide])
                ch.link(ins)
                ch.link(nc.vector.tensor_tensor(inflow[:, :], last_T[:, 0:NT], carries[:, :], ALU.mult))
                nc.vector.tensor_tensor_scan(carried[:, :], through[:, :], inflow[:, :], 0.0, ALU.mult, ALU.add
                                             ).then_inc(c["normed"].sem, 1)
                dve.wait_ge(c["normed_turned"].sem, c["normed_turned"].at(1))
                dve.wait_ge(loaded[0].sem, loaded[0].at(16))
                whole = firsts[:, :, :].rearrange("p c f -> p (c f)")
                nc.vector.tensor_tensor(whole, whole, ps[0:BP, 4 * 512:4 * 512 + BC * F], ALU.add
                                        ).then_inc(c["residual"].sem, 1)
                dve_chain.close(ch.n)
        gathered[0].close(16 * BC)
        loaded[0].close(16)
        stored[0].close(16)
        for k in ("residual", "x_turned", "normed", "normed_turned"):
            c[k].close(1)
        buf.close()

    GT, GROUPS = 4, NT // 4
    UT = 8

    def wait(eng, semaphore, n):
        if not isinstance(n, int) or n > 0:
            eng.wait_ge(semaphore.sem, semaphore.at(n))

    def message_pass(tab_in):
        buf = ExitStack()
        prep = ExitStack()
        time_parts = nc.dram_tensor("time_parts", [3, NCH * TE * TE], BF16, kind="Internal").ap()
        wt_parts = nc.dram_tensor("wt_parts", [3, F], BF16, kind="Internal").ap()
        wt9 = sb("wt9", [9, F], BF16, at=buf)
        time_f = sb("time_f", [128, NCH, TE], at=prep)
        time_b = sb("time_b", [128, 3, NCH, TE], BF16, at=prep)
        wt_f = sb("wt_f", [1, F], at=prep)
        wt_b = sb("wt_b", [1, 3, F], BF16, at=prep)
        with nc.Block() as block:
            @block.vector
            def _(dve):
                nc.vector.memset(time_f[:, CHT:NCH, :], 0.0)
        with nc.Block() as block:
            @block.sync
            def _(sp):
                v = a["edge_weight"]
                whole, rest = CHT * TE * TE, CHR * TE
                sp.dma_start(time_f[:, 0:CHT, :], v[0:whole].rearrange("(c p e) -> p c e", c=CHT, p=128)).then_inc(loaded[0].sem, 16)
                sp.dma_start(time_f[0:CHR, CHT, :], v[whole:whole + rest].rearrange("(p e) -> p e", e=TE)).then_inc(loaded[0].sem, 16)
                sp.dma_start(time_f[CHR:CHR + 1, CHT, 0:REM], v[FULL * TE:E].rearrange("(p e) -> p e", p=1)).then_inc(loaded[0].sem, 16)
                sp.wait_ge(c["dve_setup"].sem, c["dve_setup"].at(1))
                sp.dma_start(time_parts.rearrange("k (c p e) -> p k c e", p=128, e=TE)[:, 0, :, :], time_b[:, 0, :, :]).then_inc(stored[0].sem, 16)
                sp.dma_start(time_parts.rearrange("k (c p e) -> p k c e", p=128, e=TE)[:, 1, :, :], time_b[:, 1, :, :]).then_inc(stored[0].sem, 16)
                sp.dma_start(time_parts.rearrange("k (c p e) -> p k c e", p=128, e=TE)[:, 2, :, :], time_b[:, 2, :, :]).then_inc(stored[0].sem, 16)
                sp.dma_start(wt_parts.rearrange("k f -> (k f)").unsqueeze(0), wt_b[:, :, :].rearrange("p k f -> p (k f)")).then_inc(stored[0].sem, 16)
                sp.wait_ge(stored[0].sem, stored[0].at(64))
                for k in range(3):
                    sp.dma_start(wt9[3 * k:3 * k + 3, :], wt_parts).then_inc(loaded[1].sem, 16)
                sp.wait_ge(loaded[1].sem, loaded[1].at(48))

            @block.vector
            def _(dve):
                ch = Chain(dve, dve_chain)
                dve.wait_ge(loaded[0].sem, loaded[0].at(48))
                ch.link(nc.vector.tensor_copy(wt_f[:, :], m["Wt"][:, :]))
                for full, part in ((time_f[:, :, :], lambda k: time_b[:, k, :, :]), (wt_f[:, :], lambda k: wt_b[:, k, :])):
                    for k in range(3):
                        ch.link(nc.vector.tensor_copy(part(k), full))
                        if k < 2:
                            ch.link(nc.vector.tensor_tensor(full, full, part(k), ALU.subtract))
                nc.vector.memset(wt_f[:, :], 0.0).then_inc(c["dve_setup"].sem, 1)
                dve_chain.close(ch.n)
        loaded[0].close(48)
        loaded[1].close(48)
        stored[0].close(64)
        c["dve_setup"].close(1)
        prep.close()

        got = sb("m_got", [TE, 4, UT, F], at=buf)
        onehot = sb("m_onehot", [TE, 8, GT, TE], at=buf)
        sums = sb("m_sums", [TE, 8, GT, F], at=buf)
        ea = sb("ea", [TE, 2, HB, EC], at=buf)
        times = sb("times", [9, 2, HB * TE], BF16, at=buf)
        ea_T = sb("ea_T", [EC, 2, GT * TE], at=buf)
        gate = sb("gate", [F, 4, GT * TE], at=buf)
        hid = sb("hid", [F, 2, GT * TE], at=buf)
        ef = sb("ef", [F, 2, GT * TE], at=buf)
        idx4 = sb("idx4", [TE, 4, UT], I32, at=buf)
        rank4 = sb("rank4", [TE, 4, UT], at=buf)
        attr = a["edge_attr_64"]
        LAST = NPASS - 1

        def group(i, u, back):
            return 8 * i + u - back, (u - back) % 8

        def drive(eng, step):
            for u in range(8):
                step(0, u)
            with eng.Fori(1, LAST) as i:
                for u in range(8):
                    step(i, u)
            for u in range(8):
                step(LAST, u)
            for u in range(4):
                step(NPASS, u)

        def there(i, u, back):
            g = 8 * i + u - back
            return not isinstance(g, int) or 0 <= g < GROUPS

        with nc.Block() as block:
            @block.gpsimd
            def _(pool):
                with pool.Fori(0, NPASS) as i:
                    for v in range(4):
                        pool.wait_ge(idx_ready[v].sem, idx_ready[v].at(i + 1))
                        pool.sem_inc(pause.sem, 1)
                        for t in range(UT):
                            nc.gpsimd.indirect_dma_start(got[:, v, t, :], None, tab_in, bass.IndirectOffsetOnAxis(
                                ap=idx4[:, v, t:t + 1], axis=0)).then_inc(gathered[v].sem, 16)

            @block.tensor
            def _(pe):
                def step(i, u):
                    if there(i, u, 4):
                        g, r = group(i, u, 4)
                        wait(pe, onehot_ready[0], g + 1)
                        wait(pe, c["msg_out"], g + 1)
                        wait(pe, evacuated[0], g - 1)
                        for t in range(GT):
                            ins = nc.tensor.matmul(bank(5 + r % 2)[:, t * F:(t + 1) * F], onehot[:, r, t, :],
                                                   got[:, r // 2, (r % 2) * GT + t, :], start=True, stop=True)
                        ins.then_inc(sums_ready[0].sem, 1)
                    if there(i, u, 3):
                        g, r = group(i, u, 3)
                        wait(pe, c["ef_out"], g + 1)
                        wait(pe, c["z_out"], g - 1)
                        for t in range(GT):
                            ins = nc.tensor.matmul(bank((4, 7)[r % 2])[:, t * F:(t + 1) * F], ef[:, r % 2, t * TE:(t + 1) * TE],
                                                   m["Wn1"][:, 1, :], start=True, stop=True)
                        ins.then_inc(c["z_ready"].sem, 1)
                    if there(i, u, 2):
                        g, r = group(i, u, 2)
                        wait(pe, c["hid_out"], g + 1)
                        wait(pe, c["ef_out"], g)
                        nc.tensor.matmul(bank(3), m["We2"][:, :], hid[:, r % 2, :], start=True, stop=True
                                         ).then_inc(c["ef_ready"].sem, 1)
                    if there(i, u, 1):
                        g, r = group(i, u, 1)
                        wait(pe, c["ea_out"], g + 1)
                        wait(pe, c["hid_out"], g)
                        nc.tensor.matmul(bank(2), m["We1"][:, :], ea_T[:, r % 2, :], start=True, stop=True
                                         ).then_inc(c["hid_ready"].sem, 1)
                    if there(i, u, 0):
                        g, r = group(i, u, 0)
                        s = r // 4
                        if r % 4 == 0:
                            pe.wait_ge(loaded[s].sem, loaded[s].at(32 * (i + 1)))
                            if isinstance(i, int) and i == LAST and s == 1:
                                pe.wait_ge(setup_dma.sem, setup_dma.at(16))
                        wait(pe, c["ea_out"], g)
                        pe.sem_inc(pause.sem, 1)
                        for t in range(GT):
                            ins = nc.tensor.transpose(bank(0)[0:EC, t * TE:(t + 1) * TE], ea[:, s, (r % 4) * GT + t, :], ident[:, :])
                        ins.then_inc(c["ea_turned"].sem, 1)
                        wait(pe, c["gate_out"], g)
                        nc.tensor.matmul(bank(1), wt9[:, :], times[:, s, (r % 4) * GT * TE:(r % 4 + 1) * GT * TE],
                                         start=True, stop=True).then_inc(c["gate_ready"].sem, 1)
                drive(pe, step)

            @block.scalar
            def _(act):
                def step(i, u):
                    if there(i, u, 4):
                        g, r = group(i, u, 4)
                        if r % 4 == 0:
                            s = r // 4
                            act.wait_ge(stored[s].sem, stored[s].at(16 * ((i if u >= 4 else i - 1))))
                        wait(act, sums_ready[0], g + 1)
                        nc.scalar.activation(sums[:, r, :, :].rearrange("p t f -> p (t f)"), bank(5 + r % 2), ACT.Copy
                                             ).then_inc(evacuated[0].sem, 1)
                    if there(i, u, 3):
                        g, r = group(i, u, 3)
                        wait(act, c["z_out"], g + 1)
                        rows_ = got[:, r // 2, (r % 2) * GT:(r % 2 + 1) * GT, :].rearrange("p t f -> p (t f)")
                        nc.scalar.activation(rows_, rows_, ACT.Relu).then_inc(c["msg_out"].sem, 1)
                    if there(i, u, 1):
                        g, r = group(i, u, 1)
                        wait(act, c["hid_ready"], g + 1)
                        wait(act, c["ef_ready"], g - 1)
                        nc.scalar.activation(hid[:, r % 2, :], bank(2), ACT.Relu, bias=m["be1"][:, 0:1]
                                             ).then_inc(c["hid_out"].sem, 1)
                    if there(i, u, 0):
                        g, r = group(i, u, 0)
                        wait(act, c["gate_ready"], g + 1)
                        wait(act, c["ef_out"], g - 3)
                        nc.scalar.activation(gate[:, r % 4, :], bank(1), ACT.Sigmoid, bias=m["bt"][:, 0:1]
                                             ).then_inc(c["gate_out"].sem, 1)
                drive(act, step)

            @block.vector
            def _(dve):
                def numbers(i, v, unit):
                    wait(dve, sums_ready[0], 2 * unit - 6)
                    dve.sem_inc(pause.sem, 1)
                    nc.vector.tensor_copy(idx4[:, v, :], src_T[:, bass.ds(unit * UT, UT)]).then_inc(idx_ready[v].sem, 1)

                def step(i, u):
                    if u % 2 == 0 and there(i, u, 0):
                        unit = 4 * i + u // 2
                        if not (isinstance(unit, int) and unit + 1 >= 4 * NPASS):
                            numbers(i, (u // 2 + 1) % 4, unit + 1)
                    if u % 2 == 0 and there(i, u, 2):
                        unit = 4 * i + (u - 2) // 2
                        wait(dve, onehot_ready[0], 2 * unit - 6)
                        dve.sem_inc(pause.sem, 1)
                        nc.vector.tensor_copy(rank4[:, (u // 2 - 1) % 4, :], rank_T[:, bass.ds(unit * UT, UT)]
                                              ).then_inc(dve_chain.sem, 1)
                        dve.wait_ge(dve_chain.sem, dve_chain.at(unit + 1))
                    if there(i, u, 3):
                        g, r = group(i, u, 3)
                        if r % 2 == 0:
                            dve.wait_ge(gathered[r // 2].sem, gathered[r // 2].at(16 * UT * ((i + 1) if u >= 3 else i)))
                        wait(dve, c["z_ready"], g + 1)
                        rows_ = got[:, r // 2, (r % 2) * GT:(r % 2 + 1) * GT, :].rearrange("p t f -> p (t f)")
                        nc.vector.tensor_tensor(rows_, rows_, bank((4, 7)[r % 2]), ALU.add).then_inc(c["z_out"].sem, 1)
                    if there(i, u, 2):
                        g, r = group(i, u, 2)
                        wait(dve, c["ef_ready"], g + 1)
                        wait(dve, c["gate_out"], g + 1)
                        wait(dve, c["z_ready"], g - 1)
                        nc.vector.scalar_tensor_tensor(ef[:, r % 2, :], bank(3), m["be2"][:, 0:1], gate[:, r % 4, :],
                                                       ALU.add, ALU.mult).then_inc(c["ef_out"].sem, 1)
                        wait(dve, sums_ready[0], g - 7)
                        for t in range(GT):
                            ins = nc.vector.tensor_scalar(onehot[:, r, t, :], iota_run[:, :],
                                                          rank4[:, r // 2, (r % 2) * GT + t:(r % 2) * GT + t + 1], None, ALU.is_equal)
                        ins.then_inc(onehot_ready[0].sem, 1)
                    if there(i, u, 0):
                        g, r = group(i, u, 0)
                        wait(dve, c["ea_turned"], g + 1)
                        wait(dve, c["hid_ready"], g - 1)
                        nc.vector.tensor_copy(ea_T[:, r % 2, :], bank(0)[0:EC, :]).then_inc(c["ea_out"].sem, 1)
                numbers(0, 0, 0)
                drive(dve, step)

            @block.sync
            def _(sp):
                def load(i, s):
                    h = 2 * i + s
                    wait(sp, c["gate_ready"], 4 * h - 4)
                    if isinstance(h, int) and h == 2 * NPASS - 1:
                        whole = FULL - h * HB
                        sp.dma_start(ea[:, s, 0:whole, :], attr[h * HB * TE:FULL * TE, :].rearrange("(t p) c -> p t c", p=TE)
                                     ).then_inc(loaded[s].sem, 16)
                        sp.dma_start(ea[0:REM, s, whole, :], attr[FULL * TE:E, :]).then_inc(setup_dma.sem, 16)
                    else:
                        sp.dma_start(ea[:, s, :, :], attr[bass.ds(h * HB * TE, HB * TE), :].rearrange("(t p) c -> p t c", p=TE)
                                     ).then_inc(loaded[s].sem, 16)
                    sp.dma_start(times[:, s, :], time_parts[:, bass.ds(h * HB * TE, HB * TE)].unsqueeze(1).to_broadcast([3, 3, HB * TE])
                                 ).then_inc(loaded[s].sem, 16)

                def store(i, s):
                    h = 2 * i + s
                    sp.wait_ge(evacuated[0].sem, evacuated[0].at(4 * (h + 1)))
                    sp.dma_start(run_view[:, bass.ds(h * HB, HB), :], sums[:, 4 * s:4 * s + 4, :, :].rearrange("p g t f -> p (g t) f")
                                 ).then_inc(stored[s].sem, 16)

                load(0, 0)
                load(0, 1)
                load(1, 0)
                load(1, 1)
                store(0, 0)
                with sp.Fori(1, LAST - 1) as i:
                    load(i + 1, 0)
                    store(i - 1, 1)
                    load(i + 1, 1)
                    store(i, 0)
                load(LAST, 0)
                store(LAST - 2, 1)
                load(LAST, 1)
                for h in range(2 * LAST - 2, 2 * NPASS):
                    store(h // 2, h % 2)
                for s in range(2):
                    sp.wait_ge(stored[s].sem, stored[s].at(16 * NPASS))
        for k in ("ea_turned", "ea_out", "gate_ready", "gate_out", "hid_ready", "hid_out", "ef_ready", "ef_out", "z_ready",
                  "z_out", "msg_out"):
            c[k].close(GROUPS)
        for k in (onehot_ready[0], sums_ready[0], evacuated[0]):
            k.close(GROUPS)
        for v in range(4):
            gathered[v].close(16 * UT * NPASS)
            idx_ready[v].close(NPASS)
        loaded[0].close(32 * NPASS)
        loaded[1].close(32 * NPASS)
        setup_dma.close(16)
        dve_chain.close(4 * NPASS)
        for s in range(2):
            stored[s].close(16 * NPASS)
        buf.close()

    att = ExitStack()

    def attention_setup():
        kd_T = sb("kd_T", [TE, H, NT], at=att)
        kind_T = sb("kind_T", [TE, KINDS, NT], at=att)
        buf = ExitStack()
        natural = sb("natural", [128, NCH, TE, H], at=buf)
        held_kd = sb("held_kd", [128, 2, H, TE], at=buf)
        keep = sb("keep", [128, NCH, SW], at=buf)
        first_kd = sb("first_kd", [128, NCH, H], at=buf)
        key_in = sb("key_in", [128, NCH], at=buf)
        first_i = sb("first_i", [128, NCH], I32, at=buf)
        type_i = sb("type_i", [128, NCH, TE], I32, at=buf)
        type_f = sb("type_f", [128, NCH, TE], at=buf)
        with nc.Block() as block:
            @block.vector
            def _(dve):
                nc.vector.memset(type_i[:, CHT:NCH, :], 0).then_inc(c["dve_setup"].sem, 1)
                ch = Chain(dve, dve_chain)
                dve.wait_ge(loaded[0].sem, loaded[0].at(16))
                ch.link(nc.vector.tensor_scalar(key_in[:, :], key_in[:, :], float(N - 1), None, ALU.min))
                nc.vector.tensor_copy(first_i[:, :], key_in[:, :])
                dve_chain.close(ch.n)

            @block.sync
            def _(sp):
                sp.dma_start(key_in[:, :].unsqueeze(2), keys.rearrange("(c p) k -> p c k", p=128)[:, :, 0:1],
                             allow_slow_non_contiguous=True).then_inc(loaded[0].sem, 16)
                sp.dma_start(keep[:, :, :], starts_d.rearrange("(c p) k -> p c k", p=128)).then_inc(setup_dma.sem, 16)
                sp.dma_start(nodes(kd_rows), kd_node[:, :, :]).then_inc(setup_dma.sem, 16)
                sp.wait_ge(c["dve_setup"].sem, c["dve_setup"].at(1))
                v = a["edge_type_3"]
                whole, rest = CHT * TE * TE, CHR * TE
                sp.dma_start(type_i[:, 0:CHT, :], v[0:whole].rearrange("(c p e) -> p c e", c=CHT, p=128)).then_inc(setup_dma.sem, 16)
                sp.dma_start(type_i[0:CHR, CHT, :], v[whole:whole + rest].rearrange("(p e) -> p e", e=TE)).then_inc(setup_dma.sem, 16)
                sp.dma_start(type_i[CHR:CHR + 1, CHT, 0:REM], v[FULL * TE:E].rearrange("(p e) -> p e", p=1)).then_inc(setup_dma.sem, 16)
                setup_dma.close(80)
                sp.wait_ge(setup_dma.sem, setup_dma.at(0))
        c["dve_setup"].close(1)
        loaded[0].close(16)

        with nc.Block() as block:
            @block.gpsimd
            def _(pool):
                for k in range(NCH):
                    nc.gpsimd.indirect_dma_start(first_kd[:, k, :], None, kd_rows, bass.IndirectOffsetOnAxis(
                        ap=first_i[:, k:k + 1], axis=0)).then_inc(gathered[0].sem, 16)
                pool.wait_ge(gathered[0].sem, gathered[0].at(16 * NCH))

            @block.vector
            def _(dve):
                ch = Chain(dve, dve_chain)
                ch.link(nc.vector.tensor_copy(type_f[:, :, :], type_i[:, :, :]))
                nc.vector.tensor_scalar(keep[:, :, :], keep[:, :, :], 1.0 / FAR, 1.0, ALU.mult, ALU.add
                                        ).then_inc(c["dve_setup"].sem, 1)
                dve_chain.close(ch.n)

            @block.sync
            def _(sp):
                sp.dma_start(natural[:, :, :, :], kd_edge[0:NCH * TE * TE, :].rearrange("(c p e) h -> p c e h", p=128, e=TE)
                             ).then_inc(loaded[0].sem, 16)
                sp.wait_ge(loaded[0].sem, loaded[0].at(16))
        gathered[0].close(16 * NCH)
        c["dve_setup"].close(1)
        loaded[0].close(16)

        with nc.Block() as block:
            @block.vector
            def _(dve):
                ch = Chain(dve, dve_chain)
                ch.link(nc.vector.tensor_copy(natural[:, :, 0, :], first_kd[:, :, :]))
                for k in range(NCH):
                    wide = min(TE, NT - k * TE)
                    s = k % 2
                    wait(dve, c["x_turned"], k - 1)
                    for h in range(H):
                        ins = nc.vector.tensor_tensor_scan(held_kd[:, s, h, :], keep[:, k, 0:TE], natural[:, k, :, h], 0.0,
                                                           ALU.mult, ALU.add)
                    ins.then_inc(c["normed"].sem, 1)
                    dve.wait_ge(c["x_turned"].sem, c["x_turned"].at(k + 1))
                    nc.vector.tensor_copy(kd_T[:, :, k * TE:k * TE + wide],
                                          bank(2 * s).rearrange("p (h t) -> p h t", h=H)[:, :, 0:wide])
                    for j in range(KINDS):
                        ins = nc.vector.tensor_scalar(kind_T[:, j, k * TE:k * TE + wide], bank(2 * s + 1)[:, 0:wide], float(j), None,
                                                      ALU.is_equal)
                    ins.then_inc(c["x_turned_out"].sem, 1)
                dve_chain.close(ch.n)

            @block.tensor
            def _(pe):
                for k in range(NCH):
                    s = k % 2
                    pe.wait_ge(c["normed"].sem, c["normed"].at(k + 1))
                    wait(pe, c["x_turned_out"], k - 1)
                    for h in range(H):
                        nc.tensor.transpose(bank(2 * s)[:, h * TE:(h + 1) * TE], held_kd[:, s, h, :], ident[:, :])
                    nc.tensor.transpose(bank(2 * s + 1)[:, 0:TE], type_f[:, k, :], ident[:, :]).then_inc(c["x_turned"].sem, 1)
        for k in ("x_turned", "x_turned_out", "normed"):
            c[k].close(NCH)
        buf.close()
        return kd_T, kind_T

    def attention_pass(kd_T, kind_T):
        buf = ExitStack()
        HT = H * HB
        got = sb("a_got", [TE, 2, HB, TW], at=buf)
        msg = sb("a_msg", [TE, 2, HB, RW], at=buf)
        onehot = sb("a_onehot", [TE, 2, HB, TE], at=buf)
        sums = sb("a_sums", [TE, 2, HB, RW], at=buf)
        mark = sb("mark", [HT, 2, SW], at=buf)
        picked = sb("picked", [TE, KINDS, H, HB], at=buf)
        embed = sb("embed_score", [TE, H, HB], at=buf)
        score = sb("score", [TE, H, HB], at=buf)
        upward = sb("upward", [HT, TE], at=buf)
        top = sb("top", [HT, TE], at=buf)
        shifted = sb("shifted", [HT, TE], at=buf)
        ex = sb("ex", [HT, TE], at=buf)
        top_start = sb("top_start", [HT, TE], at=buf)
        runs3_view = runs3.rearrange("(r t) f -> r t f", t=NT)
        with nc.Block() as block:
            @block.gpsimd
            def _(pool):
                with pool.Fori(0, NPASS) as i:
                    for s in range(2):
                        pool.wait_ge(idx_ready[s].sem, idx_ready[s].at(i + 1))
                        pool.sem_inc(pause.sem, 1)
                        for t in range(HB):
                            nc.gpsimd.indirect_dma_start(got[:, s, t, :], None, table3, bass.IndirectOffsetOnAxis(
                                ap=idx_buf[:, s, t:t + 1], axis=0)).then_inc(gathered[s].sem, 16)

            @block.vector
            def _(dve):
                PER = 7
                for s in range(2):
                    nc.vector.tensor_copy(idx_buf[:, s, :], src_T[:, s * HB:(s + 1) * HB]).then_inc(idx_ready[s].sem, 1)
                with dve.Fori(0, NPASS) as i:
                    for s in range(2):
                        n = 2 * i + s
                        ch = Chain(dve, dve_chain, PER, n)
                        dve.wait_ge(sums_ready[s].sem, sums_ready[s].at(8 * i))
                        dve.sem_inc(pause.sem, 1)
                        ch.link(nc.vector.tensor_copy(rank_buf[:, s, :], rank_T[:, halves(i, s)]))
                        for t in range(HB):
                            ins = nc.vector.tensor_scalar(onehot[:, s, t, :], iota_run[:, :], rank_buf[:, s, t:t + 1],
                                                          None, ALU.is_equal)
                        ins.then_inc(onehot_ready[s].sem, 1)
                        dve.wait_ge(gathered[s].sem, gathered[s].at(16 * HB * (i + 1)))
                        dve.sem_inc(pause.sem, 1)
                        for k in range(KINDS):
                            ins = nc.vector.tensor_tensor(
                                picked[:, k, :, :], got[:, s, :, F + (1 + k) * H:F + (2 + k) * H].rearrange("p t h -> p h t"),
                                kind_T[:, k, halves(i, s)].unsqueeze(1).to_broadcast([TE, H, HB]), ALU.mult)
                        ch.link(ins)
                        nc.vector.tensor_reduce(embed[:, :, :], picked[:, :, :, :].rearrange("p k h t -> p h t k"), AX.X, ALU.add)
                        ch.link(nc.vector.tensor_tensor(score[:, :, :], got[:, s, :, F:F + H].rearrange("p t h -> p h t"),
                                                        kd_T[:, :, halves(i, s)], ALU.add))
                        ch.link(nc.vector.scalar_tensor_tensor(score[:, :, :], score[:, :, :], SLOPE, score[:, :, :], ALU.mult, ALU.max))
                        nc.vector.tensor_tensor(score[:, :, :], score[:, :, :], embed[:, :, :], ALU.add
                                                ).then_inc(c["ea_out"].sem, 1)
                        dve.wait_ge(c["ea_turned"].sem, c["ea_turned"].at(n + 1))
                        dve.wait_ge(loaded[s].sem, loaded[s].at(16 * H * (i + 1)))
                        turned = bank(0)[0:HT, 0:TE]
                        ch.link(nc.vector.tensor_tensor_scan(upward[:, :], mark[:, s, 0:TE], turned, -FAR, ALU.add, ALU.max))
                        ch.link(nc.vector.tensor_tensor_scan(top[:, ::-1], mark[:, s, TE:0:-1], upward[:, ::-1], -FAR,
                                                             ALU.add, ALU.max))
                        nc.vector.tensor_tensor(shifted[:, :], turned, top[:, :], ALU.subtract).then_inc(c["hid_ready"].sem, 1)
                        ch.link(nc.vector.scalar_tensor_tensor(top_start[:, :], mark[:, s, 0:TE], -1.0 / FAR, top[:, :],
                                                               ALU.mult, ALU.mult))
                        dve.sem_inc(c["hid_out"].sem, 1)
                        dve.wait_ge(c["ef_out"].sem, c["ef_out"].at(n + 1))
                        dve.sem_inc(pause.sem, 1)
                        for t in range(HB):
                            ins = nc.vector.tensor_tensor(
                                msg[:, s, t, 0:F].rearrange("p (h d) -> p h d", h=H), got[:, s, t, 0:F].rearrange("p (h d) -> p h d", h=H),
                                msg[:, s, t, F:F + H].unsqueeze(2).to_broadcast([TE, H, HD]), ALU.mult)
                        ins.then_inc(c["msg_out"].sem, 1)
                        dve.wait_ge(c["msg_out"].sem, c["msg_out"].at(n + 1))
                        dve.sem_inc(pause.sem, 1)
                        nc.vector.tensor_copy(idx_buf[:, s, :], src_T[:, bass.ds((2 * i + s + 2) * HB, HB)]
                                              ).then_inc(idx_ready[s].sem, 1)
                        assert ch.n == PER, ch.n
                dve_chain.close(PER * 2 * NPASS)

            @block.tensor
            def _(pe):
                with pe.Fori(0, NPASS) as i:
                    for s in range(2):
                        n = 2 * i + s
                        pe.wait_ge(c["ea_out"].sem, c["ea_out"].at(n + 1))
                        pe.sem_inc(pause.sem, 1)
                        nc.tensor.transpose(bank(0)[0:HT, 0:TE], score[:, :, :].rearrange("p h t -> p (h t)"), ident[:, :]
                                            ).then_inc(c["ea_turned"].sem, 1)
                        pe.wait_ge(c["hid_out"].sem, c["hid_out"].at(n + 1))
                        pe.wait_ge(c["ef_ready"].sem, c["ef_ready"].at(n + 1))
                        pe.sem_inc(pause.sem, 1)
                        nc.tensor.transpose(bank(1)[:, 0:HT], ex[:, :], ident[0:HT, 0:HT])
                        nc.tensor.transpose(bank(1)[:, HT:2 * HT], top_start[:, :], ident[0:HT, 0:HT]
                                            ).then_inc(c["z_ready"].sem, 1)
                        pe.wait_ge(onehot_ready[s].sem, onehot_ready[s].at(i + 1))
                        pe.wait_ge(c["msg_out"].sem, c["msg_out"].at(n + 1))
                        for q in range(8):
                            if q % 4 == 0:
                                pe.wait_ge(evacuated[0].sem, evacuated[0].at(8 * n + q))
                            for t in range(2 * q, 2 * q + 2):
                                ins = nc.tensor.matmul(bank(4 + q % 4)[:, (t % 2) * RW:(t % 2 + 1) * RW], onehot[:, s, t, :],
                                                       msg[:, s, t, :], start=True, stop=True)
                            ins.then_inc(sums_ready[s].sem, 1)

            @block.scalar
            def _(act):
                with act.Fori(0, NPASS) as i:
                    for s in range(2):
                        n = 2 * i + s
                        act.wait_ge(c["hid_ready"].sem, c["hid_ready"].at(n + 1))
                        nc.scalar.activation(ex[:, :], shifted[:, :], ACT.Exp).then_inc(c["ef_ready"].sem, 1)
                        act.wait_ge(c["z_ready"].sem, c["z_ready"].at(n + 1))
                        nc.scalar.activation(msg[:, s, :, F:RW].rearrange("p t (k h) -> p k h t", k=2),
                                             bank(1)[:, 0:2 * HT].rearrange("p (k h t) -> p k h t", k=2, h=H), ACT.Copy
                                             ).then_inc(c["ef_out"].sem, 1)
                        act.wait_ge(stored[s].sem, stored[s].at(16 * i))
                        for q in range(8):
                            act.wait_ge(sums_ready[s].sem, sums_ready[s].at(8 * i + q + 1))
                            nc.scalar.activation(sums[:, s, 2 * q:2 * q + 2, :].rearrange("p t f -> p (t f)"),
                                                 bank(4 + q % 4)[:, 0:2 * RW], ACT.Copy).then_inc(evacuated[0].sem, 1)

            @block.sync
            def _(sp):
                def load(i, s):
                    for h in range(H):
                        sp.dma_start(mark[h * HB:(h + 1) * HB, s, :], starts_d[halves(i, s), :]).then_inc(loaded[s].sem, 16)

                load(0, 0)
                load(0, 1)
                with sp.Fori(0, NPASS - 1) as i:
                    for s in range(2):
                        sp.wait_ge(c["z_ready"].sem, c["z_ready"].at(2 * i + s + 1))
                        load(i + 1, s)
                        sp.wait_ge(evacuated[0].sem, evacuated[0].at(8 * (2 * i + s + 1)))
                        sp.dma_start(runs3_view[:, halves(i, s), :], sums[:, s, :, :]).then_inc(stored[s].sem, 16)
                for s in range(2):
                    sp.wait_ge(evacuated[0].sem, evacuated[0].at(8 * (2 * NPASS - 1 + s)))
                    sp.dma_start(runs3_view[:, halves(NPASS - 1, s), :], sums[:, s, :, :]).then_inc(stored[s].sem, 16)
                for s in range(2):
                    sp.wait_ge(stored[s].sem, stored[s].at(16 * NPASS))
        for s in range(2):
            idx_ready[s].close(NPASS + 1)
            onehot_ready[s].close(NPASS)
            gathered[s].close(16 * HB * NPASS)
            sums_ready[s].close(8 * NPASS)
            stored[s].close(16 * NPASS)
            loaded[s].close(16 * H * NPASS)
        evacuated[0].close(16 * NPASS)
        for k in ("ea_out", "ea_turned", "hid_ready", "hid_out", "ef_ready", "ef_out", "z_ready", "msg_out"):
            c[k].close(2 * NPASS)
        buf.close()

    def attention_border():
        buf = ExitStack()
        lasts = sb("b_lasts", [BP, BC, RW], at=buf)
        firsts = sb("b_firsts", [BP, BC, RW], at=buf)
        last_T = sb("b_last_T", [F, NT + 1], at=buf)
        den_T = sb("b_den_T", [H, NT + 1], at=buf)
        max_T = sb("b_max_T", [H, NT + 1], at=buf)
        open_ = sb("b_open", [H, NT], at=buf)
        carried_m = sb("b_carried_m", [H, NT + 1], at=buf)
        alpha = sb("b_alpha", [H, NT], at=buf)
        beta = sb("b_beta", [H, NT], at=buf)
        carried_d = sb("b_carried_d", [H, NT], at=buf)
        wide_a = sb("b_wide_a", [F, NT], at=buf)
        wide_b = sb("b_wide_b", [F, NT], at=buf)
        carried = sb("b_carried", [F, NT], at=buf)
        head_of = sb("head_of", [H, F], at=buf)
        new_m = sb("b_new_m", [BP, BC, H], at=buf)
        own_f = sb("b_own_f", [BP, BC, H], at=buf)
        carry_f = sb("b_carry_f", [BP, BC, H], at=buf)
        tmp = sb("b_tmp", [BP, BC, H], at=buf)
        back = sb("b_back", [BP, BC, F], at=buf)
        first_rows = runs3[0:NT, :].rearrange("(c p) f -> p c f", p=BP)
        done = c["x_turned_out"]
        WIDE = NT // 4
        with nc.Block() as block:
            @block.gpsimd
            def _(pool):
                ch = Chain(pool, pool_chain)
                ch.link(nc.gpsimd.memset(head_of[:, :], 1.0))
                ch.link(nc.gpsimd.affine_select(out=head_of[:, :], in_=head_of[:, :], compare_op=ALU.is_ge, fill=0.0, base=0,
                                                pattern=[[1, F]], channel_multiplier=-HD))
                ch.link(nc.gpsimd.affine_select(out=head_of[:, :], in_=head_of[:, :], compare_op=ALU.is_gt, fill=0.0, base=HD,
                                                pattern=[[-1, F]], channel_multiplier=HD))
                pool_chain.close(ch.n)
                for k in range(BC):
                    nc.gpsimd.indirect_dma_start(lasts[:, k, :], None, runs3, bass.IndirectOffsetOnAxis(
                        ap=last_row[:, k:k + 1], axis=0)).then_inc(gathered[0].sem, 16)
                pool.wait_ge(gathered[0].sem, gathered[0].at(16 * BC))

            @block.sync
            def _(sp):
                sp.dma_start(firsts[:, :, :], first_rows).then_inc(loaded[0].sem, 16)
                sp.wait_ge(loaded[0].sem, loaded[0].at(16))
        gathered[0].close(16 * BC)
        loaded[0].close(16)

        def turn_all(pieces):
            with nc.Block() as block:
                @block.tensor
                def _(pe):
                    for first_bank, wide, f0, _ in pieces:
                        for k in range(BC):
                            ins = nc.tensor.transpose(bank(first_bank + k // 4)[0:wide, (k % 4) * BP:(k % 4 + 1) * BP],
                                                      lasts[:, k, f0:f0 + wide], ident[0:BP, 0:BP])
                        ins.then_inc(c["x_turned"].sem, 1)

                @block.vector
                def _(dve):
                    for n, (first_bank, wide, f0, dest) in enumerate(pieces):
                        dve.wait_ge(c["x_turned"].sem, c["x_turned"].at(n + 1))
                        nc.vector.memset(dest[:, 0:1], 0.0)
                        for k in range(4):
                            w = min(4 * BP, NT - k * 4 * BP)
                            nc.vector.tensor_copy(dest[:, 1 + k * 4 * BP:1 + k * 4 * BP + w], bank(first_bank + k)[0:wide, 0:w])
            c["x_turned"].close(len(pieces))

        turn_all([(0, F, 0, last_T), (4, H, F, den_T)])
        turn_all([(0, H, F + H, max_T)])
        with nc.Block() as block:
            @block.vector
            def _(dve):
                ch = Chain(dve, dve_chain)
                c4, t4 = carries[0:H, :], through[0:H, :]
                ch.link(nc.vector.tensor_scalar(open_[:, :], c4, -1.0, FAR, ALU.add, ALU.mult))
                ch.link(nc.vector.tensor_tensor(alpha[:, :], max_T[:, 0:NT], c4, ALU.mult))
                ch.link(nc.vector.tensor_tensor(alpha[:, :], alpha[:, :], open_[:, :], ALU.add))
                ch.link(nc.vector.tensor_scalar(open_[:, :], t4, -1.0, FAR, ALU.add, ALU.mult))
                ch.link(nc.vector.memset(carried_m[:, 0:1], -FAR))
                ch.link(nc.vector.tensor_tensor_scan(carried_m[:, 1:NT + 1], open_[:, :], alpha[:, :], -FAR, ALU.add, ALU.max))
                ch.link(nc.vector.tensor_tensor(alpha[:, :], carried_m[:, 0:NT], carried_m[:, 1:NT + 1], ALU.subtract))
                ch.link(nc.vector.tensor_scalar(alpha[:, :], alpha[:, :], 0.0, None, ALU.min))
                ch.link(nc.vector.tensor_tensor(beta[:, :], max_T[:, 0:NT], carried_m[:, 1:NT + 1], ALU.subtract))
                nc.vector.tensor_scalar(beta[:, :], beta[:, :], 0.0, None, ALU.min).then_inc(c["exponent"].sem, 1)
                dve.wait_ge(c["exponent_out"].sem, c["exponent_out"].at(1))
                ch.link(nc.vector.tensor_tensor(alpha[:, :], alpha[:, :], t4, ALU.mult))
                nc.vector.tensor_tensor(beta[:, :], beta[:, :], c4, ALU.mult).then_inc(c["normed"].sem, 1)
                dve.wait_ge(c["normed"].sem, c["normed"].at(1))
                ch.link(nc.vector.tensor_tensor(den_T[:, 0:NT], den_T[:, 0:NT], beta[:, :], ALU.mult))
                nc.vector.tensor_tensor_scan(carried_d[:, :], alpha[:, :], den_T[:, 0:NT], 0.0, ALU.mult, ALU.add)
                for k, dest in enumerate((wide_a, wide_b)):
                    for q in range(4):
                        dve.wait_ge(c["product"].sem, c["product"].at(4 * k + q + 1))
                        ins = nc.vector.tensor_copy(dest[:, q * WIDE:(q + 1) * WIDE], bank(4 * k + q)[:, 0:WIDE])
                ch.link(ins)
                ch.link(nc.vector.tensor_tensor(wide_b[:, :], wide_b[:, :], last_T[:, 0:NT], ALU.mult))
                ch.link(nc.vector.tensor_tensor_scan(carried[:, :], wide_a[:, :], wide_b[:, :], 0.0, ALU.mult, ALU.add))
                dve_chain.close(ch.n)

            @block.scalar
            def _(act):
                act.wait_ge(c["exponent"].sem, c["exponent"].at(1))
                nc.scalar.activation(alpha[:, :], alpha[:, :], ACT.Exp)
                nc.scalar.activation(beta[:, :], beta[:, :], ACT.Exp).then_inc(c["exponent_out"].sem, 1)

            @block.tensor
            def _(pe):
                pe.wait_ge(c["normed"].sem, c["normed"].at(1))
                for k, s_ in enumerate((alpha, beta)):
                    for q in range(4):
                        nc.tensor.matmul(bank(4 * k + q)[:, 0:WIDE], head_of[:, :], s_[:, q * WIDE:(q + 1) * WIDE],
                                         start=True, stop=True).then_inc(c["product"].sem, 1)
        for k, n in (("exponent", 1), ("exponent_out", 1), ("normed", 1), ("product", 8)):
            c[k].close(n)
        with nc.Block() as block:
            @block.tensor
            def _(pe):
                for k in range(BC):
                    nc.tensor.transpose(bank(k // 4)[0:BP, (k % 4) * F:(k % 4 + 1) * F], carried[:, k * BP:(k + 1) * BP], ident[:, :])
                    nc.tensor.transpose(bank(4)[0:BP, k * H:(k + 1) * H], carried_d[:, k * BP:(k + 1) * BP], ident[0:H, 0:H])
                    ins = nc.tensor.transpose(bank(5)[0:BP, k * H:(k + 1) * H], carried_m[:, 1 + k * BP:1 + (k + 1) * BP], ident[0:H, 0:H])
                ins.then_inc(c["x_turned"].sem, 1)

            @block.vector
            def _(dve):
                ch = Chain(dve, dve_chain)
                dve.wait_ge(c["x_turned"].sem, c["x_turned"].at(1))
                carry_s = ps[0:BP, 0:BC * F].rearrange("p (c f) -> p c f", f=F)
                carry_d = bank(4)[0:BP, 0:BC * H].rearrange("p (c h) -> p c h", h=H)
                carry_m = bank(5)[0:BP, 0:BC * H].rearrange("p (c h) -> p c h", h=H)
                own_s, own_d, own_m = firsts[:, :, 0:F], firsts[:, :, F:F + H], firsts[:, :, F + H:RW]
                ch.link(nc.vector.tensor_tensor(new_m[:, :, :], own_m, carry_m, ALU.max))
                nc.vector.tensor_tensor(own_f[:, :, :], own_m, new_m[:, :, :], ALU.subtract)
                nc.vector.tensor_tensor(carry_f[:, :, :], carry_m, new_m[:, :, :], ALU.subtract).then_inc(c["exponent"].sem, 1)
                dve.wait_ge(c["exponent_out"].sem, c["exponent_out"].at(1))
                ch.link(nc.vector.tensor_tensor(own_d, own_d, own_f[:, :, :], ALU.mult))
                ch.link(nc.vector.tensor_tensor(tmp[:, :, :], carry_d, carry_f[:, :, :], ALU.mult))
                ch.link(nc.vector.tensor_tensor(own_d, own_d, tmp[:, :, :], ALU.add))
                ch.link(nc.vector.tensor_copy(own_m, new_m[:, :, :]))
                for h in range(H):
                    part = slice(h * HD, (h + 1) * HD)
                    wide = lambda t: t[:, :, h:h + 1].to_broadcast([BP, BC, HD])
                    nc.vector.tensor_tensor(firsts[:, :, part], firsts[:, :, part], wide(own_f), ALU.mult)
                    ins = nc.vector.tensor_tensor(back[:, :, part], carry_s[:, :, part], wide(carry_f), ALU.mult)
                ch.link(ins)
                nc.vector.tensor_tensor(own_s, own_s, back[:, :, :], ALU.add).then_inc(c["residual"].sem, 1)
                dve_chain.close(ch.n)

            @block.scalar
            def _(act):
                act.wait_ge(c["exponent"].sem, c["exponent"].at(1))
                nc.scalar.activation(own_f[:, :, :], own_f[:, :, :], ACT.Exp)
                nc.scalar.activation(carry_f[:, :, :], carry_f[:, :, :], ACT.Exp).then_inc(c["exponent_out"].sem, 1)

            @block.sync
            def _(sp):
                sp.wait_ge(c["residual"].sem, c["residual"].at(1))
                sp.dma_start(first_rows, firsts[:, :, :]).then_inc(stored[0].sem, 16)
                sp.wait_ge(stored[0].sem, stored[0].at(16))
        stored[0].close(16)
        for k in ("x_turned", "exponent", "exponent_out", "residual"):
            c[k].close(1)
        buf.close()

    node_table("L0 messages", a["x"], None, None)
    scatter_pass()
    node_layer("L0", a["x"], x_state[0], None, table[0])
    message_pass(table[0])
    border_pass("B1")
    node_layer("L1", x_state[0], x_state[1], None, table[0])
    edge_pass("E2", table[0])
    border_pass("B2")
    node_table("L2a", None, table[0], table[1])
    edge_pass("E3", table[1])
    border_pass("B3")
    node_layer("L2b", x_state[1], x_state[0], table[1], table3)
    attention_pass(*attention_setup())
    att.close()
    attention_border()
    node_layer("L3", x_state[0], out, None, None)


_INS = ("x src dst edge_attr_64 edge_type_3 edge_weight "
        "L0_gnn_bn1_gamma L0_gnn_bn1_beta L0_gnn_bn1_mean L0_gnn_bn1_var L0_gnn_W1 L0_gnn_b1 "
        "L0_gnn_bn2_gamma L0_gnn_bn2_beta L0_gnn_bn2_mean L0_gnn_bn2_var L0_gnn_W2 L0_gnn_b2 "
        "L1_gnn_We1 L1_gnn_be1 L1_gnn_We2 L1_gnn_be2 L1_gnn_Wt L1_gnn_bt L1_gnn_Wn1 L1_gnn_bn1 L1_gnn_Wn2 L1_gnn_bn2 "
        "L2_gnn_W1 L2_gnn_b1 L2_gnn_W2 L2_gnn_b2 "
        "L3_gnn_Wq L3_gnn_Wk L3_gnn_Wv L3_gnn_attn_lin L3_gnn_edge_embed_table L3_gnn_Wout L3_gnn_bout").split()


def kernel(**inputs):
    import numpy as np
    import concourse.bacc as bacc
    from concourse.bass_utils import run_bass_kernel_spmd as run

    nc = bacc.Bacc("TRN2", target_bir_lowering=False, num_devices=1)
    arrays = {n: np.ascontiguousarray(inputs[n]) for n in _INS}
    aps = {n: nc.dram_tensor(n, v.shape, mybir.dt.from_np(v.dtype), kind="ExternalInput").ap() for n, v in arrays.items()}
    out = nc.dram_tensor("out", (N, F), F32, kind="ExternalOutput").ap()
    gnn_kernel(nc, aps, out)
    return run(nc, [arrays], core_ids=[0]).results[0]["out"]
```
